# Optimizing a Trainium2 kernel written in Bass

```python
import numpy as np
import jax
import jax.numpy as jnp

def _softmax(x, axis=-1):
    return jax.nn.softmax(x, axis=axis)

def _gelu(x):
    return jax.nn.gelu(x, approximate=True)

def _silu(x):
    return jax.nn.silu(x)

def _sigmoid(x):
    return jax.nn.sigmoid(x)

def _layernorm(x, axis=-1, eps=1e-05):
    m = jnp.mean(x, axis=axis, keepdims=True)
    v = jnp.var(x, axis=axis, keepdims=True)
    return (x - m) / jnp.sqrt(v + eps)

def _scatter_add(tgt, idx, src, axis=0):
    return tgt.at[idx].add(src)

def _segment_sum(src, seg, n):
    return jax.ops.segment_sum(src, seg, n)
kernel_name = 'mk_perceiver_d1_seqx_r8_67f90d'

def setup_inputs(seed: int=0):
    np.random.seed(seed)
    _w = jnp.asarray

    def _rec_inputs():
        import jax
        import jax.numpy as jnp
        _rk = jax.random.key(seed)
        x = 7.22e-05 + 1 * jax.random.normal(jax.random.fold_in(_rk, 1), (128, 32, 128), jnp.float32)
        _lenS = 32 - jax.random.randint(jax.random.fold_in(_rk, 7), (128,), 0, max(1, 32 // 4) + 1, jnp.int32)
        _lenS2 = 257 - jax.random.randint(jax.random.fold_in(_rk, 8), (128,), 0, max(1, 257 // 4) + 1, jnp.int32)
        _ctx_1024P = jax.random.normal(jax.random.fold_in(_rk, 11), (128, 16, 128), jnp.float32)
        _ctx_1024c = jax.random.dirichlet(jax.random.fold_in(_rk, 511), 0.3 * jnp.ones((16,), jnp.float32), (128, 257))
        _ctx_1024t = jnp.einsum('bsk,bkd->bsd', _ctx_1024c, _ctx_1024P)
        _ctx_1024t = _ctx_1024t * jax.lax.rsqrt(jnp.mean(jnp.square(_ctx_1024t)) + 1e-12) * 0.953939
        ctx_1024 = 4.13588e-05 + 0.999923 * (_ctx_1024t + 0.3 * jax.random.normal(jax.random.fold_in(_rk, 611), (128, 257, 128), jnp.float32))
        fside_SxS2_0 = jax.random.uniform(jax.random.fold_in(_rk, 12), (32, 257), jnp.float32, 0.0, 1)
        return (x, ctx_1024, fside_SxS2_0)
    x, ctx_1024, fside_SxS2_0 = _rec_inputs()

    def _L0_xattn_setup():
        import jax, jax.numpy as jnp
        import numpy as np
        D_MODEL = 128
        N_HEADS = 16
        key = jax.random.key(seed)
        k1, k2, k3, k4 = jax.random.split(key, 4)
        B, L, S = (4, 256, 256)
        return {'queries': jax.random.normal(k1, (B, L, D_MODEL), dtype=jnp.float32), 'keys': jax.random.normal(k2, (B, S, D_MODEL), dtype=jnp.float32), 'values': jax.random.normal(k3, (B, S, D_MODEL), dtype=jnp.float32), 'mask': jax.random.uniform(k4, (L, S), dtype=jnp.float32)}
    _L0_xattn_all = _L0_xattn_setup()
    _L0_xattn_in = {k: v for k, v in _L0_xattn_all.items() if k in ()}
    del _L0_xattn_all

    def _L0_attn_setup():
        import jax, jax.numpy as jnp
        import numpy as np
        import math
        D_MODEL = 128
        N_HEADS = 16
        DECAY_SCALE = 0.25

        def power_law_mask(n, decay_scale):
            i = jnp.arange(n)[:, None]
            j = jnp.arange(n)[None, :]
            delta = (i - j).astype(jnp.float32)
            decay = jnp.where(delta > 0, -decay_scale * jnp.log(jnp.maximum(delta, 1.0)), 0.0)
            return jnp.where(j > i, -jnp.inf, decay)
        key = jax.random.key(seed)
        ks = jax.random.split(key, 9)
        B, N, D = (2, 256, D_MODEL)
        s = 1.0 / math.sqrt(D)
        return {'x': jax.random.normal(ks[0], (B, N, D), dtype=jnp.float32), 'Wq': jax.random.normal(ks[1], (D, D), dtype=jnp.float32) * s, 'bq': jnp.zeros((D,), dtype=jnp.float32), 'Wk': jax.random.normal(ks[2], (D, D), dtype=jnp.float32) * s, 'bk': jnp.zeros((D,), dtype=jnp.float32), 'Wv': jax.random.normal(ks[3], (D, D), dtype=jnp.float32) * s, 'bv': jnp.zeros((D,), dtype=jnp.float32), 'Wo': jax.random.normal(ks[4], (D, D), dtype=jnp.float32) * s, 'bo': jnp.zeros((D,), dtype=jnp.float32)}
    _L0_attn_all = _L0_attn_setup()
    _L0_attn_in = {k: v for k, v in _L0_attn_all.items() if k in ('Wq', 'bq', 'Wk', 'bk', 'Wv', 'bv', 'Wo', 'bo')}
    del _L0_attn_all

    def _L0_ffn_setup():
        import jax, jax.numpy as jnp
        import numpy as np
        E, K, D = (8, 2, 128)
        B, S = (2, 512)

        def _layernorm(x, g, b, eps=1e-06):
            m = jnp.mean(x, axis=-1, keepdims=True)
            v = jnp.var(x, axis=-1, keepdims=True)
            return (x - m) * jax.lax.rsqrt(v + eps) * g + b
        key = jax.random.key(seed)
        ks = jax.random.split(key, 6)
        n = lambda k, shape, scale: jax.random.normal(k, shape, jnp.float32) * scale
        return {'x': n(ks[0], (B, S, D), 1.0), 'gate_w': n(ks[1], (D, E), 0.02), 'w1': n(ks[2], (E, D, 2 * D), 0.02), 'b1': jnp.zeros((E, 2 * D), jnp.float32), 'w2': n(ks[3], (E, 2 * D, D), 0.02), 'b2': jnp.zeros((E, D), jnp.float32), 'ln_g': jnp.ones((E, D), jnp.float32), 'ln_b': jnp.zeros((E, D), jnp.float32)}
    _L0_ffn_all = _L0_ffn_setup()
    _L0_ffn_in = {k: v for k, v in _L0_ffn_all.items() if k in ('gate_w', 'w1', 'b1', 'w2', 'b2', 'ln_g', 'ln_b')}
    del _L0_ffn_all
    return {'x': x, 'ctx_1024': ctx_1024, 'fside_SxS2_0': fside_SxS2_0, 'L0_attn_Wq': _L0_attn_in['Wq'], 'L0_attn_bq': _L0_attn_in['bq'], 'L0_attn_Wk': _L0_attn_in['Wk'], 'L0_attn_bk': _L0_attn_in['bk'], 'L0_attn_Wv': _L0_attn_in['Wv'], 'L0_attn_bv': _L0_attn_in['bv'], 'L0_attn_Wo': _L0_attn_in['Wo'], 'L0_attn_bo': _L0_attn_in['bo'], 'L0_ffn_gate_w': _L0_ffn_in['gate_w'], 'L0_ffn_w1': _L0_ffn_in['w1'], 'L0_ffn_b1': _L0_ffn_in['b1'], 'L0_ffn_w2': _L0_ffn_in['w2'], 'L0_ffn_b2': _L0_ffn_in['b2'], 'L0_ffn_ln_g': _L0_ffn_in['ln_g'], 'L0_ffn_ln_b': _L0_ffn_in['ln_b']}

def reference(x, ctx_1024, fside_SxS2_0, L0_attn_Wq, L0_attn_bq, L0_attn_Wk, L0_attn_bk, L0_attn_Wv, L0_attn_bv, L0_attn_Wo, L0_attn_bo, L0_ffn_gate_w, L0_ffn_w1, L0_ffn_b1, L0_ffn_w2, L0_ffn_b2, L0_ffn_ln_g, L0_ffn_ln_b):
    import jax
    import jax.numpy as jnp

    def _L0_xattn_ref(queries, keys, values, mask):
        import jax, jax.numpy as jnp
        import numpy as np
        D_MODEL = 128
        N_HEADS = 16
        B, L, _ = queries.shape
        S = keys.shape[1]
        H = N_HEADS
        q = queries.reshape(B, L, H, -1)
        k = keys.reshape(B, S, H, -1)
        v = values.reshape(B, S, H, -1)
        E = q.shape[-1]
        scale = 1.0 / jnp.sqrt(jnp.asarray(E, q.dtype))
        scores = jnp.einsum('blhe,bshe->bhls', q, k)
        A = jax.nn.softmax(scale * scores, axis=-1)
        A = A * mask
        out = jnp.einsum('bhls,bshd->blhd', A, v)
        out = jnp.transpose(out, (0, 2, 1, 3)).reshape(B, L, -1)
        return out

    def _L0_attn_ref(x, Wq, bq, Wk, bk, Wv, bv, Wo, bo):
        import jax, jax.numpy as jnp
        import numpy as np
        import math
        D_MODEL = 128
        N_HEADS = 16
        DECAY_SCALE = 0.25

        def power_law_mask(n, decay_scale):
            i = jnp.arange(n)[:, None]
            j = jnp.arange(n)[None, :]
            delta = (i - j).astype(jnp.float32)
            decay = jnp.where(delta > 0, -decay_scale * jnp.log(jnp.maximum(delta, 1.0)), 0.0)
            return jnp.where(j > i, -jnp.inf, decay)
        B, N, D = x.shape
        H = N_HEADS
        dk = D // H

        def proj(W, b):
            return (x @ W + b).reshape(B, N, H, dk).transpose(0, 2, 1, 3)
        Q, K, V = (proj(Wq, bq), proj(Wk, bk), proj(Wv, bv))
        scores = jnp.einsum('bhnd,bhmd->bhnm', Q, K) / jnp.sqrt(jnp.float32(dk))
        scores = scores + power_law_mask(N, DECAY_SCALE)[None, None]
        attn = jax.nn.softmax(scores, axis=-1)
        out = jnp.einsum('bhnm,bhmd->bhnd', attn, V)
        out = out.transpose(0, 2, 1, 3).reshape(B, N, D)
        return out @ Wo + bo

    def _L0_ffn_ref(x, gate_w, w1, b1, w2, b2, ln_g, ln_b):
        import jax, jax.numpy as jnp
        import numpy as np
        E, K, D = (8, 2, 128)
        B, S = (2, 512)

        def _layernorm(x, g, b, eps=1e-06):
            m = jnp.mean(x, axis=-1, keepdims=True)
            v = jnp.var(x, axis=-1, keepdims=True)
            return (x - m) * jax.lax.rsqrt(v + eps) * g + b
        orig_shape = x.shape
        xt = x.reshape(-1, orig_shape[-1])
        scores = xt @ gate_w
        ew, ei = jax.lax.top_k(scores, K)
        ew = jax.nn.softmax(ew, axis=-1)
        mask = ei[None, :, :] == jnp.arange(E)[:, None, None]
        wE = jnp.sum(ew[None, :, :] * mask, axis=-1)
        h = jax.nn.gelu(jnp.einsum('td,edf->etf', xt, w1) + b1[:, None, :], approximate=False)
        o = jnp.einsum('etf,efd->etd', h, w2) + b2[:, None, :]
        y = _layernorm(xt[None, :, :] + o, ln_g[:, None, :], ln_b[:, None, :])
        out = jnp.einsum('et,etd->td', wE, y)
        return out.reshape(orig_shape)
    x = x + _L0_xattn_ref(_layernorm(x, axis=-1), ctx_1024, ctx_1024, fside_SxS2_0)
    x = x + _L0_attn_ref(_layernorm(x, axis=-1), L0_attn_Wq, L0_attn_bq, L0_attn_Wk, L0_attn_bk, L0_attn_Wv, L0_attn_bv, L0_attn_Wo, L0_attn_bo)
    x = x + _L0_ffn_ref(_layernorm(x, axis=-1), L0_ffn_gate_w, L0_ffn_w1, L0_ffn_b1, L0_ffn_w2, L0_ffn_b2, L0_ffn_ln_g, L0_ffn_ln_b)
    return x

_drawn_inputs = setup_inputs


def setup_inputs(seed=0):
    import zlib

    import numpy as np

    out = dict(_drawn_inputs(seed))
    spreads = {'L0_attn_bq': (0.0, 0.28),
     'L0_attn_bk': (0.0, 2.0),
     'L0_attn_bv': (0.0, 0.1),
     'L0_attn_bo': (0.0, 0.1),
     'L0_ffn_b1': (0.0, 0.8),
     'L0_ffn_b2': (0.0, 0.327),
     'L0_ffn_ln_g': (1.0, 0.2),
     'L0_ffn_ln_b': (0.0, 0.1)}
    factors = {'L0_ffn_w1': 4.436, 'L0_ffn_w2': 4.023}
    for name, (base, spread) in spreads.items():
        noise = np.random.default_rng([zlib.crc32(name.encode()), seed]).standard_normal(out[name].shape)
        drawn = base * np.exp(spread * noise) if base else spread * noise
        out[name] = jnp.asarray(drawn.astype(out[name].dtype))
    for name, factor in factors.items():
        out[name] = (out[name] * factor).astype(out[name].dtype)
    return out
```

```python
from contextlib import ExitStack

import concourse.bass as bass
from concourse import mybir

F32 = mybir.dt.float32
I32 = mybir.dt.int32
U32 = mybir.dt.uint32
ALU = mybir.AluOpType
ACT = mybir.ActivationFunctionType
AX = mybir.AxisListType

B, L, D = 128, 32, 128
S = 257
H, DK = 16, 8
NE, F = 8, 256
EPS_LN, EPS_EXPERT = 1e-5, 1e-6
SCALE = float(DK) ** -0.5

P = 128
NQ, HQ = 4, 4
TB = 8
HB = TB // 2
T = B // TB
KT = 2
STEPS = 2 * TB
HSTEPS = STEPS // 2
DECAY = -0.25
MASKED = -1.0e30


def perceiver_layer(nc, x, ctx, fmask, Wq, bq, Wk, bk, Wv, bv, Wo, bo, gate_w, w1, b1, w2, b2, ln_g, ln_b, out, stages=3):
    with ExitStack() as es:
        def sb(name, shape, dt=F32):
            return es.enter_context(nc.sbuf_tensor(name, shape, dt))

        def sem(name):
            return es.enter_context(nc.semaphore(name))

        ident = sb("ident", [P, P])
        head_of = sb("head_of", [P, H])
        own_of = sb("own_of", [P, 2, HQ])
        hh_of = sb("hh_of", [P, HQ])
        hh_scaled = sb("hh_scaled", [P, HQ, L])
        own_scaled = sb("own_scaled", [P, 2, HQ, L])
        mask_T = sb("mask_T", [P, 2, KT, HQ * L])
        mask_last = sb("mask_last", [HB * NQ, HQ * L])
        last_sel = sb("last_sel", [HB * NQ, HB, D])
        X = sb("X", [P, T, 2 * D])

        setup_in = sem("setup_in")
        xperm_in = sem("xperm_in")
        pool_set = sem("pool_set")
        dve_set = sem("dve_set")
        pe_set = sem("pe_set")

        with ExitStack() as s0:
            fm = s0.enter_context(nc.sbuf_tensor("fm", [L, S], F32))
            ps0 = s0.enter_context(nc.psum_tensor("ps0", [P, 512], F32))
            block = s0.enter_context(nc.Block())

            @block.sync
            def _(sp):
                sp.dma_start(fm[:, :], fmask).then_inc(setup_in, 16)

            @block.gpsimd
            def _(pool):
                pool.memset(ident[:, :], 0.0).then_inc(pool_set, 1)
                pool.memset(head_of[:, :], 1.0).then_inc(pool_set, 1)
                pool.memset(last_sel[:, :, :], 0.0).then_inc(pool_set, 1)
                pool.wait_ge(pool_set, 3)
                pool.affine_select(out=ident[:, :], in_=ident[:, :], compare_op=ALU.not_equal, fill=1.0, base=0,
                                   pattern=[[-1, P]], channel_multiplier=1).then_inc(pool_set, 1)
                pool.affine_select(out=head_of[:, :], in_=head_of[:, :], compare_op=ALU.is_ge, fill=0.0, base=0,
                                   pattern=[[-DK, H]], channel_multiplier=1).then_inc(pool_set, 1)
                pool.wait_ge(pool_set, 5)
                pool.affine_select(out=head_of[:, :], in_=head_of[:, :], compare_op=ALU.is_ge, fill=0.0, base=DK - 1,
                                   pattern=[[DK, H]], channel_multiplier=-1).then_inc(pool_set, 1)
                pool.affine_select(out=last_sel[:, :, :].rearrange("p j (g c) -> p j g c", g=NQ),
                                   in_=last_sel[:, :, :].rearrange("p j (g c) -> p j g c", g=NQ),
                                   compare_op=ALU.not_equal, fill=1.0, base=0,
                                   pattern=[[-NQ, HB], [-1, NQ], [0, D // NQ]], channel_multiplier=1).then_inc(pool_set, 1)

            @block.tensor
            def _(pe):
                pe.wait_ge(setup_in, 16)
                pe.wait_ge(pool_set, 7)
                for k in range(KT):
                    pe.transpose(ps0[:, k * L:(k + 1) * L], fm[:, k:KT * P:KT], ident[0:L, 0:L])
                pe.matmul(ps0[0:HB * NQ, 64:64 + L], fm[:, S - 1:S].to_broadcast([L, HB * NQ]),
                          ident[0:L, 0:L], start=True, stop=True).then_inc(pe_set, 1)

            @block.vector
            def _(dve):
                dve.wait_ge(pool_set, 7)
                dve.tensor_reduce(own_of[:, :, :], head_of[:, :].rearrange("p (a u q) -> p u q a", u=2, q=HQ), AX.X,
                                  ALU.add).then_inc(dve_set, 1)
                dve.wait_ge(dve_set, 1)
                dve.tensor_scalar(own_scaled[:, :, :, :], own_of[:, :, :].unsqueeze(3).to_broadcast([P, 2, HQ, L]), SCALE, None,
                                  ALU.mult).then_inc(dve_set, 1)
                dve.tensor_tensor(hh_of[:, :], own_of[:, 0, :], own_of[:, 1, :], ALU.add).then_inc(dve_set, 1)
                dve.wait_ge(dve_set, 3)
                dve.tensor_scalar(hh_scaled[:, :, :], hh_of[:, :].unsqueeze(2).to_broadcast([P, HQ, L]), SCALE, None,
                                  ALU.mult).then_inc(dve_set, 1)
                dve.wait_ge(pe_set, 1)
                for u in range(2):
                    for k in range(KT):
                        dve.tensor_copy(mask_T[:, u, k, :].rearrange("p (q l) -> p q l", q=HQ),
                                        ps0[:, k * L:(k + 1) * L].unsqueeze(1).to_broadcast([P, HQ, L])).then_inc(dve_set, 1)
                dve.tensor_copy(mask_last[:, :].rearrange("p (q l) -> p q l", q=HQ),
                                ps0[0:HB * NQ, 64:64 + L].unsqueeze(1).to_broadcast([HB * NQ, HQ, L])).then_inc(dve_set, 1)

        with ExitStack() as s1:
            def sb1(name, shape, dt=F32):
                return s1.enter_context(nc.sbuf_tensor(name, shape, dt))

            def ps1(name, shape):
                return s1.enter_context(nc.psum_tensor(name, shape, F32))

            def sem1(name):
                return s1.enter_context(nc.semaphore(name))

            V = sb1("V", [P, TB, KT, D])
            last_row = sb1("last_row", [1, 2, HB, D])
            last_rep = sb1("last_rep", [HB * NQ, 2, D])
            last_bd = sb1("last_bd", [HB * NQ, 2, HB, D])
            xh = sb1("xh", [P, 2, D])
            xn = sb1("xn", [P, D])
            xstat = sb1("xstat", [P, 6])
            xmv = sb1("xmv", [P, 2])
            xrs = sb1("xrs", [P, 1])
            xvar = sb1("xvar", [P, 1])
            neg_half = sb1("neg_half", [P, 1])
            Qt = sb1("Qt", [P, HB * L])
            Qbd = sb1("Qbd", [P, 2, 2, HB, HQ * L])
            Kt = sb1("Kt", [P, 4, S])
            neg_max = sb1("neg_max", [P, 2, 2])
            E = sb1("E", [P, 2, HB * NQ, S])
            den = sb1("den", [P, 2, HB * NQ])
            rden = sb1("rden", [P, HB * NQ])
            Et = sb1("Et", [P, 4, 2, KT, HQ * L])
            last_Et = sb1("last_Et", [HB * NQ, HQ * L])
            O_c = sb1("O_c", [P, HB, HQ * L])
            O_n = sb1("O_n", [P, DK, TB * NQ])
            O_t = sb1("O_t", [P, DK, L])

            SC = [ps1(f"SC{i}", [P, 2, 512]) for i in range(2)]
            ETP = [ps1(f"ETP{i}", [P, 512]) for i in range(2)]
            AV = ps1("AV", [P, HB, HQ * L])
            MISC = ps1("MISC", [P, 512])
            KTP = MISC[:, 0:S]
            TURN = MISC[:, 0:P]

            ctx_in = [sem1(f"ctx_in{k}") for k in range(TB // 2)]
            last_in = [sem1(f"last_in{h}") for h in range(2)]
            x_in = [sem1(f"x_in{h}") for h in range(2)]
            consts = sem1("consts")
            kt_ps, kt_sb = sem1("kt_ps"), sem1("kt_sb")
            sc_ps, mx = sem1("sc_ps"), sem1("mx")
            ex = sem1("ex")
            et_ps, et_sb = sem1("et_ps"), sem1("et_sb")
            av_b = sem1("av_b")
            lastt_ps, lastt_sb, last_bd_set = sem1("lastt_ps"), sem1("lastt_sb"), sem1("last_bd_set")
            av_full, o_c, o_ps, o_n = sem1("av_full"), sem1("o_c"), sem1("o_ps"), sem1("o_n")
            rden_set = sem1("rden_set")
            o_t, x1 = sem1("o_t"), sem1("x1")
            st, mv, vr, rs, xn_sb = sem1("st"), sem1("mv"), sem1("vr"), sem1("rs"), sem1("xn_sb")
            qt_ps, qt_sb, q_bd = sem1("qt_ps"), sem1("qt_sb"), sem1("q_bd")

            block = s1.enter_context(nc.Block())

            @block.sync
            def _(sp):
                def load_ctx(t, k):
                    sp.dma_start(V[:, 2 * k:2 * k + 2, :, :].rearrange("p b k c -> p b (k c)"),
                                 ctx[bass.ds(TB * t + 2 * k, 2), 0:KT * P, :].rearrange("b (p k) c -> p b (k c)", p=P)
                                 ).then_inc(ctx_in[k], 16)

                def load_last(t, h):
                    b0 = TB * t + HB * h
                    sp.dma_start(last_row[0:1, h, :, :], ctx[bass.ds(b0, HB), S - 1, :].unsqueeze(0)).then_inc(last_in[h], 16)
                    for j in range(HB):
                        sp.dma_start(last_rep[NQ * j:NQ * j + NQ, h, :],
                                     ctx[bass.ds(b0 + j, 1), S - 1, :].to_broadcast([NQ, D])).then_inc(last_in[h], 16)

                def load_x(t, h):
                    sp.dma_start(xh[:, h, :], x[bass.ds(TB * t + HB * h, HB), :, :].rearrange("b l c -> (b l) c")).then_inc(x_in[h], 16)

                load_x(0, 0)
                load_ctx(0, 0)
                load_last(0, 0)
                load_ctx(0, 1)
                load_x(0, 1)
                load_ctx(0, 2)
                load_last(0, 1)
                load_ctx(0, 3)
                for q in range(HQ):
                    for b in range(TB):
                        sp.dma_start(X[32 * q + NQ * b:32 * q + NQ * b + NQ, :, :],
                                     x.rearrange("(t b) (g q e) c -> q b g t (e c)", t=T, g=NQ, q=HQ)[q, b]).then_inc(xperm_in, 16)
                with sp.Fori(1, T) as t:
                    sp.wait_ge(xn_sb, 2 * t - 1)
                    load_x(t, 0)
                    sp.wait_ge(av_b, TB * t - TB + 2)
                    load_ctx(t, 0)
                    sp.wait_ge(xn_sb, 2 * t)
                    load_x(t, 1)
                    sp.wait_ge(av_b, TB * t - TB + 4)
                    load_ctx(t, 1)
                    sp.wait_ge(av_full, 2 * t - 1)
                    load_last(t, 0)
                    sp.wait_ge(av_b, TB * t - TB + 6)
                    load_ctx(t, 2)
                    sp.wait_ge(av_b, TB * t - TB + 8)
                    load_ctx(t, 3)
                    sp.wait_ge(av_full, 2 * t)
                    load_last(t, 1)

            @block.gpsimd
            def _(pool):
                pool.wait_ge(dve_set, 2)
                pool.memset(neg_half[:, :], -0.5).then_inc(consts, 1)
                pool.wait_ge(consts, 1)

                def half(t, h, first=False):
                    m = 2 * t + h
                    pool.wait_ge(vr, m + 1)
                    pool.tensor_tensor(xrs[:, :], xvar[:, :], neg_half[:, :], ALU.pow).then_inc(rs, 1)
                    pool.wait_ge(qt_sb, m + 1)
                    if not first:
                        pool.wait_ge(sc_ps, HSTEPS * (m - 1))
                    for u in range(2):
                        i = pool.tensor_tensor(
                            Qbd[:, h, u, :, :].rearrange("p j (q l) -> p j q l", q=HQ),
                            Qt[:, :].rearrange("p (j l) -> p j l", j=HB).unsqueeze(2).to_broadcast([P, HB, HQ, L]),
                            own_scaled[:, u, :, :].unsqueeze(1).to_broadcast([P, HB, HQ, L]), ALU.mult)
                    i.then_inc(q_bd, 1)
                    pool.wait_ge(last_in[h], 16 * (HB + 1) * (t + 1))
                    if not first:
                        pool.wait_ge(av_full, m - 1)
                    for j in range(HB):
                        i = pool.tensor_tensor(last_bd[:, h, j, :], last_rep[:, h, :], last_sel[:, j, :], ALU.mult)
                    i.then_inc(last_bd_set, 1)

                for h in range(2):
                    half(0, h, first=True)
                with pool.Fori(1, T) as t:
                    for h in range(2):
                        half(t, h)

            def run_tiles(steps, eng):
                steps(0, True, False)
                with eng.Fori(1, T - 1) as t:
                    steps(t, False, False)
                steps(T - 1, False, True)

            @block.tensor
            def _(pe):
                def turn_keys(t, j, first=False):
                    b = TB * t + j
                    pe.wait_ge(ctx_in[j // 2], 16 * (t + 1))
                    pe.wait_ge(last_in[j // HB], 16 * (HB + 1) * (t + 1))
                    if not first:
                        pe.wait_ge(kt_sb, b)
                        if j % HB == 2 and not (isinstance(t, int) and t == 0 and j == 2):
                            pe.wait_ge(lastt_sb, 2 * t + j // HB)
                    if j % HB == 0:
                        pe.wait_ge(qt_sb, 2 * t + j // HB + 1)
                    for k in range(KT):
                        pe.transpose(KTP[:, k * P:(k + 1) * P], V[:, j, k, :], ident[:, :])
                    pe.transpose(KTP[:, S - 1:S], last_row[0:1, j // HB, j % HB, :], ident[0:1, 0:1]).then_inc(kt_ps, 1)

                def turn_queries(t, h, first=False):
                    m = 2 * t + h
                    pe.wait_ge(xn_sb, m + 1)
                    if not first:
                        pe.wait_ge(kt_sb, HB * m)
                    pe.transpose(TURN, xn[:, :], ident[:, :]).then_inc(qt_ps, 1)

                def scores(t, s, first=False):
                    j, n = s // 2, STEPS * t + s
                    if s % 2 == 0:
                        pe.wait_ge(kt_sb, TB * t + j + 1)
                    if s % HSTEPS == 0:
                        pe.wait_ge(q_bd, 2 * t + s // HSTEPS + 1)
                    if not first:
                        pe.wait_ge(ex, n - 1)
                    for u in range(2):
                        r = slice(64 * (s % 2), 64 * (s % 2) + 64)
                        i = pe.matmul(SC[s % 2][:, u, 0:S], Qbd[r, j // HB, u, j % HB, :],
                                      Kt[r, j % 4, :], start=True, stop=True)
                    i.then_inc(sc_ps, 1)

                def turn_probs(t, s, first=False):
                    n = STEPS * t + s
                    h, u0 = s // HSTEPS, 2 * (s % HSTEPS)
                    pe.wait_ge(ex, n + 1)
                    if not first:
                        pe.wait_ge(et_sb, n - 1)
                    for u in range(2):
                        for k in range(KT):
                            c = (2 * u + k) * P
                            i = pe.transpose(ETP[s % 2][:, c:c + P], E[:, h, u0 + u, k * P:(k + 1) * P], ident[:, :])
                    i.then_inc(et_ps, 1)

                def weigh_values(t, j, first=False):
                    h = j // HB
                    pe.wait_ge(et_sb, STEPS * t + 2 * j + 2)
                    if j % HB == 0 and not first:
                        pe.wait_ge(o_n, 2 * t + h)
                    for k in range(KT):
                        for g in range(NQ):
                            i = pe.matmul(AV[32 * g:32 * g + 32, j % HB, :], V[:, j, k, 32 * g:32 * g + 32],
                                          Et[:, 2 * (j % 2) + g // 2, g % 2, k, :],
                                          start=(j % HB == 0 and k == 0), stop=False, skip_group_check=True)
                    i.then_inc(av_b, 1)

                def turn_last(t, h, final=False):
                    m = 2 * t + h
                    if not final:
                        pe.wait_ge(kt_sb, HB * m + HB + 2)
                    pe.transpose(TURN[0:HB * NQ, :], E[:, h, :, S - 1], ident[:, :]).then_inc(lastt_ps, 1)

                def weigh_last(t, h):
                    m = 2 * t + h
                    pe.wait_ge(lastt_sb, m + 1)
                    pe.wait_ge(last_bd_set, m + 1)
                    for j in range(HB):
                        i = pe.matmul(AV[:, j, :], last_bd[:, h, j, :], last_Et[:, :], start=False, stop=(j == HB - 1),
                                      skip_group_check=True)
                    i.then_inc(av_full, 1)

                def turn_out(t, h):
                    pe.wait_ge(o_c, 2 * t + h + 1)
                    for j in range(HB):
                        i = pe.transpose(AV[:, j, :], O_c[:, j, :], ident[:, :])
                    i.then_inc(o_ps, 1)

                def back(t, s, lag):
                    return (t, s - lag) if s >= lag else (t - 1, s + STEPS - lag)

                def lagging(t, s):
                    fresh = isinstance(t, int) and t == 0
                    if not (fresh and s < 2):
                        tt, ss = back(t, s, 2)
                        turn_probs(tt, ss, first=fresh and s < 4)
                    if s % 2 == 1 and not (fresh and s < 5):
                        tt, ss = back(t, s, 5)
                        weigh_values(tt, ss // 2, first=fresh and s == 5)
                    if not (fresh and s < HSTEPS):
                        tt, ss = back(t, s, HSTEPS)
                        if s % HSTEPS == 1:
                            turn_last(tt, ss // HSTEPS)
                        if s % HSTEPS == 3:
                            weigh_last(tt, ss // HSTEPS)

                def steps(t, fresh, final):
                    for s in range(STEPS):
                        scores(t, s, first=fresh and s < 2)
                        if s % HSTEPS == 4 and not (fresh and s < HSTEPS):
                            tt, ss = back(t, s, HSTEPS)
                            turn_out(tt, ss // HSTEPS)
                        if s % 2 == 0:
                            if s < STEPS - 2:
                                turn_keys(t, s // 2 + 1)
                            elif not final:
                                turn_keys(t + 1, 0)
                        if s == 5:
                            turn_queries(t, 1)
                        if s == 13 and not final:
                            turn_queries(t + 1, 0)
                        lagging(t, s)

                pe.wait_ge(pool_set, 7)
                turn_queries(0, 0, first=True)
                turn_keys(0, 0, first=True)
                run_tiles(steps, pe)
                turn_probs(T - 1, STEPS - 2)
                turn_probs(T - 1, STEPS - 1)
                turn_last(T - 1, 1, final=True)
                weigh_values(T - 1, TB - 2)
                weigh_values(T - 1, TB - 1)
                weigh_last(T - 1, 1)
                turn_out(T - 1, 1)

            @block.scalar
            def _(act):
                def keep_keys(t, j, first=False):
                    b = TB * t + j
                    act.wait_ge(kt_ps, b + 1)
                    if not first:
                        act.wait_ge(sc_ps, 2 * (b - 3))
                    act.activation(Kt[:, j % 4, :], KTP, ACT.Copy).then_inc(kt_sb, 1)

                def keep_queries(t, h, first=False):
                    m = 2 * t + h
                    act.wait_ge(qt_ps, m + 1)
                    if not first:
                        act.wait_ge(q_bd, m)
                    act.activation(Qt[:, :], TURN, ACT.Copy).then_inc(qt_sb, 1)

                def exponentials(t, s, first=False):
                    n = STEPS * t + s
                    h, u0 = s // HSTEPS, 2 * (s % HSTEPS)
                    act.wait_ge(mx, n + 1)
                    if s % HSTEPS == 0 and not first:
                        act.wait_ge(lastt_ps, 2 * t + h - 1)
                        act.wait_ge(rden_set, 2 * t + h - 1)
                    for u in range(2):
                        i = act.activation(E[:, h, u0 + u, :], SC[s % 2][:, u, 0:S], ACT.Exp,
                                           bias=neg_max[:, s % 2, u:u + 1], accum_out=den[:, h, u0 + u:u0 + u + 1])
                    i.then_inc(ex, 1)

                def keep_sums(t, h):
                    act.wait_ge(av_full, 2 * t + h + 1)
                    act.activation(O_c[:, :, :], AV[:, :, :], ACT.Copy).then_inc(o_c, 1)

                def steps(t, fresh, final):
                    for s in range(STEPS):
                        if s % 2 == 0:
                            if s < STEPS - 2:
                                keep_keys(t, s // 2 + 1, first=fresh and s < 6)
                            elif not final:
                                keep_keys(t + 1, 0)
                        exponentials(t, s, first=fresh)
                        if s % HSTEPS == 5 and not (final and s >= HSTEPS):
                            keep_queries(t if s < HSTEPS else t + 1, 1 if s < HSTEPS else 0)
                        if s % HSTEPS == 3 and not (fresh and s < HSTEPS):
                            keep_sums(t if s >= HSTEPS else t - 1, 0 if s >= HSTEPS else 1)

                keep_queries(0, 0, first=True)
                keep_keys(0, 0, first=True)
                run_tiles(steps, act)
                keep_sums(T - 1, 1)

            @block.vector
            def _(dve):
                def normalise(t, h, first=False):
                    m = 2 * t + h
                    dve.wait_ge(x_in[h], 16 * (t + 1))
                    dve.bn_stats(xstat[:, :], xh[:, h, :]).then_inc(st, 1)
                    dve.wait_ge(st, m + 1)
                    dve.nop(nofuse=True)
                    dve.bn_aggr(xmv[:, :], xstat[:, :]).then_inc(mv, 1)
                    dve.wait_ge(mv, m + 1)
                    if not first:
                        dve.wait_ge(rs, m)
                    dve.tensor_scalar(xvar[:, :], xmv[:, 1:2], EPS_LN, None, ALU.add).then_inc(vr, 1)

                def normalise2(t, h, first=False):
                    m = 2 * t + h
                    dve.wait_ge(rs, m + 1)
                    if not first:
                        dve.wait_ge(qt_ps, m)
                    dve.tensor_scalar(xn[:, :], xh[:, h, :], xmv[:, 0:1], xrs[:, 0:1], ALU.subtract, ALU.mult).then_inc(xn_sb, 1)

                def maxima(t, s, first=False):
                    n = STEPS * t + s
                    dve.wait_ge(sc_ps, n + 1)
                    if not first:
                        dve.wait_ge(ex, n - 1)
                    dve.tensor_reduce(neg_max[:, s % 2, :], SC[s % 2][:, :, 0:S], AX.X, ALU.max, negate=True).then_inc(mx, 1)

                def keep_probs(t, s, first=False):
                    n = STEPS * t + s
                    dve.wait_ge(et_ps, n + 1)
                    if not first:
                        dve.wait_ge(av_b, (STEPS // 2) * t + s // 2 - 1)
                    dve.tensor_tensor(Et[:, s % 4, :, :, :].rearrange("p u k c -> p (u k c)"), ETP[s % 2][:, :],
                                      mask_T[:, :, :, :].rearrange("p u k c -> p (u k c)"), ALU.mult).then_inc(et_sb, 1)

                def keep_last(t, h):
                    m = 2 * t + h
                    dve.wait_ge(lastt_ps, m + 1)
                    if not (isinstance(t, int) and t == 0 and h == 0):
                        dve.wait_ge(av_full, m)
                    dve.tensor_tensor(last_Et[:, :], TURN[0:HB * NQ, :], mask_last[:, :], ALU.mult).then_inc(lastt_sb, 1)

                def invert(t, h):
                    m = 2 * t + h
                    dve.reciprocal(rden[:, :], den[:, h, :]).then_inc(rden_set, 1)

                def own_outputs(t, h):
                    m = 2 * t + h
                    dve.wait_ge(o_ps, m + 1)
                    dve.wait_ge(rden_set, m + 1)
                    if not (isinstance(t, int) and t == 0):
                        if h == 0:
                            dve.wait_ge(o_t, t)
                    for q in range(HQ):
                        r = slice(32 * q, 32 * q + 32)
                        i = dve.tensor_tensor(
                            O_n[r, :, HB * NQ * h:HB * NQ * (h + 1)].rearrange("p d u -> p u d"),
                            AV[r, :, :].rearrange("p j (g c) -> p (j g) c", g=NQ)[:, :, DK * q:DK * q + DK],
                            rden[r, :].unsqueeze(2).to_broadcast([32, HB * NQ, DK]), ALU.mult)
                    i.then_inc(o_n, 1)

                def add_tile(t):
                    dve.wait_ge(o_n, 2 * t + 2)
                    dve.transpose(O_t[:, :, :].rearrange("p d l -> p (d l)"), O_n[:, :, :].rearrange("p d u -> p (d u)")).then_inc(o_t, 1)
                    dve.wait_ge(o_t, t + 1)
                    xt = X[:, t, :] if isinstance(t, int) else X[:, bass.ds(t, 1), :].rearrange("p a c -> p (a c)")
                    dve.tensor_tensor(xt.rearrange("p (l d) -> p l d", d=DK), O_t[:, :, :].rearrange("p d l -> p l d"),
                                      xt.rearrange("p (l d) -> p l d", d=DK), ALU.add).then_inc(x1, 1)

                def back(t, s, lag):
                    return (t, s - lag) if s >= lag else (t - 1, s + STEPS - lag)

                def steps(t, fresh, final):
                    for s in range(STEPS):
                        maxima(t, s, first=fresh and s < 2)
                        if not (fresh and s < 2):
                            tt, ss = back(t, s, 2)
                            keep_probs(tt, ss, first=fresh and s < 6)
                        if not (fresh and s < HSTEPS):
                            tt, ss = back(t, s, HSTEPS)
                            hh = ss // HSTEPS
                            if s % HSTEPS == 1:
                                keep_last(tt, hh)
                            if s % HSTEPS == 3:
                                invert(tt, hh)
                            if s % HSTEPS == 4:
                                own_outputs(tt, hh)
                            if s == 5:
                                add_tile(tt)
                        q = (t, 1) if s < HSTEPS else (t + 1, 0)
                        if not (final and s >= HSTEPS):
                            if s % HSTEPS == 2:
                                normalise(*q)
                            if s % HSTEPS == 4:
                                normalise2(*q)

                dve.wait_ge(dve_set, 9)
                normalise(0, 0, first=True)
                normalise2(0, 0, first=True)
                dve.wait_ge(xperm_in, 16 * HQ * TB)
                run_tiles(steps, dve)
                for s in range(2):
                    keep_probs(T - 1, STEPS - 2 + s)
                keep_last(T - 1, 1)
                invert(T - 1, 1)
                own_outputs(T - 1, 1)
                add_tile(T - 1)

        if stages == 1:
            store(nc, es, X, out)
            return
        attend(nc, es, X, ident, hh_of, hh_scaled, Wq, bq, Wk, bk, Wv, bv, Wo, bo)
        if stages == 2:
            store(nc, es, X, out)
            return
        mix_experts(nc, es, X, ident, gate_w, w1, b1, w2, b2, ln_g, ln_b, out)


def attend(nc, es, X, ident, hh_of, hh_scaled, Wq, bq, Wk, bk, Wv, bv, Wo, bo):
    with ExitStack() as s2:
        def sb(name, shape, dt=F32):
            return s2.enter_context(nc.sbuf_tensor(name, shape, dt))

        def ps(name, shape):
            return s2.enter_context(nc.psum_tensor(name, shape, F32))

        def sem(name):
            return s2.enter_context(nc.semaphore(name))

        W = {n: sb(f"W{n}", [P, D]) for n in "qkvo"}
        brow = sb("brow", [3, D])
        bo_row = sb("bo_row", [1, D])
        ones_row = sb("ones_row", [1, P])
        bcol = sb("bcol", [P, 3])
        out_bias = sb("out_bias", [P, D])
        lag_i = sb("lag_i", [L, L], I32)
        lag = sb("lag", [L, L])
        lag_ln = sb("lag_ln", [L, L])
        lag_p = sb("lag_p", [L, L])
        turn_l = sb("turn_l", [L, HQ, L])
        hh_wide = sb("hh_wide", [P, HQ, TB])
        decay = sb("decay", [P, HB * NQ, L])
        neg_half = sb("neg_half2", [P, 2])
        stat = sb("stat2", [P, 2, 6])
        mv = sb("mv2", [P, 2, 2])
        var = sb("var2", [P, 2])
        rs = sb("rs2", [P, 2])
        xn = sb("xn2", [P, 2, D])
        xT = sb("xT2", [P, TB, L])
        xT4 = sb("xT4", [P, TB, NQ, L])
        Qt = sb("Qt2", [P, TB, L])
        Qbd = sb("Qbd2", [P, TB, HQ, L])
        Kbd = sb("Kbd2", [P, TB, NQ, L])
        Vbd = sb("Vbd2", [P, 2, TB, D])
        E = sb("E2", [P, 2, HB * NQ, L])
        mx = sb("mx2", [P, 2, HB * NQ])
        sm = sb("sm2", [P, 2, HB * NQ])
        En = sb("En2", [P, 2, HB * NQ, L])
        Et = sb("Et2", [P, 2, HB, HQ * L])
        Oc = sb("Oc2", [P, HQ * TB, TB, NQ])
        Xb = sb("Xb2", [P, 2 * D])

        PA = ps("PA", [P, 512])
        PV = [ps(f"PV{h}", [P, HB, D]) for h in range(2)]
        PS = [ps(f"PS{h}", [P, 512]) for h in range(2)]
        PE_ = [ps(f"PE{h}", [P, HB, HQ * L]) for h in range(2)]
        PY = ps("PY", [P, 2 * D])

        w_in, set_pool, set_pe, set_act, set_dve = sem("w_in"), sem("set_pool"), sem("set_pe"), sem("set_act"), sem("set_dve")
        with nc.Block() as block:
            @block.sync
            def _(sp):
                for n, src in zip("qkvo", (Wq, Wk, Wv, Wo)):
                    sp.dma_start(W[n][:, :], src).then_inc(w_in, 16)
                for i, src in enumerate((bq, bk, bv)):
                    sp.dma_start(brow[i:i + 1, :], src.unsqueeze(0)).then_inc(w_in, 16)
                sp.dma_start(bo_row[:, :], bo.unsqueeze(0)).then_inc(w_in, 16)

            @block.gpsimd
            def _(pool):
                pool.iota(lag_i[:, :], pattern=[[-1, L]], base=0, channel_multiplier=1).then_inc(set_pool, 1)
                pool.memset(neg_half[:, :], -0.5).then_inc(set_pool, 1)
                pool.memset(ones_row[:, :], 1.0).then_inc(set_pool, 1)
                pool.memset(Kbd[:, :, :, :], 0.0).then_inc(set_pool, 1)
                pool.memset(Vbd[:, :, :, :], 0.0).then_inc(set_pool, 1)
                pool.wait_ge(set_act, 2)
                pool.affine_select(out=lag_ln[:, :], in_=lag_ln[:, :], compare_op=ALU.is_ge, fill=MASKED, base=0,
                                   pattern=[[-1, L]], channel_multiplier=1).then_inc(set_pool, 1)

            @block.vector
            def _(dve):
                dve.wait_ge(set_pool, 1)
                dve.tensor_copy(lag[:, :], lag_i[:, :]).then_inc(set_dve, 1)
                dve.wait_ge(set_dve, 1)
                dve.tensor_scalar(lag[:, :], lag[:, :], 1.0, None, ALU.max).then_inc(set_dve, 1)
                for q in range(HQ):
                    dve.tensor_copy(turn_l[:, q, :].rearrange("p (e r g) -> p e r g", e=2, r=HQ),
                                    ident[0:L, 0:L].rearrange("p (g r e) -> p e r g", r=HQ, e=2)).then_inc(set_dve, 1)
                dve.tensor_copy(hh_wide[:, :, :], hh_of[:, :].unsqueeze(2).to_broadcast([P, HQ, TB])).then_inc(set_dve, 1)
                dve.wait_ge(set_pool, 6)
                dve.tensor_copy(lag_p[:, :].rearrange("p (e r g) -> p e r g", e=2, r=HQ),
                                lag_ln[:, :].rearrange("p (g r e) -> p e r g", r=HQ, e=2)).then_inc(set_dve, 1)
                dve.wait_ge(set_pe, 1)
                dve.tensor_copy(decay[:, :, :], PA[:, 0:L].unsqueeze(1).to_broadcast([P, HB * NQ, L])).then_inc(set_dve, 1)
                dve.tensor_copy(bcol[:, :], PA[:, 64:67]).then_inc(set_dve, 1)
                dve.wait_ge(set_pe, 2)
                dve.tensor_copy(out_bias[:, :], PA[:, 128:128 + D]).then_inc(set_dve, 1)

            @block.scalar
            def _(act):
                act.wait_ge(set_dve, 2)
                act.activation(lag_ln[:, :], lag[:, :], ACT.Ln).then_inc(set_act, 1)
                act.wait_ge(set_act, 1)
                act.activation(lag_ln[:, :], lag_ln[:, :], ACT.Copy, scale=DECAY).then_inc(set_act, 1)

            @block.tensor
            def _(pe):
                pe.wait_ge(set_dve, 8)
                pe.wait_ge(w_in, 16 * 8)
                pe.matmul(PA[:, 0:L], turn_l[:, :, :].rearrange("p q l -> p (q l)"), lag_p[:, :], start=True, stop=True)
                pe.transpose(PA[:, 64:67], brow[:, :], ident[0:3, 0:3]).then_inc(set_pe, 1)
                pe.wait_ge(set_dve, 10)
                pe.matmul(PA[:, 128:128 + D], bcol[:, 2:3].to_broadcast([P, P]), W["o"][:, :], start=True, stop=False)
                pe.matmul(PA[:, 128:128 + D], ones_row[:, :], bo_row[:, :], start=False, stop=True).then_inc(set_pe, 1)

        n_stat, n_mv, n_var, n_rs, n_xn = sem("n_stat"), sem("n_mv"), sem("n_var"), sem("n_rs"), sem("n_xn")
        xt_ps, xt_sb, xt4_sb = sem("xt_ps"), sem("xt_sb"), sem("xt4_sb")
        qk_ps, qt_sb, q_bd, k_bd = sem("qk_ps"), sem("qt_sb2"), sem("q_bd2"), sem("k_bd")
        v_ps, v_bd = [sem(f"v_ps{h}") for h in range(2)], [sem(f"v_bd{h}") for h in range(2)]
        s_ps, s_sb, m_sb, d_sb = sem("s_ps"), sem("s_sb"), sem("m_sb"), sem("d_sb")
        e_sb, sum_sb, inv_sb, en_sb = sem("e_sb"), sem("sum_sb"), sem("inv_sb"), sem("en_sb")
        et_ps, et_sb = sem("et_ps2"), sem("et_sb2")
        o_ps, o_sb = sem("o_ps2"), sem("o_sb2")
        y_ps, x2, xb = sem("y_ps"), sem("x2"), sem("xb")

        def tile_of(t):
            return X[:, t, :] if isinstance(t, int) else X[:, bass.ds(t, 1), :].rearrange("p a c -> p (a c)")

        def run(body, eng):
            body(0, True, False)
            body(1, True, True)
            with eng.Fori(2, T) as t:
                body(t, True, True)
            body(T, False, True)

        def later(t, k=1):
            return not (isinstance(t, int) and t < k)

        with nc.Block() as block:
            @block.vector
            def _(dve):
                def norm_stats(t):
                    xt = tile_of(t)
                    for e in range(2):
                        i = dve.bn_stats(stat[:, e, :], xt[:, e * D:(e + 1) * D])
                    i.then_inc(n_stat, 1)
                    dve.wait_ge(n_stat, t + 1)
                    dve.nop(nofuse=True)
                    for e in range(2):
                        i = dve.bn_aggr(mv[:, e, :], stat[:, e, :])
                    i.then_inc(n_mv, 1)
                    dve.wait_ge(n_mv, t + 1)
                    dve.tensor_scalar(var[:, :], mv[:, :, 1], EPS_LN, None, ALU.add).then_inc(n_var, 1)

                def norm(t):
                    dve.wait_ge(n_rs, t + 1)
                    if later(t):
                        dve.wait_ge(xt_ps, t)
                    xt = tile_of(t)
                    for e in range(2):
                        i = dve.tensor_scalar(xn[:, e, :], xt[:, e * D:(e + 1) * D], mv[:, e, 0:1], rs[:, e:e + 1],
                                              ALU.subtract, ALU.mult)
                    i.then_inc(n_xn, 1)

                def softmax_front(t, h):
                    m = 2 * t + h
                    dve.wait_ge(s_ps, m + 1)
                    if later(t):
                        dve.wait_ge(en_sb, m - 1)
                    flat = E[:, h, :, :].rearrange("p u s -> p (u s)")
                    dve.tensor_tensor(flat, PS[h][:, :], decay[:, :, :].rearrange("p u s -> p (u s)"), ALU.add).then_inc(s_sb, 1)
                    dve.wait_ge(s_sb, m + 1)
                    dve.tensor_reduce(mx[:, h, :], E[:, h, :, :], AX.X, ALU.max).then_inc(m_sb, 1)
                    dve.wait_ge(m_sb, m + 1)
                    dve.tensor_tensor(E[:, h, :, :], E[:, h, :, :], mx[:, h, :].unsqueeze(2).to_broadcast([P, HB * NQ, L]),
                                      ALU.subtract).then_inc(d_sb, 1)

                def softmax_sums(t, h):
                    m = 2 * t + h
                    dve.wait_ge(e_sb, m + 1)
                    dve.tensor_reduce(sm[:, h, :], E[:, h, :, :], AX.X, ALU.add).then_inc(sum_sb, 1)
                    dve.wait_ge(sum_sb, m + 1)
                    dve.reciprocal(sm[:, h, :], sm[:, h, :]).then_inc(inv_sb, 1)

                def own(t, h):
                    m = 2 * t + h
                    dve.wait_ge(o_ps, m + 1)
                    if later(t):
                        dve.wait_ge(y_ps, t)
                    dve.tensor_tensor(Oc[:, :, HB * h:HB * h + HB, :].rearrange("p a b g -> p b a g"),
                                      PE_[h][:, :, :].rearrange("p j (a g) -> p j a g", g=NQ),
                                      hh_wide[:, :, :].rearrange("p q a -> p (q a)").unsqueeze(1).unsqueeze(3).to_broadcast(
                                          [P, HB, HQ * TB, NQ]), ALU.mult).then_inc(o_sb, 1)

                def add(t):
                    dve.wait_ge(y_ps, t + 1)
                    dve.wait_ge(xb, t + 1)
                    dve.tensor_tensor(tile_of(t), PY[:, :], Xb[:, :], ALU.add).then_inc(x2, 1)

                def body(t, front, back):
                    if front:
                        norm(t)
                    if back:
                        own(t - 1, 0)
                    if back:
                        own(t - 1, 1)
                    if front:
                        softmax_front(t, 0)
                        softmax_front(t, 1)
                        norm_stats(t + 1)
                        softmax_sums(t, 0)
                        softmax_sums(t, 1)
                    if back:
                        add(t - 1)

                norm_stats(0)
                body(0, True, False)
                body(1, True, True)
                with dve.Fori(2, T - 1) as t:
                    body(t, True, True)
                norm(T - 1)
                own(T - 2, 0)
                own(T - 2, 1)
                for h in range(2):
                    softmax_front(T - 1, h)
                for h in range(2):
                    softmax_sums(T - 1, h)
                add(T - 2)
                own(T - 1, 0)
                own(T - 1, 1)
                add(T - 1)

            @block.gpsimd
            def _(pool):
                def front(t):
                    pool.wait_ge(qt_sb, t + 1)
                    if later(t):
                        pool.wait_ge(s_ps, 2 * t)
                    pool.tensor_tensor(Qbd[:, :, :, :], Qt[:, :, :].unsqueeze(2).to_broadcast([P, TB, HQ, L]),
                                       hh_scaled[:, :, :].unsqueeze(1).to_broadcast([P, TB, HQ, L]), ALU.mult).then_inc(q_bd, 1)

                def normalise(t, h):
                    m = 2 * t + h
                    pool.wait_ge(inv_sb, m + 1)
                    if later(t):
                        pool.wait_ge(et_ps, m - 1)
                    pool.tensor_tensor(En[:, h, :, :], E[:, h, :, :], sm[:, h, :].unsqueeze(2).to_broadcast([P, HB * NQ, L]),
                                       ALU.mult).then_inc(en_sb, 1)

                def power(t):
                    pool.wait_ge(n_var, t + 1)
                    if later(t):
                        pool.wait_ge(n_xn, t)
                    pool.tensor_tensor(rs[:, :], var[:, :], neg_half[:, :], ALU.pow).then_inc(n_rs, 1)

                def bias(t):
                    pool.wait_ge(n_xn, t + 1)
                    if later(t):
                        pool.wait_ge(x2, t)
                    xt = tile_of(t)
                    pool.tensor_tensor(Xb[:, :].rearrange("p (e c) -> p e c", e=2), xt.rearrange("p (e c) -> p e c", e=2),
                                       out_bias[:, :].unsqueeze(1).to_broadcast([P, 2, D]), ALU.add).then_inc(xb, 1)

                def body(t, last=False):
                    front(t)
                    if not last:
                        power(t + 1)
                    normalise(t, 0)
                    normalise(t, 1)
                    bias(t)

                pool.wait_ge(set_dve, 11)
                power(0)
                body(0)
                with pool.Fori(1, T - 1) as t:
                    body(t)
                body(T - 1, last=True)

            @block.scalar
            def _(act):
                def turned(t):
                    act.wait_ge(xt_ps, t + 1)
                    if later(t):
                        act.wait_ge(v_ps[1], t)
                    for e in range(2):
                        i = act.activation(xT[:, :, 16 * e:16 * e + 16].rearrange("p b (q g) -> p q b g", q=HQ),
                                           PA[:, e * P:(e + 1) * P].rearrange("p (q b g) -> p q b g", q=HQ, b=TB), ACT.Copy)
                    i.then_inc(xt_sb, 1)

                def repeated(t):
                    act.wait_ge(xt_sb, t + 1)
                    act.activation(xT4[:, :, :, :], xT[:, :, :].unsqueeze(2).to_broadcast([P, TB, NQ, L]), ACT.Copy).then_inc(xt4_sb, 1)

                def projected(t):
                    act.wait_ge(qk_ps, t + 1)
                    if later(t):
                        act.wait_ge(q_bd, t)
                    act.activation(Qt[:, :, :].rearrange("p b l -> p (b l)"), PA[:, 0:256], ACT.Identity,
                                   bias=bcol[:, 0:1]).then_inc(qt_sb, 1)
                    if later(t):
                        act.wait_ge(s_ps, 2 * t)
                    for g in range(NQ):
                        r = slice(32 * g, 32 * g + 32)
                        i = act.activation(Kbd[r, :, g, :], PA[r, 256:512].rearrange("p (b s) -> p b s", b=TB), ACT.Identity,
                                           bias=bcol[r, 1:2])
                    i.then_inc(k_bd, 1)

                def values(t, h):
                    act.wait_ge(v_ps[h], t + 1)
                    if later(t):
                        act.wait_ge(o_ps, 2 * t - 1 + h)
                    for g in range(NQ):
                        r = slice(32 * g, 32 * g + 32)
                        i = act.activation(Vbd[r, 0, HB * h:HB * h + HB, 32 * g:32 * g + 32],
                                           PV[h][r, :, 32 * g:32 * g + 32], ACT.Copy)
                    i.then_inc(v_bd[h], 1)

                def exponentials(t, h):
                    act.wait_ge(d_sb, 2 * t + h + 1)
                    flat = E[:, h, :, :].rearrange("p u s -> p (u s)")
                    act.activation(flat, flat, ACT.Exp).then_inc(e_sb, 1)

                def probs(t, h):
                    m = 2 * t + h
                    act.wait_ge(et_ps, m + 1)
                    if later(t):
                        act.wait_ge(o_ps, m - 1)
                    act.activation(Et[:, h, :, :], PE_[h][:, :, :], ACT.Copy).then_inc(et_sb, 1)

                def body(t, front, back):
                    if front:
                        turned(t)
                    if back:
                        probs(t - 1, 0)
                    if front:
                        projected(t)
                        repeated(t)
                    if back:
                        probs(t - 1, 1)
                    if front:
                        values(t, 0)
                        values(t, 1)
                        exponentials(t, 0)
                        exponentials(t, 1)

                act.wait_ge(set_pool, 6)
                act.wait_ge(set_dve, 11)
                run(body, act)

            @block.tensor
            def _(pe):
                def turn(t):
                    pe.wait_ge(n_xn, t + 1)
                    if later(t):
                        pe.wait_ge(k_bd, t)
                    for e in range(2):
                        i = pe.transpose(PA[:, e * P:(e + 1) * P], xn[:, e, :], ident[:, :])
                    i.then_inc(xt_ps, 1)

                def project(t):
                    pe.wait_ge(xt_sb, t + 1)
                    rhs = xT[:, :, :].rearrange("p b l -> p (b l)")
                    pe.matmul(PA[:, 0:256], W["q"][:, :], rhs, start=True, stop=True)
                    pe.matmul(PA[:, 256:512], W["k"][:, :], rhs, start=True, stop=True).then_inc(qk_ps, 1)

                def values(t, h):
                    if later(t):
                        pe.wait_ge(v_bd[h], t)
                    pe.wait_ge(xt4_sb, t + 1)
                    for j in range(HB):
                        i = pe.matmul(PV[h][:, j, :], xT4[:, HB * h + j, :, :].rearrange("p g l -> p (g l)"), W["v"][:, :],
                                      start=True, stop=True)
                    i.then_inc(v_ps[h], 1)

                def scores(t, h):
                    m = 2 * t + h
                    if h == 0:
                        pe.wait_ge(q_bd, t + 1)
                        pe.wait_ge(k_bd, t + 1)
                    if later(t):
                        pe.wait_ge(s_sb, m - 1)
                    for j in range(HB):
                        b = HB * h + j
                        i = pe.matmul(PS[h][:, j * P:(j + 1) * P], Qbd[:, b, :, :].rearrange("p q l -> p (q l)"),
                                      Kbd[:, b, :, :].rearrange("p g s -> p (g s)"), start=True, stop=True)
                    i.then_inc(s_ps, 1)

                def turn_probs(t, h):
                    m = 2 * t + h
                    pe.wait_ge(en_sb, m + 1)
                    if later(t):
                        pe.wait_ge(o_sb, m - 1)
                    for j in range(HB):
                        i = pe.transpose(PE_[h][:, j, :], En[:, h, NQ * j:NQ * j + NQ, :].rearrange("p g s -> p (g s)"),
                                         ident[:, :])
                    i.then_inc(et_ps, 1)

                def weigh(t, h):
                    m = 2 * t + h
                    pe.wait_ge(et_sb, m + 1)
                    pe.wait_ge(v_bd[h], t + 1)
                    for j in range(HB):
                        i = pe.matmul(PE_[h][:, j, :], Vbd[:, 0, HB * h + j, :], Et[:, h, j, :], start=True, stop=True)
                    i.then_inc(o_ps, 1)

                def project_out(t):
                    pe.wait_ge(o_sb, 2 * t + 2)
                    if later(t):
                        pe.wait_ge(x2, t)
                    for e in range(2):
                        for q in range(HQ):
                            a = TB * q + HQ * e
                            i = pe.matmul(PY[:, e * D:(e + 1) * D], Oc[:, a:a + HQ, :, :].rearrange("p a b g -> p (a b g)"),
                                          W["o"][:, :], start=(q == 0), stop=(q == HQ - 1))
                    i.then_inc(y_ps, 1)

                def body(t, front, back):
                    if front:
                        turn(t)
                    if back:
                        turn_probs(t - 1, 0)
                    if front:
                        project(t)
                    if back:
                        turn_probs(t - 1, 1)
                        weigh(t - 1, 0)
                        weigh(t - 1, 1)
                    if front:
                        values(t, 0)
                        scores(t, 0)
                        scores(t, 1)
                        values(t, 1)
                    if back:
                        project_out(t - 1)

                run(body, pe)


def mix_experts(nc, es, X, ident, gate_w, w1, b1, w2, b2, ln_g, ln_b, out):
    with ExitStack() as s3:
        def sb(name, shape, dt=F32):
            return s3.enter_context(nc.sbuf_tensor(name, shape, dt))

        def ps(name, shape):
            return s3.enter_context(nc.psum_tensor(name, shape, F32))

        def sem(name):
            return s3.enter_context(nc.semaphore(name))

        FH = F // P
        NP = NE // 2
        G = sb("G3", [P, NE])
        W1 = sb("W13", [P, NE, F])
        W2 = sb("W23", [P, NE, FH, D])
        b1_rows = sb("b1_rows", [NE * FH, P])
        b1c = sb("b1c", [P, NE * FH])
        b2r = sb("b2r", [P, NE, D])
        gr = sb("gr", [P, NE, D])
        b_rows = sb("b_rows", [NE, D])
        iota_i = sb("iota_i", [P, NE], I32)
        iota_f = sb("iota_f", [P, NE])
        neg_half = sb("neg_half3", [P, 4])
        stat = sb("stat3", [P, 2, 6])
        mv = sb("mv3", [P, 2, 2])
        var = sb("var3", [P, 2])
        rs = sb("rs3", [P, 2])
        xn = sb("xn3", [P, 2, D])
        xT = sb("xT3", [P, 2 * P])
        XB = sb("XB", [P, NE, 2, D])
        gs = sb("gs", [P, 2, NE])
        top = sb("top", [P, 2, 8])
        top_i = sb("top_i", [P, 2, 8], U32)
        top_f = sb("top_f", [P, 2, 2])
        gap = sb("gap", [P, 2])
        th = sb("th", [P, 2])
        pr = sb("pr", [P, 2, 2])
        hot = sb("hot", [P, 2, 2, NE])
        wt = sb("wt", [P, 2, NE])
        wT = sb("wT", [NE, 2 * P])
        hid = sb("hid", [P, 2, FH, 2 * P])
        Z = sb("Z", [P, 2, 4, D])
        zstat = sb("zstat", [P, 2, 4, 6])
        zm = sb("zm", [P, 2, 4])
        zd = sb("zd", [P, 2, 4])
        zv = sb("zv", [P, 2, 4])
        zr = sb("zr", [P, 2, 4])
        zs = sb("zs", [P, 2, 4])
        zb = sb("zb", [P, 2, 4])
        Y = sb("Y", [P, 2, 4, D])
        U = sb("U", [P, 2, 4, D])
        acc = sb("acc", [P, 4, D])
        res = sb("res", [P, 2 * D])
        Xo = sb("Xo", [P, 2, 2 * D])

        PH = [ps(f"PH{i}", [P, FH, 2 * P]) for i in range(2)]
        PO = [ps(f"PO{i}", [P, 4, D]) for i in range(2)]
        PA = ps("PA3", [P, 512])
        PW = ps("PW3", [P, 512])
        PB = ps("PB3", [P, 2 * D])

        w_in, set_pool, set_pe, set_dve = sem("w_in3"), sem("set_pool3"), sem("set_pe3"), sem("set_dve3")
        n_stat, n_mv, n_var, n_rs, n_xn = sem("n_stat3"), sem("n_mv3"), sem("n_var3"), sem("n_rs3"), sem("n_xn3")
        xt_ps, xt_sb, xb_sb = sem("xt_ps3"), sem("xt_sb3"), sem("xb_sb3")
        g_ps, g_sb, t_max, t_idx, t_gap, t_th, t_pr, t_hot, w_sb = (sem(n) for n in (
            "g_ps", "g_sb", "t_max", "t_idx", "t_gap", "t_th", "t_pr", "t_hot", "w_sb"))
        wt_ps, wt_sb, b_ps = sem("wt_ps3"), sem("wt_sb3"), sem("b_ps3")
        h_ps, h_sb, o_ps = sem("h_ps3"), sem("h_sb3"), sem("o_ps3")
        z_sb, z_st, z_m, z_v, z_r, z_s, z_b, y_sb, u_sb, acc_sb = (sem(n) for n in (
            "z_sb", "z_st", "z_m", "z_v", "z_r", "z_s", "z_b", "y_sb3", "u_sb3", "acc_sb"))
        r1, r2, x3 = sem("r1"), sem("r2"), sem("x3")
        stored = [sem("stored")]

        def tile_of(t):
            return X[:, t, :] if isinstance(t, int) else X[:, bass.ds(t, 1), :].rearrange("p a c -> p (a c)")

        def later(t):
            return not (isinstance(t, int) and t == 0)

        def run(slots, eng):
            slots(0)
            slots(1)
            with eng.Fori(2, T - 1) as t:
                slots(t)
            slots(T - 1)

        block = s3.enter_context(nc.Block())

        @block.sync
        def _(sp):
            sp.dma_start(W1[:, :, :], w1.rearrange("e c f -> c e f")).then_inc(w_in, 16)
            sp.dma_start(G[:, :], gate_w).then_inc(w_in, 16)
            sp.dma_start(b1_rows[:, :], b1.rearrange("e (a f) -> (e a) f", a=FH)).then_inc(w_in, 16)
            for a in range(FH):
                sp.dma_start(W2[:, :, a, :], w2[:, a * P:(a + 1) * P, :].rearrange("e f d -> f e d")).then_inc(w_in, 16)
            sp.dma_start(b2r[:, :, :].rearrange("p e d -> p (e d)"),
                         b2.rearrange("e d -> (e d)").unsqueeze(0).to_broadcast([P, NE * D])).then_inc(w_in, 16)
            sp.dma_start(gr[:, :, :].rearrange("p e d -> p (e d)"),
                         ln_g.rearrange("e d -> (e d)").unsqueeze(0).to_broadcast([P, NE * D])).then_inc(w_in, 16)
            sp.dma_start(b_rows[:, :], ln_b).then_inc(w_in, 16)

            def keep(t):
                sp.wait_ge(x3, t + 1)
                for q in range(HQ):
                    sp.dma_start(out[bass.ds(TB * t, TB), :, :].rearrange("b (g q e) c -> q b g (e c)", g=NQ, q=HQ)[q],
                                 Xo[32 * q:32 * q + 32, 0, :]).then_inc(stored[0], 16)

            keep(0)
            with sp.Fori(1, T) as t:
                keep(t)
            sp.wait_ge(stored[0], 16 * HQ * T)

        @block.gpsimd
        def _(pool):
            pool.iota(iota_i[:, :], pattern=[[1, NE]], base=0, channel_multiplier=0).then_inc(set_pool, 1)
            pool.memset(neg_half[:, :], -0.5).then_inc(set_pool, 1)
            pool.wait_ge(w_in, 16 * 8)
            pool.wait_ge(set_pool, 2)

            def power(t):
                pool.wait_ge(n_var, t + 1)
                if later(t):
                    pool.wait_ge(n_xn, t)
                pool.tensor_tensor(rs[:, :], var[:, :], neg_half[:, 0:2], ALU.pow).then_inc(n_rs, 1)

            def spread(t, p):
                pool.wait_ge(n_xn, t + 1)
                if later(t):
                    pool.wait_ge(z_sb, NP * (t - 1) + p + 1)
                pool.tensor_tensor(XB[:, 2 * p:2 * p + 2, :, :], xn[:, :, :].unsqueeze(1).to_broadcast([P, 2, 2, D]),
                                   b2r[:, 2 * p:2 * p + 2, :].unsqueeze(2).to_broadcast([P, 2, 2, D]), ALU.add).then_inc(xb_sb, 1)

            def inverse(t, p):
                n = NP * t + p
                pool.wait_ge(z_v, n + 1)
                if not (isinstance(t, int) and t == 0 and p < 2):
                    pool.wait_ge(z_s, n - 1)
                pool.tensor_tensor(zr[:, p % 2, :], zv[:, p % 2, :], neg_half[:, :], ALU.pow).then_inc(z_r, 1)

            def gather(t, p):
                pool.wait_ge(u_sb, NP * t + p + 1)
                if p == 1:
                    if later(t):
                        pool.wait_ge(r1, t)
                    pool.tensor_tensor(acc[:, :, :], U[:, 0, :, :], U[:, 1, :, :], ALU.add).then_inc(acc_sb, 1)
                else:
                    pool.wait_ge(acc_sb, (NP - 1) * t + p - 1)
                    pool.tensor_tensor(acc[:, :, :], acc[:, :, :], U[:, p % 2, :, :], ALU.add).then_inc(acc_sb, 1)

            def slots(t):
                last = isinstance(t, int) and t == T - 1
                spread(t, 0)
                if later(t):
                    inverse(t - 1, NP - 1)
                    gather(t - 1, NP - 2)
                spread(t, 1)
                spread(t, 2)
                inverse(t, 0)
                if later(t):
                    gather(t - 1, NP - 1)
                spread(t, 3)
                if not last:
                    power(t + 1)
                inverse(t, 1)
                inverse(t, 2)
                gather(t, 1)

            power(0)
            run(slots, pool)
            inverse(T - 1, NP - 1)
            gather(T - 1, NP - 2)
            gather(T - 1, NP - 1)

        @block.tensor
        def _(pe):
            def turn(t):
                pe.wait_ge(n_xn, t + 1)
                if later(t):
                    pe.wait_ge(g_sb, t)
                for e in range(2):
                    i = pe.transpose(PA[:, e * P:(e + 1) * P], xn[:, e, :], ident[:, :])
                i.then_inc(xt_ps, 1)

            def gates(t):
                for e in range(2):
                    i = pe.matmul(PA[:, 256 + NE * e:256 + NE * e + NE], xT[:, e * P:(e + 1) * P], G[:, :], start=True, stop=True)
                i.then_inc(g_ps, 1)

            def turn_weights(t):
                pe.wait_ge(w_sb, t + 1)
                if later(t):
                    pe.wait_ge(wt_sb, t)
                for e in range(2):
                    i = pe.transpose(PW[0:NE, e * P:(e + 1) * P], wt[:, e, :], ident[:, :])
                i.then_inc(wt_ps, 1)

            def mix_bias(t):
                pe.wait_ge(wt_sb, t + 1)
                if later(t):
                    pe.wait_ge(r2, t)
                for e in range(2):
                    i = pe.matmul(PB[:, e * D:(e + 1) * D], wT[:, e * P:(e + 1) * P], b_rows[:, :], start=True, stop=True)
                i.then_inc(b_ps, 1)

            def first(t, x):
                n = NE * t + x
                if x == 0:
                    pe.wait_ge(xt_sb, t + 1)
                if not (isinstance(t, int) and t == 0 and x < 2):
                    pe.wait_ge(h_sb, n - 1)
                for a in range(FH):
                    i = pe.matmul(PH[x % 2][:, a, :], W1[:, x, a * P:(a + 1) * P], xT[:, :], start=True, stop=True)
                i.then_inc(h_ps, 1)

            def second(t, x):
                n = NE * t + x
                pe.wait_ge(h_sb, n + 1)
                p = x // 2
                if x % 2 == 0 and not (isinstance(t, int) and t == 0 and p < 2):
                    pe.wait_ge(z_sb, NP * t + p - 1)
                for e in range(2):
                    for a in range(FH):
                        i = pe.matmul(PO[p % 2][:, 2 * (x % 2) + e, :], hid[:, x % 2, a, e * P:(e + 1) * P], W2[:, x, a, :],
                                      start=(a == 0), stop=(a == FH - 1))
                i.then_inc(o_ps, 1)

            def slots(t):
                last = isinstance(t, int) and t == T - 1
                for x in range(NE):
                    first(t, x)
                    if x == 0:
                        gates(t)
                    if x == NE - 1 and not last:
                        turn(t + 1)
                    if x > 0:
                        second(t, x - 1)
                    elif later(t):
                        second(t - 1, NE - 1)
                    if x == 2:
                        turn_weights(t)
                    if x == 5:
                        mix_bias(t)

            pe.wait_ge(w_in, 16 * 8)
            pe.transpose(PW[:, 0:NE * FH], b1_rows[:, :], ident[0:NE * FH, 0:NE * FH]).then_inc(set_pe, 1)
            pe.wait_ge(set_dve, 1)
            turn(0)
            run(slots, pe)
            second(T - 1, NE - 1)

        @block.scalar
        def _(act):
            def turned(t):
                act.wait_ge(xt_ps, t + 1)
                if later(t):
                    act.wait_ge(h_ps, NE * t)
                    act.wait_ge(g_ps, t)
                act.activation(xT[:, :], PA[:, 0:256], ACT.Copy).then_inc(xt_sb, 1)

            def gelu(t, x):
                n = NE * t + x
                act.wait_ge(h_ps, n + 1)
                if not (isinstance(t, int) and t == 0 and x < 2):
                    act.wait_ge(o_ps, n - 1)
                for a in range(FH):
                    i = act.activation(hid[:, x % 2, a, :], PH[x % 2][:, a, :], ACT.Gelu, bias=b1c[:, FH * x + a:FH * x + a + 1])
                i.then_inc(h_sb, 1)

            def half_tangent(t):
                act.wait_ge(t_gap, t + 1)
                if later(t):
                    act.wait_ge(t_pr, t)
                act.activation(th[:, :], gap[:, :], ACT.Tanh, scale=0.5).then_inc(t_th, 1)

            def weights(t):
                act.wait_ge(wt_ps, t + 1)
                if later(t):
                    act.wait_ge(b_ps, t)
                act.activation(wT[:, :], PW[0:NE, 0:2 * P], ACT.Copy).then_inc(wt_sb, 1)

            def scaled(t, p):
                n = NP * t + p
                act.wait_ge(z_b, n + 1)
                if not (isinstance(t, int) and t == 0 and p < 2):
                    act.wait_ge(u_sb, n - 1)
                for k in range(4):
                    i = act.activation(Y[:, p % 2, k, :], Z[:, p % 2, k, :], ACT.Identity, scale=zs[:, p % 2, k:k + 1],
                                       bias=zb[:, p % 2, k:k + 1])
                i.then_inc(y_sb, 1)

            def slots(t):
                last = isinstance(t, int) and t == T - 1
                for x in range(NE):
                    if x == NE - 1 and not last:
                        gelu(t, x)
                        turned(t + 1)
                    else:
                        gelu(t, x)
                    if x == 1:
                        half_tangent(t)
                        if later(t):
                            scaled(t - 1, NP - 1)
                    if x == 2:
                        weights(t)
                    if x % 2 == 1 and x > 1:
                        scaled(t, (x - 3) // 2)

            act.wait_ge(set_dve, 1)
            turned(0)
            run(slots, act)
            scaled(T - 1, NP - 1)

        @block.vector
        def _(dve):
            def norm_stats(t):
                xt = tile_of(t)
                for e in range(2):
                    i = dve.bn_stats(stat[:, e, :], xt[:, e * D:(e + 1) * D])
                i.then_inc(n_stat, 1)
                dve.wait_ge(n_stat, t + 1)
                dve.nop(nofuse=True)
                for e in range(2):
                    i = dve.bn_aggr(mv[:, e, :], stat[:, e, :])
                i.then_inc(n_mv, 1)
                dve.wait_ge(n_mv, t + 1)
                dve.tensor_scalar(var[:, :], mv[:, :, 1], EPS_LN, None, ALU.add).then_inc(n_var, 1)

            def norm(t):
                dve.wait_ge(n_rs, t + 1)
                if later(t):
                    dve.wait_ge(xt_ps, t)
                    dve.wait_ge(xb_sb, NP * t)
                xt = tile_of(t)
                for e in range(2):
                    i = dve.tensor_scalar(xn[:, e, :], xt[:, e * D:(e + 1) * D], mv[:, e, 0:1], rs[:, e:e + 1],
                                          ALU.subtract, ALU.mult)
                i.then_inc(n_xn, 1)

            def choose(t):
                dve.wait_ge(g_ps, t + 1)
                dve.tensor_copy(gs[:, :, :], PA[:, 256:256 + 2 * NE].rearrange("p (e x) -> p e x", e=2)).then_inc(g_sb, 1)
                dve.wait_ge(g_sb, t + 1)
                dve.nop(nofuse=True)
                for e in range(2):
                    i = dve.max(top[:, e, :], gs[:, e, :])
                i.then_inc(t_max, 1)
                dve.wait_ge(t_max, t + 1)
                dve.tensor_tensor(gap[:, :], top[:, :, 0], top[:, :, 1], ALU.subtract).then_inc(t_gap, 1)
                for e in range(2):
                    i = dve.max_index(top_i[:, e, :], top[:, e, :], gs[:, e, :])
                i.then_inc(t_idx, 1)
                dve.wait_ge(t_idx, 2 * t + 1)
                dve.tensor_copy(top_f[:, :, :], top_i[:, :, 0:2]).then_inc(t_idx, 1)

            def weigh(t):
                dve.wait_ge(t_th, t + 1)
                dve.tensor_scalar(pr[:, :, 0], th[:, :], 0.5, 0.5, ALU.mult, ALU.add)
                dve.tensor_scalar(pr[:, :, 1], th[:, :], -0.5, 0.5, ALU.mult, ALU.add).then_inc(t_pr, 1)
                dve.wait_ge(t_pr, t + 1)
                dve.wait_ge(t_idx, 2 * t + 2)
                for e in range(2):
                    for k in range(2):
                        i = dve.tensor_scalar(hot[:, e, k, :], iota_f[:, :], top_f[:, e, k:k + 1], pr[:, e, k:k + 1],
                                              ALU.is_equal, ALU.mult)
                i.then_inc(t_hot, 1)
                dve.wait_ge(t_hot, t + 1)
                if later(t):
                    dve.wait_ge(wt_ps, t)
                dve.tensor_tensor(wt[:, :, :], hot[:, :, 0, :], hot[:, :, 1, :], ALU.add).then_inc(w_sb, 1)

            def stats(t, p):
                n = NP * t + p
                k = p % 2
                dve.wait_ge(o_ps, NE * t + 2 * p + 2)
                dve.wait_ge(xb_sb, n + 1)
                if not (isinstance(t, int) and t == 0 and p < 2):
                    dve.wait_ge(y_sb, n - 1)
                dve.tensor_tensor(Z[:, k, :, :], PO[k][:, :, :], XB[:, 2 * p:2 * p + 2, :, :].rearrange("p x e d -> p (x e) d"),
                                  ALU.add).then_inc(z_sb, 1)
                dve.wait_ge(z_sb, n + 1)
                for i4 in range(4):
                    i = dve.bn_stats(zstat[:, k, i4, :], Z[:, k, i4, :])
                i.then_inc(z_st, 1)
                dve.wait_ge(z_st, n + 1)
                dve.tensor_tensor(zd[:, k, :], zstat[:, k, :, 1], zstat[:, k, :, 4], ALU.subtract)
                dve.tensor_tensor(zv[:, k, :], zstat[:, k, :, 2], zstat[:, k, :, 5], ALU.add)
                dve.tensor_tensor(zm[:, k, :], zstat[:, k, :, 1], zstat[:, k, :, 4], ALU.add).then_inc(z_m, 1)
                dve.wait_ge(z_m, 2 * n + 1)
                dve.tensor_tensor(zd[:, k, :], zd[:, k, :], zd[:, k, :], ALU.mult)
                dve.tensor_scalar(zv[:, k, :], zv[:, k, :], 1.0 / D, EPS_EXPERT, ALU.mult, ALU.add).then_inc(z_m, 1)
                dve.wait_ge(z_m, 2 * n + 2)
                dve.scalar_tensor_tensor(zv[:, k, :], zd[:, k, :], 0.25, zv[:, k, :], ALU.mult, ALU.add).then_inc(z_v, 1)

            def factors(t, p):
                n = NP * t + p
                k = p % 2
                dve.wait_ge(z_r, n + 1)
                dve.wait_ge(w_sb, t + 1)
                if not (isinstance(t, int) and t == 0 and p < 2):
                    dve.wait_ge(y_sb, n - 1)
                dve.tensor_tensor(zs[:, k, :].rearrange("p (x e) -> p e x", x=2), zr[:, k, :].rearrange("p (x e) -> p e x", x=2),
                                  wt[:, :, 2 * p:2 * p + 2], ALU.mult).then_inc(z_s, 1)
                dve.wait_ge(z_s, n + 1)
                dve.scalar_tensor_tensor(zb[:, k, :], zm[:, k, :], -0.5, zs[:, k, :], ALU.mult, ALU.mult).then_inc(z_b, 1)

            def gained(t, p):
                n = NP * t + p
                k = p % 2
                dve.wait_ge(y_sb, n + 1)
                if p >= 2:
                    dve.wait_ge(acc_sb, (NP - 1) * t + 1)
                elif later(t):
                    dve.wait_ge(acc_sb, (NP - 1) * (t - 1) + 2 + p)
                dve.tensor_tensor(U[:, k, :, :].rearrange("p (x e) d -> p x e d", x=2),
                                  Y[:, k, :, :].rearrange("p (x e) d -> p x e d", x=2),
                                  gr[:, 2 * p:2 * p + 2, :].unsqueeze(2).to_broadcast([P, 2, 2, D]), ALU.mult).then_inc(u_sb, 1)

            def finish(t):
                dve.wait_ge(acc_sb, (NP - 1) * t + NP - 1)
                dve.tensor_tensor(res[:, :].rearrange("p (e d) -> p e d", e=2), acc[:, 0:2, :], acc[:, 2:4, :], ALU.add).then_inc(r1, 1)
                dve.wait_ge(b_ps, t + 1)
                dve.wait_ge(r1, t + 1)
                dve.tensor_tensor(res[:, :], res[:, :], PB[:, :], ALU.add).then_inc(r2, 1)
                dve.wait_ge(r2, t + 1)
                if later(t):
                    dve.wait_ge(stored[0], 16 * HQ * t)
                dve.tensor_tensor(Xo[:, 0, :], res[:, :], tile_of(t), ALU.add).then_inc(x3, 1)

            def slots(t):
                last = isinstance(t, int) and t == T - 1
                for x in range(NE):
                    if x == 0:
                        if later(t):
                            stats(t - 1, NP - 1)
                        choose(t)
                    if x == 1:
                        if later(t):
                            factors(t - 1, NP - 1)
                            gained(t - 1, NP - 2)
                        weigh(t)
                    if x == 2:
                        stats(t, 0)
                        if later(t):
                            gained(t - 1, NP - 1)
                    if x == 3:
                        factors(t, 0)
                        if not last:
                            norm_stats(t + 1)
                        if later(t):
                            finish(t - 1)
                    if x == 4:
                        stats(t, 1)
                        gained(t, 0)
                    if x == 5:
                        factors(t, 1)
                    if x == 6:
                        stats(t, 2)
                        gained(t, 1)
                        if not last:
                            norm(t + 1)
                    if x == 7:
                        factors(t, 2)

            dve.wait_ge(set_pool, 2)
            dve.tensor_copy(iota_f[:, :], iota_i[:, :])
            dve.wait_ge(set_pe, 1)
            dve.tensor_copy(b1c[:, :], PW[:, 0:NE * FH]).then_inc(set_dve, 1)
            norm_stats(0)
            norm(0)
            run(slots, dve)
            stats(T - 1, NP - 1)
            factors(T - 1, NP - 1)
            gained(T - 1, NP - 2)
            gained(T - 1, NP - 1)
            finish(T - 1)


def store(nc, es, X, out):
    done = es.enter_context(nc.semaphore("stored_dbg"))
    block = es.enter_context(nc.Block())

    @block.sync
    def _(sp):
        for q in range(HQ):
            for b in range(TB):
                sp.dma_start(out.rearrange("(t b) (g q e) c -> q b g t (e c)", t=T, g=NQ, q=HQ)[q, b],
                             X[32 * q + NQ * b:32 * q + NQ * b + NQ, :, :]).then_inc(done, 16)
        sp.wait_ge(done, 16 * HQ * TB)


_INS = ["x", "ctx_1024", "fside_SxS2_0"] + ["L0_attn_" + n for n in ("Wq", "bq", "Wk", "bk", "Wv", "bv", "Wo", "bo")] + [
    "L0_ffn_" + n for n in ("gate_w", "w1", "b1", "w2", "b2", "ln_g", "ln_b")]


def kernel(**inputs):
    import numpy as _np
    import concourse.bacc as _bacc
    from concourse import mybir as _mybir
    from concourse.bass_utils import run_bass_kernel_spmd as _run

    nc = _bacc.Bacc("TRN2", target_bir_lowering=False, num_devices=1)
    arrays, args = {}, []
    for name in _INS:
        a = _np.ascontiguousarray(inputs[name])
        arrays[f"in_{name}_dram"] = a
        args.append(nc.dram_tensor(f"in_{name}_dram", a.shape, _mybir.dt.from_np(a.dtype), kind="ExternalInput").ap())
    args.append(nc.dram_tensor("out_0_dram", (B, L, D), F32, kind="ExternalOutput").ap())
    perceiver_layer(nc, *args)
    r = _run(nc, [arrays], core_ids=[0])
    return r.results[0]["out_0_dram"]
```

```python
from contextlib import ExitStack

import concourse.bass as bass
from concourse import mybir

F32 = mybir.dt.float32
F32R = mybir.dt.float32r
I32 = mybir.dt.int32
U32 = mybir.dt.uint32
ALU = mybir.AluOpType
ACT = mybir.ActivationFunctionType
AX = mybir.AxisListType

B, L, D = 128, 32, 128
S = 257
H, DK = 16, 8
NE, F = 8, 256
EPS_LN, EPS_EXPERT = 1e-5, 1e-6
SCALE = float(DK) ** -0.5

P = 128
NQ, HQ = 4, 4
TB = 8
HB = TB // 2
T = B // TB
KT = 2
STEPS = 2 * TB
HSTEPS = STEPS // 2
DECAY = -0.25
MASKED = -1.0e30


def perceiver_layer(nc, x, ctx, fmask, Wq, bq, Wk, bk, Wv, bv, Wo, bo, gate_w, w1, b1, w2, b2, ln_g, ln_b, out, stages=3):
    with ExitStack() as es:
        def sb(name, shape, dt=F32):
            return es.enter_context(nc.sbuf_tensor(name, shape, dt))

        def sem(name):
            return es.enter_context(nc.semaphore(name))

        ident = sb("ident", [P, P])
        head_of = sb("head_of", [P, H])
        own_of = sb("own_of", [P, 2, HQ])
        hh_of = sb("hh_of", [P, HQ])
        hh_scaled = sb("hh_scaled", [P, HQ, L])
        mask_T = sb("mask_T", [P, 2, KT, HQ * L])
        mask_last = sb("mask_last", [HB * NQ, HQ * L])
        last_sel = sb("last_sel", [HB * NQ, HB, D])
        X = sb("X", [P, T, 2 * D])

        setup_in = sem("setup_in")
        xperm_in = sem("xperm_in")
        pool_set = sem("pool_set")
        dve_set = sem("dve_set")
        pe_set = sem("pe_set")

        with ExitStack() as s1:
            def sb1(name, shape, dt=F32):
                return s1.enter_context(nc.sbuf_tensor(name, shape, dt))

            def ps1(name, shape):
                return s1.enter_context(nc.psum_tensor(name, shape, F32))

            def sem1(name):
                return s1.enter_context(nc.semaphore(name))

            V = sb1("V", [P, TB, KT, D])
            last_rep = sb1("last_rep", [HB * NQ, 2, D])
            V_split = sb1("V_split", [P, 4, KT, H, 2, DK], F32R)
            last_split = sb1("last_split", [HB * NQ, 2, H, 2, DK], F32R)
            last_bd = sb1("last_bd", [HB * NQ, 2, HB, D])
            xh = sb1("xh", [P, 2, D])
            xn = sb1("xn", [P, H, 2, DK])
            xstat = sb1("xstat", [P, 6])
            xmv = sb1("xmv", [P, 2])
            xrs = sb1("xrs", [P, 1])
            xvar = sb1("xvar", [P, 1])
            neg_half = sb1("neg_half", [P, 1])
            ones = sb1("ones", [P, KT * D])
            QX = 2 * 2 * HB
            Qt = sb1("Qt", [P, L, QX], F32R)
            Qbd = sb1("Qbd", [P, 2, 2, HQ * L, QX], F32R)
            Kt = sb1("Kt", [P, 4, 2, S + 1], F32R)
            K_last = sb1("K_last", [P, 2, 2, HB], F32R)
            neg_max = sb1("neg_max", [P, 2, 2])
            E = sb1("E", [P, 2, HB * NQ, S])
            den = sb1("den", [P, 2, HB * NQ])
            rden = sb1("rden", [P, HB * NQ])
            Et = sb1("Et", [P, 4, 2, KT, HQ * L])
            last_Et = sb1("last_Et", [HB * NQ, HQ * L])
            O_c = sb1("O_c", [P, HB, HQ * L])
            O_n = sb1("O_n", [P, DK, TB * NQ])
            O_t = sb1("O_t", [P, DK, L])

            SC = [ps1(f"SC{i}", [P, 2, 512]) for i in range(2)]
            ETP = [ps1(f"ETP{i}", [P, 512]) for i in range(2)]
            AV = ps1("AV", [P, HB, HQ * L])
            MISC = ps1("MISC", [P, 512])
            QT_LAST = MISC[:, 2 * P:2 * P + 2 * HB * NQ]
            TURN = MISC[:, 0:P]

            ctx_in = [sem1(f"ctx_in{k}") for k in range(TB // 2)]
            last_in = [sem1(f"last_in{h}") for h in range(2)]
            x_in = [sem1(f"x_in{h}") for h in range(2)]
            consts = sem1("consts")
            vs_sb, last_sb = sem1("vs_sb"), sem1("last_sb")
            kt_ps, kt_sb, kl_sb = sem1("kt_ps"), sem1("kt_sb"), sem1("kl_sb")
            sc_ps, mx = sem1("sc_ps"), sem1("mx")
            ex = sem1("ex")
            et_ps, et_sb = sem1("et_ps"), sem1("et_sb")
            av_b = sem1("av_b")
            lastt_ps, lastt_sb, last_bd_set = sem1("lastt_ps"), sem1("lastt_sb"), sem1("last_bd_set")
            av_full, o_c, o_ps, o_n = sem1("av_full"), sem1("o_c"), sem1("o_ps"), sem1("o_n")
            rden_set = sem1("rden_set")
            o_t, x1 = sem1("o_t"), sem1("x1")
            st, mv, vr, rs, xn_sb = sem1("st"), sem1("mv"), sem1("vr"), sem1("rs"), sem1("xn_sb")
            qt_ps, q_hi, q_lo = sem1("qt_ps"), sem1("q_hi"), sem1("q_lo")
            q_in = [sem1(f"q_in{h}") for h in range(2)]
            q_zero = sem1("q_zero")
            Q_DMAS = 16 * 2 * HQ

            def load_ctx(sp, t, k):
                sp.dma_start(V[:, 2 * k:2 * k + 2, :, :].rearrange("p b k c -> p b (k c)"),
                             ctx[bass.ds(TB * t + 2 * k, 2), 0:KT * P, :].rearrange("b (p k) c -> p b (k c)", p=P)
                             ).then_inc(ctx_in[k], 16)

            def load_last(sp, t, h):
                b0 = TB * t + HB * h
                for j in range(HB):
                    sp.dma_start(last_rep[NQ * j:NQ * j + NQ, h, :],
                                 ctx[bass.ds(b0 + j, 1), S - 1, :].to_broadcast([NQ, D])).then_inc(last_in[h], 16)

            def load_x(sp, t, h):
                sp.dma_start(xh[:, h, :], x[bass.ds(TB * t + HB * h, HB), :, :].rearrange("b l c -> (b l) c")).then_inc(x_in[h], 16)

            with ExitStack() as s0:
                fm = s0.enter_context(nc.sbuf_tensor("fm", [L, S], F32))
                block = s0.enter_context(nc.Block())

                @block.sync
                def _(sp):
                    sp.dma_start(fm[:, :], fmask).then_inc(setup_in, 16)
                    load_x(sp, 0, 0)
                    load_last(sp, 0, 0)
                    load_ctx(sp, 0, 0)
                    load_x(sp, 0, 1)
                    load_ctx(sp, 0, 1)
                    load_last(sp, 0, 1)
                    load_ctx(sp, 0, 2)
                    load_ctx(sp, 0, 3)

                @block.gpsimd
                def _(pool):
                    pool.memset(ident[:, :], 0.0).then_inc(pool_set, 1)
                    pool.memset(head_of[:, :], 1.0).then_inc(pool_set, 1)
                    pool.memset(last_sel[:, :, :], 0.0).then_inc(pool_set, 1)
                    pool.wait_ge(pool_set, 3)
                    pool.affine_select(out=ident[:, :], in_=ident[:, :], compare_op=ALU.not_equal, fill=1.0, base=0,
                                       pattern=[[-1, P]], channel_multiplier=1).then_inc(pool_set, 1)
                    pool.affine_select(out=head_of[:, :], in_=head_of[:, :], compare_op=ALU.is_ge, fill=0.0, base=0,
                                       pattern=[[-DK, H]], channel_multiplier=1).then_inc(pool_set, 1)
                    pool.wait_ge(pool_set, 5)
                    pool.affine_select(out=head_of[:, :], in_=head_of[:, :], compare_op=ALU.is_ge, fill=0.0, base=DK - 1,
                                       pattern=[[DK, H]], channel_multiplier=-1).then_inc(pool_set, 1)
                    pool.affine_select(out=last_sel[:, :, :].rearrange("p j (g c) -> p j g c", g=NQ),
                                       in_=last_sel[:, :, :].rearrange("p j (g c) -> p j g c", g=NQ),
                                       compare_op=ALU.not_equal, fill=1.0, base=0,
                                       pattern=[[-NQ, HB], [-1, NQ], [0, D // NQ]], channel_multiplier=1).then_inc(pool_set, 1)

                @block.tensor
                def _(pe):
                    pe.wait_ge(setup_in, 16)
                    pe.wait_ge(pool_set, 7)
                    for k in range(KT):
                        pe.transpose(MISC[:, k * L:(k + 1) * L], fm[:, k:KT * P:KT], ident[0:L, 0:L])
                    pe.matmul(MISC[0:HB * NQ, 64:64 + L], fm[:, S - 1:S].to_broadcast([L, HB * NQ]),
                              ident[0:L, 0:L], start=True, stop=True).then_inc(pe_set, 1)

                @block.vector
                def _(dve):
                    for h in range(2):
                        dve.memset(Qbd[:, h, :, :, :].bitcast(F32), 0.0).then_inc(q_zero, 1)
                    dve.memset(Kt[:, :, :, S:S + 1].bitcast(F32), 0.0)
                    dve.wait_ge(pool_set, 7)
                    dve.tensor_reduce(own_of[:, :, :], head_of[:, :].rearrange("p (a u q) -> p u q a", u=2, q=HQ), AX.X,
                                      ALU.add).then_inc(dve_set, 1)
                    dve.wait_ge(dve_set, 1)
                    dve.tensor_tensor(hh_of[:, :], own_of[:, 0, :], own_of[:, 1, :], ALU.add).then_inc(dve_set, 1)
                    dve.wait_ge(dve_set, 2)
                    dve.tensor_scalar(hh_scaled[:, :, :], hh_of[:, :].unsqueeze(2).to_broadcast([P, HQ, L]), SCALE, None,
                                      ALU.mult).then_inc(dve_set, 1)
                    dve.wait_ge(pe_set, 1)
                    for u in range(2):
                        for k in range(KT):
                            dve.tensor_copy(mask_T[:, u, k, :].rearrange("p (q l) -> p q l", q=HQ),
                                            MISC[:, k * L:(k + 1) * L].unsqueeze(1).to_broadcast([P, HQ, L])).then_inc(dve_set, 1)
                    dve.tensor_copy(mask_last[:, :].rearrange("p (q l) -> p q l", q=HQ),
                                    MISC[0:HB * NQ, 64:64 + L].unsqueeze(1).to_broadcast([HB * NQ, HQ, L])).then_inc(dve_set, 1)

            def run_tiles(steps, eng):
                steps(0, True, False)
                with eng.Fori(1, T - 1) as t:
                    steps(t, False, False)
                steps(T - 1, False, True)

            block = s1.enter_context(nc.Block())

            @block.sync
            def _(sp):
                def place_queries(t, h):
                    sp.wait_ge(q_lo, 2 * t + h + 1)
                    if isinstance(t, int) and t == 0:
                        sp.wait_ge(q_zero, h + 1)
                    for u in range(2):
                        for q in range(HQ):
                            r = slice(64 * u + 16 * q, 64 * u + 16 * q + 16)
                            sp.dma_start(Qbd[r, h, u, L * q:L * q + L, :].bitcast(F32), Qt[r, :, :].bitcast(F32)).then_inc(q_in[h], 16)

                def load_residual(q):
                    for b in range(TB):
                        sp.dma_start(X[32 * q + NQ * b:32 * q + NQ * b + NQ, :, :],
                                     x.rearrange("(t b) (g q e) c -> q b g t (e c)", t=T, g=NQ, q=HQ)[q, b]).then_inc(xperm_in, 16)

                def steps(t, fresh):
                    place_queries(t, 1)
                    sp.wait_ge(xn_sb, 2 * t + 1)
                    sp.nop(nofuse=True)
                    load_x(sp, t + 1, 0)
                    sp.wait_ge(last_bd_set, 2 * t + 1)
                    sp.nop(nofuse=True)
                    load_last(sp, t + 1, 0)
                    sp.wait_ge(xn_sb, 2 * t + 2)
                    sp.nop(nofuse=True)
                    load_x(sp, t + 1, 1)
                    if fresh:
                        for q in range(HQ // 2):
                            load_residual(q)
                    sp.wait_ge(av_b, TB * t + 2)
                    sp.nop(nofuse=True)
                    load_ctx(sp, t + 1, 0)
                    sp.wait_ge(av_b, TB * t + 4)
                    sp.nop(nofuse=True)
                    load_ctx(sp, t + 1, 1)
                    place_queries(t + 1, 0)
                    sp.wait_ge(last_bd_set, 2 * t + 2)
                    sp.nop(nofuse=True)
                    load_last(sp, t + 1, 1)
                    if fresh:
                        for q in range(HQ // 2, HQ):
                            load_residual(q)
                    sp.wait_ge(av_b, TB * t + 6)
                    sp.nop(nofuse=True)
                    load_ctx(sp, t + 1, 2)
                    sp.wait_ge(av_b, TB * t + 8)
                    sp.nop(nofuse=True)
                    load_ctx(sp, t + 1, 3)

                place_queries(0, 0)
                steps(0, True)
                with sp.Fori(1, T - 1) as t:
                    steps(t, False)
                place_queries(T - 1, 1)

            @block.gpsimd
            def _(pool):
                pool.wait_ge(dve_set, 8)
                pool.memset(neg_half[:, :], -0.5).then_inc(consts, 1)
                pool.memset(ones[:, :], 1.0).then_inc(consts, 1)
                pool.wait_ge(consts, 2)

                def split(t, j, first=False):
                    b = TB * t + j
                    pool.wait_ge(ctx_in[j // 2], 16 * (t + 1))
                    if not first:
                        pool.wait_ge(kt_ps, b - 3)
                    r = j % 4
                    v = V[:, j, :, :].rearrange("p k (g c) -> p k g c", g=H)
                    pool.tensor_tensor(V_split[:, r, :, :, 0, :], v, ones[:, :].rearrange("p (k g c) -> p k g c", k=KT, g=H),
                                       ALU.mult).then_inc(vs_sb, 1)
                    pool.wait_ge(vs_sb, 2 * b + 1)
                    pool.tensor_tensor(V_split[:, r, :, :, 1, :], v, V_split[:, r, :, :, 0, :], ALU.subtract).then_inc(vs_sb, 1)

                def split_last(t, h):
                    m = 2 * t + h
                    pool.wait_ge(last_in[h], 16 * HB * (t + 1))
                    if not (isinstance(t, int) and t == 0):
                        pool.wait_ge(qt_ps, m - 1)
                    v = last_rep[:, h, :].rearrange("p (g c) -> p g c", g=H)
                    pool.tensor_tensor(last_split[:, h, :, 0, :], v, ones[0:HB * NQ, 0:D].rearrange("p (g c) -> p g c", g=H),
                                       ALU.mult).then_inc(last_sb, 1)
                    pool.wait_ge(last_sb, 2 * m + 1)
                    pool.tensor_tensor(last_split[:, h, :, 1, :], v, last_split[:, h, :, 0, :], ALU.subtract).then_inc(last_sb, 1)

                def power(t, h):
                    pool.wait_ge(vr, 2 * t + h + 1)
                    pool.tensor_tensor(xrs[:, :], xvar[:, :], neg_half[:, :], ALU.pow).then_inc(rs, 1)

                def place_last(t, h):
                    m = 2 * t + h
                    pool.wait_ge(last_in[h], 16 * HB * (t + 1))
                    if not (isinstance(t, int) and t == 0):
                        pool.wait_ge(av_full, m - 1)
                    pool.tensor_tensor(last_bd[:, h, :, :], last_rep[:, h, :].unsqueeze(1).to_broadcast([HB * NQ, HB, D]),
                                       last_sel[:, :, :], ALU.mult).then_inc(last_bd_set, 1)

                def add_tile(t):
                    pool.wait_ge(o_t, t + 1)
                    pool.wait_ge(xperm_in, 16 * HQ * TB)
                    xt = X[:, t, :] if isinstance(t, int) else X[:, bass.ds(t, 1), :].rearrange("p a c -> p (a c)")
                    pool.tensor_tensor(xt.rearrange("p (l d) -> p l d", d=DK), O_t[:, :, :].rearrange("p d l -> p l d"),
                                       xt.rearrange("p (l d) -> p l d", d=DK), ALU.add).then_inc(x1, 1)

                def steps(t, fresh, final):
                    for h in range(2):
                        t1, h1 = (t, 1) if h == 0 else (t + 1, 0)
                        more = not (final and h == 1)
                        if more:
                            power(t1, h1)
                            split_last(t1, h1)
                            split(t1, HB * h1)
                        place_last(t, h)
                        if more:
                            for j in range(1, HB):
                                split(t1, HB * h1 + j)
                        if h == 0 and not fresh:
                            add_tile(t - 1)

                split(0, 0, first=True)
                power(0, 0)
                split_last(0, 0)
                for j in range(1, HB):
                    split(0, j, first=True)
                run_tiles(steps, pool)
                add_tile(T - 1)

            @block.tensor
            def _(pe):
                def turn_keys(t, j, first=False):
                    b, m = TB * t + j, 2 * t + j // HB
                    pe.wait_ge(vs_sb, 2 * b + 2)
                    if first:
                        pe.wait_ge(q_lo, 1)
                        pe.wait_ge(q_hi, 1)
                    else:
                        pe.wait_ge(kt_sb, b)
                    if j % HB == 0 and not first and not (isinstance(t, int) and t == 0):
                        pe.wait_ge(o_n, m - 1)
                    if j % HB == 2 and not (isinstance(t, int) and t == 0 and j == 2):
                        pe.wait_ge(lastt_sb, m)
                    if j % HB == 3 and not (isinstance(t, int) and t == T - 1 and j == TB - 1):
                        pe.wait_ge(q_hi, m + 2)
                        pe.wait_ge(q_lo, m + 2)
                    for p in range(2):
                        for k in range(KT):
                            c = (KT * p + k) * P
                            i = pe.transpose(MISC[:, c:c + P],
                                             V_split[:, j % 4, k, 8 * p:8 * p + 8, :, :].rearrange("p g x c -> p (g x c)").bitcast(F32),
                                             ident[:, :])
                    i.then_inc(kt_ps, 1)

                def turn_queries(t, h, first=False):
                    m = 2 * t + h
                    pe.wait_ge(xn_sb, m + 1)
                    pe.wait_ge(last_sb, 2 * m + 2)
                    if not first:
                        pe.wait_ge(kt_sb, HB * m - 1)
                    for p in range(2):
                        pe.transpose(MISC[:, p * P:(p + 1) * P], xn[:, 8 * p:8 * p + 8, :, :].rearrange("p g x c -> p (g x c)"),
                                     ident[:, :])
                        n = HB * NQ
                        i = pe.transpose(QT_LAST[:, p * n:(p + 1) * n],
                                         last_split[:, h, 8 * p:8 * p + 8, :, :].rearrange("p g x c -> p (g x c)").bitcast(F32),
                                         ident[0:n, 0:n])
                    i.then_inc(qt_ps, 1)

                def scores(t, s, first=False):
                    j, n = s // 2, STEPS * t + s
                    if s % 2 == 0:
                        pe.wait_ge(kt_sb, TB * t + j + 1)
                        pe.wait_ge(kl_sb, TB * t + j + 1)
                    if s % HSTEPS == 0:
                        pe.wait_ge(q_in[s // HSTEPS], Q_DMAS * (t + 1))
                    if not first:
                        pe.wait_ge(ex, n - 1)
                    for u in range(2):
                        for x in range(2):
                            i = pe.matmul(SC[s % 2][:, u, 0:S + 1], Qbd[:, j // HB, u, :, (2 * x + s % 2) * HB + j % HB],
                                          Kt[:, j % 4, s % 2, :], start=(x == 0), stop=(x == 1))
                    i.then_inc(sc_ps, 1)

                def turn_probs(t, s, first=False):
                    n = STEPS * t + s
                    h, u0 = s // HSTEPS, 2 * (s % HSTEPS)
                    pe.wait_ge(ex, n + 1)
                    if not first:
                        pe.wait_ge(et_sb, n - 1)
                    for u in range(2):
                        for k in range(KT):
                            c = (2 * u + k) * P
                            i = pe.transpose(ETP[s % 2][:, c:c + P], E[:, h, u0 + u, k * P:(k + 1) * P], ident[:, :])
                    i.then_inc(et_ps, 1)

                def weigh_values(t, j, first=False):
                    h = j // HB
                    pe.wait_ge(et_sb, STEPS * t + 2 * j + 2)
                    if j % HB == 0 and not first:
                        pe.wait_ge(o_c, 2 * t + h)
                    for k in range(KT):
                        for g in range(NQ):
                            i = pe.matmul(AV[32 * g:32 * g + 32, j % HB, :], V[:, j, k, 32 * g:32 * g + 32],
                                          Et[:, 2 * (j % 2) + g // 2, g % 2, k, :],
                                          start=(j % HB == 0 and k == 0), stop=False, skip_group_check=True)
                    i.then_inc(av_b, 1)

                def turn_last(t, h, final=False):
                    m = 2 * t + h
                    if not final:
                        pe.wait_ge(kt_sb, HB * m + HB + 2)
                    pe.transpose(TURN[0:HB * NQ, :], E[:, h, :, S - 1], ident[:, :]).then_inc(lastt_ps, 1)

                def weigh_last(t, h):
                    m = 2 * t + h
                    pe.wait_ge(lastt_sb, m + 1)
                    pe.wait_ge(last_bd_set, m + 1)
                    for j in range(HB):
                        i = pe.matmul(AV[:, j, :], last_bd[:, h, j, :], last_Et[:, :], start=False, stop=(j == HB - 1),
                                      skip_group_check=True)
                    i.then_inc(av_full, 1)

                def turn_out(t, h, final=False):
                    m = 2 * t + h
                    pe.wait_ge(o_c, m + 1)
                    if not final:
                        pe.wait_ge(kt_sb, HB * m + HB + 4)
                    for j in range(HB):
                        i = pe.transpose(MISC[:, P * j:P * j + P], O_c[:, j, :], ident[:, :])
                    i.then_inc(o_ps, 1)

                def back(t, s, lag):
                    return (t, s - lag) if s >= lag else (t - 1, s + STEPS - lag)

                def lagging(t, s):
                    fresh = isinstance(t, int) and t == 0
                    if not (fresh and s < 2):
                        tt, ss = back(t, s, 2)
                        turn_probs(tt, ss, first=fresh and s < 4)
                    if s % 2 == 1 and not (fresh and s < 5):
                        tt, ss = back(t, s, 5)
                        weigh_values(tt, ss // 2, first=fresh and s == 5)
                    if not (fresh and s < HSTEPS):
                        tt, ss = back(t, s, HSTEPS)
                        if s % HSTEPS == 1:
                            turn_last(tt, ss // HSTEPS)
                        if s % HSTEPS == 3:
                            weigh_last(tt, ss // HSTEPS)
                        if s % HSTEPS == 5:
                            turn_out(tt, ss // HSTEPS)

                def steps(t, fresh, final):
                    for s in range(STEPS):
                        scores(t, s, first=fresh and s < 2)
                        if s % 2 == 0 and s % HSTEPS not in (2, 6):
                            if s < STEPS - 2:
                                turn_keys(t, s // 2 + 1)
                            elif not final:
                                turn_keys(t + 1, 0)
                        if s == 3:
                            turn_queries(t, 1)
                        if s == 11 and not final:
                            turn_queries(t + 1, 0)
                        lagging(t, s)
                        if s % 2 == 0 and s % HSTEPS in (2, 6):
                            if s < STEPS - 2:
                                turn_keys(t, s // 2 + 1)
                            elif not final:
                                turn_keys(t + 1, 0)

                pe.wait_ge(pool_set, 7)
                turn_queries(0, 0, first=True)
                turn_keys(0, 0, first=True)
                run_tiles(steps, pe)
                turn_probs(T - 1, STEPS - 2)
                turn_probs(T - 1, STEPS - 1)
                turn_last(T - 1, 1, final=True)
                weigh_values(T - 1, TB - 2)
                weigh_values(T - 1, TB - 1)
                weigh_last(T - 1, 1)
                turn_out(T - 1, 1, final=True)

            @block.scalar
            def _(act):
                def keep_keys(t, j, first=False):
                    b = TB * t + j
                    act.wait_ge(kt_ps, b + 1)
                    if not first:
                        act.wait_ge(sc_ps, 2 * (b - 3))
                    act.activation(Kt[:, j % 4, :, 0:KT * P], MISC[:, :].rearrange("p (a s) -> p a s", a=2), ACT.Copy).then_inc(kt_sb, 1)

                def keep_queries(t, h, first=False):
                    m = 2 * t + h
                    act.wait_ge(qt_ps, m + 1)
                    if not first:
                        act.wait_ge(q_in[1 - h], Q_DMAS * (t + h))
                    act.activation(Qt[:, :, 0:QX // 2].rearrange("p l (a j) -> p a j l", a=2),
                                   MISC[:, 0:2 * P].rearrange("p (a j l) -> p a j l", a=2, j=HB), ACT.Copy,
                                   scale=SCALE).then_inc(q_hi, 1)

                def exponentials(t, s, first=False):
                    n = STEPS * t + s
                    h, u0 = s // HSTEPS, 2 * (s % HSTEPS)
                    act.wait_ge(mx, n + 1)
                    if s % HSTEPS == 0 and not first:
                        act.wait_ge(lastt_ps, 2 * t + h - 1)
                        act.wait_ge(rden_set, 2 * t + h - 1)
                    for u in range(2):
                        i = act.activation(E[:, h, u0 + u, :], SC[s % 2][:, u, 0:S], ACT.Exp,
                                           bias=neg_max[:, s % 2, u:u + 1], accum_out=den[:, h, u0 + u:u0 + u + 1])
                    i.then_inc(ex, 1)

                def keep_sums(t, h):
                    act.wait_ge(av_full, 2 * t + h + 1)
                    act.activation(O_c[:, :, :], AV[:, :, :], ACT.Copy).then_inc(o_c, 1)

                def steps(t, fresh, final):
                    for s in range(STEPS):
                        if s % 2 == 0:
                            if s < STEPS - 2:
                                keep_keys(t, s // 2 + 1, first=fresh and s < 6)
                            elif not final:
                                keep_keys(t + 1, 0)
                        exponentials(t, s, first=fresh)
                        if s % HSTEPS == 3 and not (final and s >= HSTEPS):
                            keep_queries(t if s < HSTEPS else t + 1, 1 if s < HSTEPS else 0)
                        if s % HSTEPS == 3 and not (fresh and s < HSTEPS):
                            keep_sums(t if s >= HSTEPS else t - 1, 0 if s >= HSTEPS else 1)

                keep_queries(0, 0, first=True)
                keep_keys(0, 0, first=True)
                run_tiles(steps, act)
                keep_sums(T - 1, 1)

            @block.vector
            def _(dve):
                def norm_stats(t, h):
                    dve.wait_ge(x_in[h], 16 * (t + 1))
                    dve.bn_stats(xstat[:, :], xh[:, h, :]).then_inc(st, 1)

                def norm_mean(t, h, first=False):
                    m = 2 * t + h
                    dve.wait_ge(st, m + 1)
                    dve.nop(nofuse=True)
                    dve.bn_aggr(xmv[:, :], xstat[:, :]).then_inc(mv, 1)

                def norm_var(t, h, first=False):
                    m = 2 * t + h
                    dve.wait_ge(mv, m + 1)
                    if not first:
                        dve.wait_ge(rs, m)
                    dve.tensor_scalar(xvar[:, :], xmv[:, 1:2], EPS_LN, None, ALU.add).then_inc(vr, 1)

                def normalise(t, h, first=False):
                    m = 2 * t + h
                    dve.wait_ge(rs, m + 1)
                    if not first:
                        dve.wait_ge(qt_ps, m)
                    dve.tensor_scalar(xn[:, :, :, :], xh[:, h, :].rearrange("p (g c) -> p g c", g=H).unsqueeze(2).to_broadcast([P, H, 2, DK]),
                                      xmv[:, 0:1], xrs[:, 0:1], ALU.subtract, ALU.mult).then_inc(xn_sb, 1)

                def keep_queries(t, h):
                    m = 2 * t + h
                    dve.wait_ge(q_hi, m + 1)
                    dve.scalar_tensor_tensor(Qt[:, :, QX // 2:QX].rearrange("p l (a j) -> p a j l", a=2),
                                             MISC[:, 0:2 * P].rearrange("p (a j l) -> p a j l", a=2, j=HB), SCALE,
                                             Qt[:, :, 0:QX // 2].rearrange("p l (a j) -> p a j l", a=2), ALU.mult, ALU.subtract)
                    dve.tensor_copy(K_last[:, h, :, :], QT_LAST.rearrange("p (a j g) -> p a j g", a=2, g=NQ)[:, :, :, 0]).then_inc(q_lo, 1)

                def place_last(t, j, first=False):
                    b = TB * t + j
                    dve.wait_ge(q_lo, 2 * t + j // HB + 1)
                    if not first:
                        dve.wait_ge(sc_ps, 2 * (b - 3))
                    dve.tensor_copy(Kt[:, j % 4, :, S - 1:S], K_last[:, j // HB, :, j % HB:j % HB + 1]).then_inc(kl_sb, 1)

                def maxima(t, s, first=False):
                    n = STEPS * t + s
                    dve.wait_ge(sc_ps, n + 1)
                    if not first:
                        dve.wait_ge(ex, n - 1)
                    dve.tensor_reduce(neg_max[:, s % 2, :], SC[s % 2][:, :, 0:S], AX.X, ALU.max, negate=True).then_inc(mx, 1)

                def keep_probs(t, s, first=False):
                    n = STEPS * t + s
                    dve.wait_ge(et_ps, n + 1)
                    if not first:
                        dve.wait_ge(av_b, (STEPS // 2) * t + s // 2 - 1)
                    dve.tensor_tensor(Et[:, s % 4, :, :, :].rearrange("p u k c -> p (u k c)"), ETP[s % 2][:, :],
                                      mask_T[:, :, :, :].rearrange("p u k c -> p (u k c)"), ALU.mult).then_inc(et_sb, 1)

                def keep_last(t, h):
                    m = 2 * t + h
                    dve.wait_ge(lastt_ps, m + 1)
                    if not (isinstance(t, int) and t == 0 and h == 0):
                        dve.wait_ge(av_full, m)
                    dve.tensor_tensor(last_Et[:, :], TURN[0:HB * NQ, :], mask_last[:, :], ALU.mult).then_inc(lastt_sb, 1)

                def invert(t, h):
                    m = 2 * t + h
                    dve.reciprocal(rden[:, :], den[:, h, :]).then_inc(rden_set, 1)

                def own_outputs(t, h):
                    m = 2 * t + h
                    dve.wait_ge(o_ps, m + 1)
                    dve.wait_ge(rden_set, m + 1)
                    if not (isinstance(t, int) and t == 0):
                        if h == 0:
                            dve.wait_ge(o_t, t)
                    for q in range(HQ):
                        r = slice(32 * q, 32 * q + 32)
                        i = dve.tensor_tensor(
                            O_n[r, :, HB * NQ * h:HB * NQ * (h + 1)].rearrange("p d u -> p u d"),
                            MISC[r, :].rearrange("p (u c) -> p u c", c=D // NQ)[:, :, DK * q:DK * q + DK],
                            rden[r, :].unsqueeze(2).to_broadcast([32, HB * NQ, DK]), ALU.mult)
                    i.then_inc(o_n, 1)

                def turn_tile(t):
                    dve.wait_ge(o_n, 2 * t + 2)
                    if not (isinstance(t, int) and t == 0):
                        dve.wait_ge(x1, t)
                    dve.transpose(O_t[:, :, :].rearrange("p d l -> p (d l)"), O_n[:, :, :].rearrange("p d u -> p (d u)")).then_inc(o_t, 1)

                def back(t, s, lag):
                    return (t, s - lag) if s >= lag else (t - 1, s + STEPS - lag)

                def steps(t, fresh, final):
                    for s in range(STEPS):
                        q = (t, 1) if s < HSTEPS else (t + 1, 0)
                        more = not (final and s >= HSTEPS)
                        if more and s % HSTEPS == 0:
                            norm_stats(*q)
                        maxima(t, s, first=fresh and s < 2)
                        if more and s % HSTEPS == 0:
                            norm_mean(*q)
                        if not (fresh and s < 2):
                            tt, ss = back(t, s, 2)
                            keep_probs(tt, ss, first=fresh and s < 6)
                        if more and s % HSTEPS == 0:
                            norm_var(*q)
                        if not (fresh and s < HSTEPS):
                            tt, ss = back(t, s, HSTEPS)
                            hh = ss // HSTEPS
                            if s % HSTEPS == 1:
                                keep_last(tt, hh)
                            if s % HSTEPS == 3:
                                invert(tt, hh)
                            if s % HSTEPS == 5:
                                own_outputs(tt, hh)
                            if s == 6:
                                turn_tile(tt)
                        if more:
                            if s % HSTEPS == 1:
                                normalise(*q)
                            if s % HSTEPS == 3:
                                keep_queries(*q)
                        if s % 2 == 0:
                            if s < STEPS - 2:
                                place_last(t, s // 2 + 1, first=fresh and s < 6)
                            elif not final:
                                place_last(t + 1, 0)

                dve.wait_ge(dve_set, 8)
                norm_stats(0, 0)
                norm_mean(0, 0)
                norm_var(0, 0, first=True)
                normalise(0, 0, first=True)
                keep_queries(0, 0)
                place_last(0, 0, first=True)
                run_tiles(steps, dve)
                for s in range(2):
                    keep_probs(T - 1, STEPS - 2 + s)
                keep_last(T - 1, 1)
                invert(T - 1, 1)
                own_outputs(T - 1, 1)
                turn_tile(T - 1)

        if stages == 1:
            store(nc, es, X, out)
            return
        attend(nc, es, X, ident, hh_of, hh_scaled, Wq, bq, Wk, bk, Wv, bv, Wo, bo)
        if stages == 2:
            store(nc, es, X, out)
            return
        mix_experts(nc, es, X, ident, gate_w, w1, b1, w2, b2, ln_g, ln_b, out)


def attend(nc, es, X, ident, hh_of, hh_scaled, Wq, bq, Wk, bk, Wv, bv, Wo, bo):
    with ExitStack() as s2:
        def sb(name, shape, dt=F32):
            return s2.enter_context(nc.sbuf_tensor(name, shape, dt))

        def ps(name, shape):
            return s2.enter_context(nc.psum_tensor(name, shape, F32))

        def sem(name):
            return s2.enter_context(nc.semaphore(name))

        W = {n: sb(f"W{n}", [P, D]) for n in "qkvo"}
        brow = sb("brow", [3, D])
        bo_row = sb("bo_row", [1, D])
        ones_row = sb("ones_row", [1, P])
        bcol = sb("bcol", [P, 3])
        out_bias = sb("out_bias", [P, D])
        lag_i = sb("lag_i", [L, L], I32)
        lag = sb("lag", [L, L])
        lag_ln = sb("lag_ln", [L, L])
        lag_p = sb("lag_p", [L, L])
        turn_l = sb("turn_l", [L, HQ, L])
        hh_wide = sb("hh_wide", [P, HQ, TB])
        decay = sb("decay", [P, HB * NQ, L])
        neg_half = sb("neg_half2", [P, 2])
        stat = sb("stat2", [P, 2, 6])
        mv = sb("mv2", [P, 2, 2])
        var = sb("var2", [P, 2])
        rs = sb("rs2", [P, 2])
        xn = sb("xn2", [P, 2, D])
        xT = sb("xT2", [P, TB, L])
        xT4 = sb("xT4", [P, TB, NQ, L])
        Qt = sb("Qt2", [P, TB, L])
        Qbd = sb("Qbd2", [P, TB, HQ, L])
        Kbd = sb("Kbd2", [P, TB, NQ, L])
        Vbd = sb("Vbd2", [P, TB, D])
        E = sb("E2", [P, 2, HB * NQ, L])
        mx = sb("mx2", [P, 2, HB * NQ])
        sm = sb("sm2", [P, 2, HB * NQ])
        En = sb("En2", [P, 2, HB * NQ, L])
        Et = sb("Et2", [P, 2, HB, HQ * L])
        Oc = sb("Oc2", [P, HQ * TB, TB, NQ])
        Xb = sb("Xb2", [P, 2 * D])

        PA = ps("PA", [P, 512])
        PV = [ps(f"PV{h}", [P, HB, D]) for h in range(2)]
        PS = [ps(f"PS{h}", [P, 512]) for h in range(2)]
        PE_ = [ps(f"PE{h}", [P, HB, HQ * L]) for h in range(2)]
        PY = ps("PY", [P, 2 * D])

        w_in, set_pool, set_pe, set_act, set_dve = sem("w_in"), sem("set_pool"), sem("set_pe"), sem("set_act"), sem("set_dve")
        with nc.Block() as block:
            @block.sync
            def _(sp):
                for n, src in zip("qkvo", (Wq, Wk, Wv, Wo)):
                    sp.dma_start(W[n][:, :], src).then_inc(w_in, 16)
                for i, src in enumerate((bq, bk, bv)):
                    sp.dma_start(brow[i:i + 1, :], src.unsqueeze(0)).then_inc(w_in, 16)
                sp.dma_start(bo_row[:, :], bo.unsqueeze(0)).then_inc(w_in, 16)

            @block.gpsimd
            def _(pool):
                pool.iota(lag_i[:, :], pattern=[[-1, L]], base=0, channel_multiplier=1).then_inc(set_pool, 1)
                pool.memset(neg_half[:, :], -0.5).then_inc(set_pool, 1)
                pool.memset(ones_row[:, :], 1.0).then_inc(set_pool, 1)
                pool.memset(Kbd[:, :, :, :], 0.0).then_inc(set_pool, 1)
                pool.memset(Vbd[:, :, :], 0.0).then_inc(set_pool, 1)
                pool.wait_ge(set_act, 2)
                pool.affine_select(out=lag_ln[:, :], in_=lag_ln[:, :], compare_op=ALU.is_ge, fill=MASKED, base=0,
                                   pattern=[[-1, L]], channel_multiplier=1).then_inc(set_pool, 1)

            @block.vector
            def _(dve):
                dve.wait_ge(set_pool, 1)
                dve.tensor_copy(lag[:, :], lag_i[:, :]).then_inc(set_dve, 1)
                dve.wait_ge(set_dve, 1)
                dve.tensor_scalar(lag[:, :], lag[:, :], 1.0, None, ALU.max).then_inc(set_dve, 1)
                for q in range(HQ):
                    dve.tensor_copy(turn_l[:, q, :].rearrange("p (e r g) -> p e r g", e=2, r=HQ),
                                    ident[0:L, 0:L].rearrange("p (g r e) -> p e r g", r=HQ, e=2)).then_inc(set_dve, 1)
                dve.tensor_copy(hh_wide[:, :, :], hh_of[:, :].unsqueeze(2).to_broadcast([P, HQ, TB])).then_inc(set_dve, 1)
                dve.wait_ge(set_pool, 6)
                dve.tensor_copy(lag_p[:, :].rearrange("p (e r g) -> p e r g", e=2, r=HQ),
                                lag_ln[:, :].rearrange("p (g r e) -> p e r g", r=HQ, e=2)).then_inc(set_dve, 1)
                dve.wait_ge(set_pe, 1)
                dve.tensor_copy(decay[:, :, :], PA[:, 0:L].unsqueeze(1).to_broadcast([P, HB * NQ, L])).then_inc(set_dve, 1)
                dve.tensor_copy(bcol[:, :], PA[:, 64:67]).then_inc(set_dve, 1)
                dve.wait_ge(set_pe, 2)
                dve.tensor_copy(out_bias[:, :], PA[:, 128:128 + D]).then_inc(set_dve, 1)

            @block.scalar
            def _(act):
                act.wait_ge(set_dve, 2)
                act.activation(lag_ln[:, :], lag[:, :], ACT.Ln).then_inc(set_act, 1)
                act.wait_ge(set_act, 1)
                act.activation(lag_ln[:, :], lag_ln[:, :], ACT.Copy, scale=DECAY).then_inc(set_act, 1)

            @block.tensor
            def _(pe):
                pe.wait_ge(set_dve, 8)
                pe.wait_ge(w_in, 16 * 8)
                pe.matmul(PA[:, 0:L], turn_l[:, :, :].rearrange("p q l -> p (q l)"), lag_p[:, :], start=True, stop=True)
                pe.transpose(PA[:, 64:67], brow[:, :], ident[0:3, 0:3]).then_inc(set_pe, 1)
                pe.wait_ge(set_dve, 10)
                pe.matmul(PA[:, 128:128 + D], bcol[:, 2:3].to_broadcast([P, P]), W["o"][:, :], start=True, stop=False)
                pe.matmul(PA[:, 128:128 + D], ones_row[:, :], bo_row[:, :], start=False, stop=True).then_inc(set_pe, 1)

        n_stat, n_mv, n_var, n_rs, n_xn = sem("n_stat"), sem("n_mv"), sem("n_var"), sem("n_rs"), sem("n_xn")
        xt_ps, xt_sb, xt4_sb = sem("xt_ps"), sem("xt_sb"), sem("xt4_sb")
        qk_ps, qt_sb, q_bd, k_bd = sem("qk_ps"), sem("qt_sb2"), sem("q_bd2"), sem("k_bd")
        v_ps, v_bd = [sem(f"v_ps{h}") for h in range(2)], [sem(f"v_bd{h}") for h in range(2)]
        s_ps, s_sb, m_sb, d_sb = sem("s_ps"), sem("s_sb"), sem("m_sb"), sem("d_sb")
        e_sb, sum_sb, inv_sb, en_sb = sem("e_sb"), sem("sum_sb"), sem("inv_sb"), sem("en_sb")
        et_ps, et_sb = sem("et_ps2"), sem("et_sb2")
        o_ps, o_sb = sem("o_ps2"), sem("o_sb2")
        y_ps, x2, xb = sem("y_ps"), sem("x2"), sem("xb")

        def tile_of(t):
            return X[:, t, :] if isinstance(t, int) else X[:, bass.ds(t, 1), :].rearrange("p a c -> p (a c)")

        def run(body, eng):
            body(0, True)
            with eng.Fori(1, T - 1) as t:
                body(t, True)
            body(T - 1, False)

        def later(t):
            return not (isinstance(t, int) and t == 0)

        with nc.Block() as block:
            @block.vector
            def _(dve):
                def norm_stats(t):
                    xt = tile_of(t)
                    for e in range(2):
                        i = dve.bn_stats(stat[:, e, :], xt[:, e * D:(e + 1) * D])
                    i.then_inc(n_stat, 1)
                    dve.wait_ge(n_stat, t + 1)
                    dve.nop(nofuse=True)
                    for e in range(2):
                        i = dve.bn_aggr(mv[:, e, :], stat[:, e, :])
                    i.then_inc(n_mv, 1)
                    dve.wait_ge(n_mv, t + 1)
                    dve.tensor_scalar(var[:, :], mv[:, :, 1], EPS_LN, None, ALU.add).then_inc(n_var, 1)

                def norm(t):
                    dve.wait_ge(n_rs, t + 1)
                    if later(t):
                        dve.wait_ge(xt_ps, t)
                    xt = tile_of(t)
                    for e in range(2):
                        i = dve.tensor_scalar(xn[:, e, :], xt[:, e * D:(e + 1) * D], mv[:, e, 0:1], rs[:, e:e + 1],
                                              ALU.subtract, ALU.mult)
                    i.then_inc(n_xn, 1)

                def softmax_front(t, h):
                    m = 2 * t + h
                    dve.wait_ge(s_ps, m + 1)
                    if later(t):
                        dve.wait_ge(en_sb, m - 1)
                    flat = E[:, h, :, :].rearrange("p u s -> p (u s)")
                    dve.tensor_tensor(flat, PS[h][:, :], decay[:, :, :].rearrange("p u s -> p (u s)"), ALU.add).then_inc(s_sb, 1)
                    dve.wait_ge(s_sb, m + 1)
                    dve.tensor_reduce(mx[:, h, :], E[:, h, :, :], AX.X, ALU.max).then_inc(m_sb, 1)
                    dve.wait_ge(m_sb, m + 1)
                    dve.tensor_tensor(E[:, h, :, :], E[:, h, :, :], mx[:, h, :].unsqueeze(2).to_broadcast([P, HB * NQ, L]),
                                      ALU.subtract).then_inc(d_sb, 1)

                def softmax_sums(t, h):
                    m = 2 * t + h
                    dve.wait_ge(e_sb, m + 1)
                    dve.tensor_reduce(sm[:, h, :], E[:, h, :, :], AX.X, ALU.add).then_inc(sum_sb, 1)
                    dve.wait_ge(sum_sb, m + 1)
                    dve.reciprocal(sm[:, h, :], sm[:, h, :]).then_inc(inv_sb, 1)

                def own(t, h):
                    m = 2 * t + h
                    dve.wait_ge(o_ps, m + 1)
                    if later(t):
                        dve.wait_ge(y_ps, t)
                    dve.tensor_tensor(Oc[:, :, HB * h:HB * h + HB, :].rearrange("p a b g -> p b a g"),
                                      PE_[h][:, :, :].rearrange("p j (a g) -> p j a g", g=NQ),
                                      hh_wide[:, :, :].rearrange("p q a -> p (q a)").unsqueeze(1).unsqueeze(3).to_broadcast(
                                          [P, HB, HQ * TB, NQ]), ALU.mult).then_inc(o_sb, 1)

                def add(t):
                    dve.wait_ge(y_ps, t + 1)
                    dve.wait_ge(xb, t + 1)
                    dve.tensor_tensor(tile_of(t), PY[:, :], Xb[:, :], ALU.add).then_inc(x2, 1)

                def body(t, more):
                    softmax_front(t, 0)
                    softmax_front(t, 1)
                    softmax_sums(t, 0)
                    softmax_sums(t, 1)
                    if more:
                        norm_stats(t + 2)
                    own(t, 0)
                    own(t, 1)
                    if more:
                        norm(t + 2)
                    add(t)

                norm_stats(0)
                norm(0)
                norm_stats(1)
                norm(1)
                body(0, True)
                with dve.Fori(1, T - 2) as t:
                    body(t, True)
                body(T - 2, False)
                body(T - 1, False)

            @block.gpsimd
            def _(pool):
                def front(t):
                    pool.wait_ge(qt_sb, t + 1)
                    if later(t):
                        pool.wait_ge(s_ps, 2 * t)
                    pool.tensor_tensor(Qbd[:, :, :, :], Qt[:, :, :].unsqueeze(2).to_broadcast([P, TB, HQ, L]),
                                       hh_scaled[:, :, :].unsqueeze(1).to_broadcast([P, TB, HQ, L]), ALU.mult).then_inc(q_bd, 1)

                def normalise(t, h):
                    m = 2 * t + h
                    pool.wait_ge(inv_sb, m + 1)
                    if later(t):
                        pool.wait_ge(et_ps, m - 1)
                    pool.tensor_tensor(En[:, h, :, :], E[:, h, :, :], sm[:, h, :].unsqueeze(2).to_broadcast([P, HB * NQ, L]),
                                       ALU.mult).then_inc(en_sb, 1)

                def power(t):
                    pool.wait_ge(n_var, t + 1)
                    if later(t):
                        pool.wait_ge(n_xn, t)
                    pool.tensor_tensor(rs[:, :], var[:, :], neg_half[:, :], ALU.pow).then_inc(n_rs, 1)

                def bias(t):
                    pool.wait_ge(n_xn, t + 1)
                    if later(t):
                        pool.wait_ge(x2, t)
                    xt = tile_of(t)
                    pool.tensor_tensor(Xb[:, :].rearrange("p (e c) -> p e c", e=2), xt.rearrange("p (e c) -> p e c", e=2),
                                       out_bias[:, :].unsqueeze(1).to_broadcast([P, 2, D]), ALU.add).then_inc(xb, 1)

                def body(t, more, power_too=True):
                    if more:
                        front(t + 1)
                    normalise(t, 0)
                    normalise(t, 1)
                    if more and power_too:
                        power(t + 2)
                    bias(t)

                power(0)
                power(1)
                front(0)
                body(0, True)
                with pool.Fori(1, T - 2) as t:
                    body(t, True)
                body(T - 2, True, power_too=False)
                body(T - 1, False)

            @block.scalar
            def _(act):
                def turned(t):
                    act.wait_ge(xt_ps, t + 1)
                    if later(t):
                        act.wait_ge(v_ps[1], t)
                    for e in range(2):
                        i = act.activation(xT[:, :, 16 * e:16 * e + 16].rearrange("p b (q g) -> p q b g", q=HQ),
                                           PA[:, e * P:(e + 1) * P].rearrange("p (q b g) -> p q b g", q=HQ, b=TB), ACT.Copy)
                    i.then_inc(xt_sb, 1)

                def repeated(t):
                    act.wait_ge(xt_sb, t + 1)
                    act.activation(xT4[:, :, :, :], xT[:, :, :].unsqueeze(2).to_broadcast([P, TB, NQ, L]), ACT.Copy).then_inc(xt4_sb, 1)

                def projected(t):
                    act.wait_ge(qk_ps, t + 1)
                    if later(t):
                        act.wait_ge(q_bd, t)
                    act.activation(Qt[:, :, :].rearrange("p b l -> p (b l)"), PA[:, 0:256], ACT.Identity,
                                   bias=bcol[:, 0:1]).then_inc(qt_sb, 1)
                    if later(t):
                        act.wait_ge(s_ps, 2 * t)
                    for g in range(NQ):
                        r = slice(32 * g, 32 * g + 32)
                        i = act.activation(Kbd[r, :, g, :], PA[r, 256:512].rearrange("p (b s) -> p b s", b=TB), ACT.Identity,
                                           bias=bcol[r, 1:2])
                    i.then_inc(k_bd, 1)

                def values(t, h):
                    act.wait_ge(v_ps[h], t + 1)
                    if later(t):
                        act.wait_ge(o_ps, 2 * t - 1 + h)
                    for g in range(NQ):
                        r = slice(32 * g, 32 * g + 32)
                        i = act.activation(Vbd[r, HB * h:HB * h + HB, 32 * g:32 * g + 32],
                                           PV[h][r, :, 32 * g:32 * g + 32], ACT.Copy)
                    i.then_inc(v_bd[h], 1)

                def exponentials(t, h):
                    act.wait_ge(d_sb, 2 * t + h + 1)
                    flat = E[:, h, :, :].rearrange("p u s -> p (u s)")
                    act.activation(flat, flat, ACT.Exp).then_inc(e_sb, 1)

                def probs(t, h):
                    m = 2 * t + h
                    act.wait_ge(et_ps, m + 1)
                    if later(t):
                        act.wait_ge(o_ps, m - 1)
                    act.activation(Et[:, h, :, :], PE_[h][:, :, :], ACT.Copy).then_inc(et_sb, 1)

                def body(t, more):
                    if more:
                        turned(t + 1)
                    exponentials(t, 0)
                    if more:
                        projected(t + 1)
                        repeated(t + 1)
                    exponentials(t, 1)
                    probs(t, 0)
                    probs(t, 1)
                    if more:
                        values(t + 1, 0)
                        values(t + 1, 1)

                turned(0)
                projected(0)
                repeated(0)
                values(0, 0)
                values(0, 1)
                run(body, act)

            @block.tensor
            def _(pe):
                def turn(t):
                    pe.wait_ge(n_xn, t + 1)
                    if later(t):
                        pe.wait_ge(k_bd, t)
                    for e in range(2):
                        i = pe.transpose(PA[:, e * P:(e + 1) * P], xn[:, e, :], ident[:, :])
                    i.then_inc(xt_ps, 1)

                def project(t):
                    pe.wait_ge(xt_sb, t + 1)
                    rhs = xT[:, :, :].rearrange("p b l -> p (b l)")
                    pe.matmul(PA[:, 0:256], W["q"][:, :], rhs, start=True, stop=True)
                    pe.matmul(PA[:, 256:512], W["k"][:, :], rhs, start=True, stop=True).then_inc(qk_ps, 1)

                def values(t, h):
                    if later(t):
                        pe.wait_ge(v_bd[h], t)
                    pe.wait_ge(xt4_sb, t + 1)
                    for j in range(HB):
                        i = pe.matmul(PV[h][:, j, :], xT4[:, HB * h + j, :, :].rearrange("p g l -> p (g l)"), W["v"][:, :],
                                      start=True, stop=True)
                    i.then_inc(v_ps[h], 1)

                def scores(t, h):
                    m = 2 * t + h
                    if h == 0:
                        pe.wait_ge(q_bd, t + 1)
                        pe.wait_ge(k_bd, t + 1)
                    if later(t):
                        pe.wait_ge(s_sb, m - 1)
                    for j in range(HB):
                        b = HB * h + j
                        i = pe.matmul(PS[h][:, j * P:(j + 1) * P], Qbd[:, b, :, :].rearrange("p q l -> p (q l)"),
                                      Kbd[:, b, :, :].rearrange("p g s -> p (g s)"), start=True, stop=True)
                    i.then_inc(s_ps, 1)

                def turn_probs(t, h):
                    m = 2 * t + h
                    pe.wait_ge(en_sb, m + 1)
                    if later(t):
                        pe.wait_ge(o_sb, m - 1)
                    for j in range(HB):
                        i = pe.transpose(PE_[h][:, j, :], En[:, h, NQ * j:NQ * j + NQ, :].rearrange("p g s -> p (g s)"),
                                         ident[:, :])
                    i.then_inc(et_ps, 1)

                def weigh(t, h):
                    m = 2 * t + h
                    pe.wait_ge(et_sb, m + 1)
                    pe.wait_ge(v_bd[h], t + 1)
                    for j in range(HB):
                        i = pe.matmul(PE_[h][:, j, :], Vbd[:, HB * h + j, :], Et[:, h, j, :], start=True, stop=True)
                    i.then_inc(o_ps, 1)

                def project_out(t):
                    pe.wait_ge(o_sb, 2 * t + 2)
                    if later(t):
                        pe.wait_ge(x2, t)
                    for e in range(2):
                        for q in range(HQ):
                            a = TB * q + HQ * e
                            i = pe.matmul(PY[:, e * D:(e + 1) * D], Oc[:, a:a + HQ, :, :].rearrange("p a b g -> p (a b g)"),
                                          W["o"][:, :], start=(q == 0), stop=(q == HQ - 1))
                    i.then_inc(y_ps, 1)

                def body(t, more):
                    scores(t, 0)
                    scores(t, 1)
                    if more:
                        turn(t + 1)
                        project(t + 1)
                        values(t + 1, 0)
                        values(t + 1, 1)
                    turn_probs(t, 0)
                    weigh(t, 0)
                    turn_probs(t, 1)
                    weigh(t, 1)
                    project_out(t)

                turn(0)
                project(0)
                values(0, 0)
                values(0, 1)
                run(body, pe)


def mix_experts(nc, es, X, ident, gate_w, w1, b1, w2, b2, ln_g, ln_b, out):
    with ExitStack() as s3:
        def sb(name, shape, dt=F32):
            return s3.enter_context(nc.sbuf_tensor(name, shape, dt))

        def ps(name, shape):
            return s3.enter_context(nc.psum_tensor(name, shape, F32))

        def sem(name):
            return s3.enter_context(nc.semaphore(name))

        FH = F // P
        NP = NE // 2
        G = sb("G3", [P, NE])
        W1 = sb("W13", [P, NE, F])
        W2 = sb("W23", [P, NE, FH, D])
        b1_rows = sb("b1_rows", [NE * FH, P])
        b1c = sb("b1c", [P, NE * FH])
        b2r = sb("b2r", [P, NE, D])
        gr = sb("gr", [P, NE, D])
        b_rows = sb("b_rows", [NE, D])
        iota_i = sb("iota_i", [P, NE], I32)
        iota_f = sb("iota_f", [P, NE])
        neg_half = sb("neg_half3", [P, 8])
        stat = sb("stat3", [P, 2, 6])
        mv = sb("mv3", [P, 2, 2])
        var = sb("var3", [P, 2])
        rs = sb("rs3", [P, 2])
        xn = sb("xn3", [P, 2, D])
        xT = sb("xT3", [P, 2 * P])
        XB = sb("XB", [P, NE, 2, D])
        gs = sb("gs", [P, 2, NE])
        top = sb("top", [P, 2, 8])
        top_i = sb("top_i", [P, 2, 8], U32)
        top_f = sb("top_f", [P, 2, 2])
        gap = sb("gap", [P, 2])
        th = sb("th", [P, 2])
        pr = sb("pr", [P, 2, 2])
        hot = sb("hot", [P, 2, 2, NE])
        wt = sb("wt", [P, 2, NE])
        w_kept = sb("w_kept", [P, 2, NE // 2])
        wT = sb("wT", [NE, 2 * P])
        hid = sb("hid", [P, 2, FH, 2 * P])
        Z = sb("Z", [P, NP, 4, D])
        zstat = sb("zstat", [P, NP, 4, 6])
        zm = sb("zm", [P, 2, 8])
        zd = sb("zd", [P, 2, 8])
        zv = sb("zv", [P, 2, 8])
        zr = sb("zr", [P, 2, 8])
        zs = sb("zs", [P, 2, 8])
        zb = sb("zb", [P, 2, 8])
        Y = sb("Y", [P, 2, 4, D])
        U = sb("U", [P, 2, 4, D])
        acc = sb("acc", [P, 4, D])
        res = sb("res", [P, 2, D])
        Xo = sb("Xo", [P, 2 * D])

        PH = [ps(f"PH{i}", [P, FH, 2 * P]) for i in range(2)]
        PO = [ps(f"PO{i}", [P, 4, D]) for i in range(2)]
        PA = ps("PA3", [P, 512])
        PW = ps("PW3", [P, 512])
        PB = ps("PB3", [P, 2 * D])

        w_in, set_pool, set_pe, set_dve = sem("w_in3"), sem("set_pool3"), sem("set_pe3"), sem("set_dve3")
        n_stat, n_mv, n_var, n_rs, n_xn = sem("n_stat3"), sem("n_mv3"), sem("n_var3"), sem("n_rs3"), sem("n_xn3")
        xt_ps, xt_sb, xb_sb = sem("xt_ps3"), sem("xt_sb3"), sem("xb_sb3")
        g_ps, g_sb, t_max, t_idx, t_gap, t_th, t_pr, t_hot, w_sb = (sem(n) for n in (
            "g_ps", "g_sb", "t_max", "t_idx", "t_gap", "t_th", "t_pr", "t_hot", "w_sb"))
        wt_ps, wt_sb, b_ps = sem("wt_ps3"), sem("wt_sb3"), sem("b_ps3")
        h_ps, h_sb, o_ps = sem("h_ps3"), sem("h_sb3"), sem("o_ps3")
        z_sb, z_st, z_m, z_v, z_r, z_s, z_b, y_sb, u_sb, acc_sb = (sem(n) for n in (
            "z_sb", "z_st", "z_m", "z_v", "z_r", "z_s", "z_b", "y_sb3", "u_sb3", "acc_sb"))
        x_b, r1, x3 = sem("x_b"), sem("r1"), sem("x3")
        stored = sem("stored")

        def tile_of(t):
            return X[:, t, :] if isinstance(t, int) else X[:, bass.ds(t, 1), :].rearrange("p a c -> p (a c)")

        def later(t):
            return not (isinstance(t, int) and t == 0)

        def run(slots, eng):
            slots(0)
            slots(1)
            with eng.Fori(2, T - 1) as t:
                slots(t)
            slots(T - 1)

        block = s3.enter_context(nc.Block())

        @block.sync
        def _(sp):
            sp.dma_start(W1[:, :, :], w1.rearrange("e c f -> c e f")).then_inc(w_in, 16)
            sp.dma_start(G[:, :], gate_w).then_inc(w_in, 16)
            sp.dma_start(b1_rows[:, :], b1.rearrange("e (a f) -> (e a) f", a=FH)).then_inc(w_in, 16)
            for a in range(FH):
                sp.dma_start(W2[:, :, a, :], w2[:, a * P:(a + 1) * P, :].rearrange("e f d -> f e d")).then_inc(w_in, 16)
            sp.dma_start(b2r[:, :, :].rearrange("p e d -> p (e d)"),
                         b2.rearrange("e d -> (e d)").unsqueeze(0).to_broadcast([P, NE * D])).then_inc(w_in, 16)
            sp.dma_start(gr[:, :, :].rearrange("p e d -> p (e d)"),
                         ln_g.rearrange("e d -> (e d)").unsqueeze(0).to_broadcast([P, NE * D])).then_inc(w_in, 16)
            sp.dma_start(b_rows[:, :], ln_b).then_inc(w_in, 16)

            def keep(t):
                sp.wait_ge(x3, t + 1)
                for q in range(HQ):
                    sp.dma_start(out[bass.ds(TB * t, TB), :, :].rearrange("b (g q e) c -> q b g (e c)", g=NQ, q=HQ)[q],
                                 Xo[32 * q:32 * q + 32, :]).then_inc(stored, 16)

            keep(0)
            with sp.Fori(1, T) as t:
                keep(t)
            sp.wait_ge(stored, 16 * HQ * T)

        @block.gpsimd
        def _(pool):
            pool.iota(iota_i[:, :], pattern=[[1, NE]], base=0, channel_multiplier=0).then_inc(set_pool, 1)
            pool.memset(neg_half[:, :], -0.5).then_inc(set_pool, 1)
            pool.wait_ge(w_in, 16 * 8)
            pool.wait_ge(set_pool, 2)

            def power(t):
                pool.wait_ge(n_var, t + 1)
                if later(t):
                    pool.wait_ge(n_xn, t)
                pool.tensor_tensor(rs[:, :], var[:, :], neg_half[:, 0:2], ALU.pow).then_inc(n_rs, 1)

            def spread(t, p):
                pool.wait_ge(n_xn, t + 1)
                if later(t):
                    pool.wait_ge(z_sb, NP * (t - 1) + p + 1)
                pool.tensor_tensor(XB[:, 2 * p:2 * p + 2, :, :], xn[:, :, :].unsqueeze(1).to_broadcast([P, 2, 2, D]),
                                   b2r[:, 2 * p:2 * p + 2, :].unsqueeze(2).to_broadcast([P, 2, 2, D]), ALU.add).then_inc(xb_sb, 1)

            def inverse(t, q):
                pool.wait_ge(z_v, 2 * t + q + 1)
                pool.tensor_tensor(zr[:, q, :], zv[:, q, :], neg_half[:, :], ALU.pow).then_inc(z_r, 1)

            def gather(t, p):
                pool.wait_ge(u_sb, NP * t + p + 1)
                if p == 1:
                    pool.tensor_tensor(acc[:, :, :], U[:, 0, :, :], U[:, 1, :, :], ALU.add).then_inc(acc_sb, 1)
                else:
                    pool.wait_ge(acc_sb, (NP - 1) * t + p - 1)
                    pool.tensor_tensor(acc[:, :, :], acc[:, :, :], U[:, p % 2, :, :], ALU.add).then_inc(acc_sb, 1)

            def finish(t):
                pool.wait_ge(acc_sb, (NP - 1) * t + NP - 1)
                pool.tensor_tensor(res[:, :, :], acc[:, 0:2, :], acc[:, 2:4, :], ALU.add).then_inc(r1, 1)
                pool.wait_ge(x_b, t + 1)
                pool.wait_ge(r1, t + 1)
                if later(t):
                    pool.wait_ge(stored, 16 * HQ * t)
                pool.tensor_tensor(Xo[:, :], res[:, :, :].rearrange("p e d -> p (e d)"), tile_of(t), ALU.add).then_inc(x3, 1)

            def slots(t):
                last = isinstance(t, int) and t == T - 1
                if later(t):
                    inverse(t - 1, 1)
                    spread(t, 2)
                    if not (isinstance(t, int) and t == 1):
                        finish(t - 2)
                    spread(t, 3)
                    gather(t - 1, 1)
                if not last:
                    power(t + 1)
                inverse(t, 0)
                if later(t):
                    gather(t - 1, 2)
                if not last:
                    spread(t + 1, 0)
                if later(t):
                    gather(t - 1, 3)
                if not last:
                    spread(t + 1, 1)

            power(0)
            for p in range(NP):
                spread(0, p)
            run(slots, pool)
            inverse(T - 1, 1)
            finish(T - 2)
            for p in range(1, NP):
                gather(T - 1, p)
            finish(T - 1)

        @block.tensor
        def _(pe):
            def turn(t):
                pe.wait_ge(n_xn, t + 1)
                if later(t):
                    pe.wait_ge(g_sb, t)
                for e in range(2):
                    i = pe.transpose(PA[:, e * P:(e + 1) * P], xn[:, e, :], ident[:, :])
                i.then_inc(xt_ps, 1)

            def gates(t):
                for e in range(2):
                    i = pe.matmul(PA[:, 256 + NE * e:256 + NE * e + NE], xT[:, e * P:(e + 1) * P], G[:, :], start=True, stop=True)
                i.then_inc(g_ps, 1)

            def turn_weights(t):
                pe.wait_ge(w_sb, t + 1)
                if later(t):
                    pe.wait_ge(wt_sb, t)
                for e in range(2):
                    i = pe.transpose(PW[0:NE, e * P:(e + 1) * P], wt[:, e, :], ident[:, :])
                i.then_inc(wt_ps, 1)

            def mix_bias(t):
                pe.wait_ge(wt_sb, t + 1)
                if later(t):
                    pe.wait_ge(x_b, t)
                for e in range(2):
                    i = pe.matmul(PB[:, e * D:(e + 1) * D], wT[:, e * P:(e + 1) * P], b_rows[:, :], start=True, stop=True)
                i.then_inc(b_ps, 1)

            def first(t, x):
                n = NE * t + x
                if x == 0:
                    pe.wait_ge(xt_sb, t + 1)
                if not (isinstance(t, int) and t == 0 and x < 2):
                    pe.wait_ge(h_sb, n - 1)
                for a in range(FH):
                    i = pe.matmul(PH[x % 2][:, a, :], W1[:, x, a * P:(a + 1) * P], xT[:, :], start=True, stop=True)
                i.then_inc(h_ps, 1)

            def second(t, x):
                n = NE * t + x
                pe.wait_ge(h_sb, n + 1)
                p = x // 2
                if x % 2 == 0 and not (isinstance(t, int) and t == 0 and p < 2):
                    pe.wait_ge(z_sb, NP * t + p - 1)
                for e in range(2):
                    for a in range(FH):
                        i = pe.matmul(PO[p % 2][:, 2 * (x % 2) + e, :], hid[:, x % 2, a, e * P:(e + 1) * P], W2[:, x, a, :],
                                      start=(a == 0), stop=(a == FH - 1))
                i.then_inc(o_ps, 1)

            def slots(t):
                last = isinstance(t, int) and t == T - 1
                for x in range(NE):
                    first(t, x)
                    if x == 0:
                        gates(t)
                    if x == NE - 1 and not last:
                        turn(t + 1)
                    if x > 0:
                        second(t, x - 1)
                    elif later(t):
                        second(t - 1, NE - 1)
                    if x == 4:
                        turn_weights(t)
                    if x == 5:
                        mix_bias(t)

            pe.wait_ge(w_in, 16 * 8)
            pe.transpose(PW[:, 0:NE * FH], b1_rows[:, :], ident[0:NE * FH, 0:NE * FH]).then_inc(set_pe, 1)
            pe.wait_ge(set_dve, 1)
            turn(0)
            run(slots, pe)
            second(T - 1, NE - 1)

        @block.scalar
        def _(act):
            def turned(t):
                act.wait_ge(xt_ps, t + 1)
                if later(t):
                    act.wait_ge(h_ps, NE * t)
                    act.wait_ge(g_ps, t)
                act.activation(xT[:, :], PA[:, 0:256], ACT.Copy).then_inc(xt_sb, 1)

            def gelu(t, x):
                n = NE * t + x
                act.wait_ge(h_ps, n + 1)
                if not (isinstance(t, int) and t == 0 and x < 2):
                    act.wait_ge(o_ps, n - 1)
                for a in range(FH):
                    i = act.activation(hid[:, x % 2, a, :], PH[x % 2][:, a, :], ACT.Gelu, bias=b1c[:, FH * x + a:FH * x + a + 1])
                i.then_inc(h_sb, 1)

            def half_tangent(t):
                act.wait_ge(t_gap, t + 1)
                if later(t):
                    act.wait_ge(t_pr, t)
                act.activation(th[:, :], gap[:, :], ACT.Tanh, scale=0.5).then_inc(t_th, 1)

            def weights(t):
                act.wait_ge(wt_ps, t + 1)
                if later(t):
                    act.wait_ge(b_ps, t)
                act.activation(wT[:, :], PW[0:NE, 0:2 * P], ACT.Copy).then_inc(wt_sb, 1)

            def scaled(t, p, x):
                n = NP * t + p
                if x == 0:
                    act.wait_ge(z_b, 2 * t + p // 2 + 1)
                    if not (isinstance(t, int) and t == 0 and p < 2):
                        act.wait_ge(u_sb, n - 1)
                for k in range(2 * x, 2 * x + 2):
                    f = 4 * (p % 2) + k
                    i = act.activation(Y[:, p % 2, k, :], Z[:, p, k, :], ACT.Identity, scale=zs[:, p // 2, f:f + 1],
                                       bias=zb[:, p // 2, f:f + 1])
                if x == 1:
                    i.then_inc(y_sb, 1)

            def slots(t):
                last = isinstance(t, int) and t == T - 1
                for x in range(NE):
                    gelu(t, x)
                    if x == NE - 1 and not last:
                        turned(t + 1)
                    if x == 4:
                        weights(t)
                    if x == NE - 1:
                        scaled(t, 0, 0)
                    elif later(t):
                        scaled(t - 1, (x + 1) // 2, (x + 1) % 2)
                    if x == 1:
                        half_tangent(t)

            act.wait_ge(set_dve, 1)
            turned(0)
            run(slots, act)
            for x in range(NE - 1):
                scaled(T - 1, (x + 1) // 2, (x + 1) % 2)

        @block.vector
        def _(dve):
            def norm_stats(t):
                xt = tile_of(t)
                for e in range(2):
                    i = dve.bn_stats(stat[:, e, :], xt[:, e * D:(e + 1) * D])
                i.then_inc(n_stat, 1)

            def norm_mean(t):
                dve.wait_ge(n_stat, t + 1)
                dve.nop(nofuse=True)
                for e in range(2):
                    i = dve.bn_aggr(mv[:, e, :], stat[:, e, :])
                i.then_inc(n_mv, 1)

            def norm_var(t):
                dve.wait_ge(n_mv, t + 1)
                dve.tensor_scalar(var[:, :], mv[:, :, 1], EPS_LN, None, ALU.add).then_inc(n_var, 1)

            def norm(t):
                dve.wait_ge(n_rs, t + 1)
                if later(t):
                    dve.wait_ge(xt_ps, t)
                    dve.wait_ge(xb_sb, NP * t)
                xt = tile_of(t)
                for e in range(2):
                    i = dve.tensor_scalar(xn[:, e, :], xt[:, e * D:(e + 1) * D], mv[:, e, 0:1], rs[:, e:e + 1],
                                          ALU.subtract, ALU.mult)
                i.then_inc(n_xn, 1)

            def keep_gates(t):
                dve.wait_ge(g_ps, t + 1)
                dve.tensor_copy(gs[:, :, :], PA[:, 256:256 + 2 * NE].rearrange("p (e x) -> p e x", e=2)).then_inc(g_sb, 1)

            def choose(t):
                dve.wait_ge(g_sb, t + 1)
                dve.nop(nofuse=True)
                for e in range(2):
                    i = dve.max(top[:, e, :], gs[:, e, :])
                i.then_inc(t_max, 1)

            def places(t):
                dve.wait_ge(t_max, t + 1)
                dve.tensor_tensor(gap[:, :], top[:, :, 0], top[:, :, 1], ALU.subtract).then_inc(t_gap, 1)
                for e in range(2):
                    i = dve.max_index(top_i[:, e, :], top[:, e, :], gs[:, e, :])
                i.then_inc(t_idx, 1)

            def one_hot(t):
                dve.wait_ge(t_idx, 3 * t + 1)
                dve.tensor_copy(top_f[:, :, :], top_i[:, :, 0:2]).then_inc(t_idx, 1)

            def one_hot2(t):
                dve.wait_ge(t_idx, 3 * t + 2)
                dve.tensor_tensor(hot[:, :, :, :], iota_f[:, :].unsqueeze(1).unsqueeze(1).to_broadcast([P, 2, 2, NE]),
                                  top_f[:, :, :].unsqueeze(3).to_broadcast([P, 2, 2, NE]), ALU.is_equal).then_inc(t_idx, 1)

            def shares(t):
                dve.wait_ge(t_th, t + 1)
                dve.tensor_scalar(pr[:, :, 0], th[:, :], 0.5, 0.5, ALU.mult, ALU.add)
                dve.tensor_scalar(pr[:, :, 1], th[:, :], -0.5, 0.5, ALU.mult, ALU.add).then_inc(t_pr, 1)

            def weigh(t):
                if later(t):
                    dve.wait_ge(wt_ps, t)
                    dve.tensor_copy(w_kept[:, :, :], wt[:, :, NE // 2:NE])
                dve.wait_ge(t_pr, t + 1)
                dve.wait_ge(t_idx, 3 * t + 3)
                dve.tensor_tensor(hot[:, :, :, :], hot[:, :, :, :], pr[:, :, :].unsqueeze(3).to_broadcast([P, 2, 2, NE]),
                                  ALU.mult).then_inc(t_hot, 1)

            def weigh2(t):
                dve.wait_ge(t_hot, t + 1)
                dve.tensor_tensor(wt[:, :, :], hot[:, :, 0, :], hot[:, :, 1, :], ALU.add).then_inc(w_sb, 1)

            def collect(t, p):
                n = NP * t + p
                dve.wait_ge(o_ps, NE * t + 2 * p + 2)
                dve.wait_ge(xb_sb, n + 1)
                if later(t):
                    dve.wait_ge(y_sb, NP * (t - 1) + p + 1)
                dve.tensor_tensor(Z[:, p, :, :], PO[p % 2][:, :, :], XB[:, 2 * p:2 * p + 2, :, :].rearrange("p x e d -> p (x e) d"),
                                  ALU.add).then_inc(z_sb, 1)

            def stats(t, p):
                n = NP * t + p
                dve.wait_ge(z_sb, n + 1)
                for i4 in range(4):
                    i = dve.bn_stats(zstat[:, p, i4, :], Z[:, p, i4, :])
                i.then_inc(z_st, 1)

            def spans(q):
                return [zstat[:, 2 * q:2 * q + 2, :, j] for j in (1, 2, 4, 5)]

            def wide(a, q):
                return a[:, q, :].rearrange("p (a b) -> p a b", a=2)

            def variance(t, q):
                m = 2 * t + q
                me, ve, mo, vo = spans(q)
                dve.wait_ge(z_st, NP * t + 2 * q + 2)
                dve.tensor_tensor(wide(zd, q), me, mo, ALU.subtract)
                dve.tensor_tensor(wide(zv, q), ve, vo, ALU.add)
                dve.tensor_tensor(wide(zm, q), me, mo, ALU.add).then_inc(z_m, 1)
                dve.wait_ge(z_m, 2 * m + 1)
                dve.tensor_tensor(zd[:, q, :], zd[:, q, :], zd[:, q, :], ALU.mult)
                dve.tensor_scalar(zv[:, q, :], zv[:, q, :], 1.0 / D, EPS_EXPERT, ALU.mult, ALU.add).then_inc(z_m, 1)

            def variance2(t, q):
                m = 2 * t + q
                dve.wait_ge(z_m, 2 * m + 2)
                dve.scalar_tensor_tensor(zv[:, q, :], zd[:, q, :], 0.25, zv[:, q, :], ALU.mult, ALU.add).then_inc(z_v, 1)

            def factors(t, q):
                m = 2 * t + q
                dve.wait_ge(z_r, m + 1)
                dve.wait_ge(w_sb, t + 1 + q)
                if later(t):
                    dve.wait_ge(y_sb, NP * (t - 1) + 2 * q + 2)
                dve.tensor_tensor(zs[:, q, :].rearrange("p (x e) -> p e x", x=4), zr[:, q, :].rearrange("p (x e) -> p e x", x=4),
                                  (wt[:, :, 0:NE // 2] if q == 0 else w_kept[:, :, :]), ALU.mult).then_inc(z_s, 1)

            def factors2(t, q):
                m = 2 * t + q
                dve.wait_ge(z_s, m + 1)
                dve.scalar_tensor_tensor(zb[:, q, :], zm[:, q, :], -0.5, zs[:, q, :], ALU.mult, ALU.mult).then_inc(z_b, 1)

            def gained(t, p):
                n = NP * t + p
                k = p % 2
                dve.wait_ge(y_sb, n + 1)
                if p >= 2:
                    dve.wait_ge(acc_sb, (NP - 1) * t + p - 1)
                elif later(t):
                    dve.wait_ge(acc_sb, (NP - 1) * (t - 1) + 2 + p)
                dve.tensor_tensor(U[:, k, :, :].rearrange("p (x e) d -> p x e d", x=2),
                                  Y[:, k, :, :].rearrange("p (x e) d -> p x e d", x=2),
                                  gr[:, 2 * p:2 * p + 2, :].unsqueeze(2).to_broadcast([P, 2, 2, D]), ALU.mult).then_inc(u_sb, 1)

            def biased(t):
                dve.wait_ge(b_ps, t + 1)
                dve.tensor_tensor(tile_of(t), tile_of(t), PB[:, :], ALU.add).then_inc(x_b, 1)

            def slots(t):
                last = isinstance(t, int) and t == T - 1
                keep_gates(t)
                if later(t):
                    collect(t - 1, 3)
                choose(t)
                if later(t):
                    stats(t - 1, 3)
                places(t)
                if later(t):
                    variance(t - 1, 1)
                if later(t):
                    variance2(t - 1, 1)
                    gained(t - 1, 0)
                one_hot(t)
                collect(t, 0)
                one_hot2(t)
                stats(t, 0)
                shares(t)
                weigh(t)
                if not last:
                    norm_stats(t + 1)
                weigh2(t)
                if later(t):
                    factors(t - 1, 1)
                if not last:
                    norm_mean(t + 1)
                if later(t):
                    factors2(t - 1, 1)
                    gained(t - 1, 1)
                if not last:
                    norm_var(t + 1)
                collect(t, 1)
                stats(t, 1)
                if later(t):
                    gained(t - 1, 2)
                variance(t, 0)
                variance2(t, 0)
                if not last:
                    norm(t + 1)
                collect(t, 2)
                biased(t)
                stats(t, 2)
                factors(t, 0)
                if later(t):
                    gained(t - 1, 3)
                factors2(t, 0)

            dve.wait_ge(set_pool, 2)
            dve.tensor_copy(iota_f[:, :], iota_i[:, :])
            dve.wait_ge(set_pe, 1)
            dve.tensor_copy(b1c[:, :], PW[:, 0:NE * FH]).then_inc(set_dve, 1)
            norm_stats(0)
            norm_mean(0)
            norm_var(0)
            norm(0)
            run(slots, dve)
            collect(T - 1, 3)
            stats(T - 1, 3)
            gained(T - 1, 0)
            variance(T - 1, 1)
            variance2(T - 1, 1)
            gained(T - 1, 1)
            dve.wait_ge(w_sb, T)
            dve.tensor_copy(w_kept[:, :, :], wt[:, :, NE // 2:NE]).then_inc(w_sb, 1)
            factors(T - 1, 1)
            factors2(T - 1, 1)
            gained(T - 1, 2)
            gained(T - 1, 3)


def store(nc, es, X, out):
    done = es.enter_context(nc.semaphore("stored_dbg"))
    block = es.enter_context(nc.Block())

    @block.sync
    def _(sp):
        for q in range(HQ):
            for b in range(TB):
                sp.dma_start(out.rearrange("(t b) (g q e) c -> q b g t (e c)", t=T, g=NQ, q=HQ)[q, b],
                             X[32 * q + NQ * b:32 * q + NQ * b + NQ, :, :]).then_inc(done, 16)
        sp.wait_ge(done, 16 * HQ * TB)


_INS = ["x", "ctx_1024", "fside_SxS2_0"] + ["L0_attn_" + n for n in ("Wq", "bq", "Wk", "bk", "Wv", "bv", "Wo", "bo")] + [
    "L0_ffn_" + n for n in ("gate_w", "w1", "b1", "w2", "b2", "ln_g", "ln_b")]


def kernel(**inputs):
    import numpy as _np
    import concourse.bacc as _bacc
    from concourse import mybir as _mybir
    from concourse.bass_utils import run_bass_kernel_spmd as _run

    nc = _bacc.Bacc("TRN2", target_bir_lowering=False, num_devices=1)
    arrays, args = {}, []
    for name in _INS:
        a = _np.ascontiguousarray(inputs[name])
        arrays[f"in_{name}_dram"] = a
        args.append(nc.dram_tensor(f"in_{name}_dram", a.shape, _mybir.dt.from_np(a.dtype), kind="ExternalInput").ap())
    args.append(nc.dram_tensor("out_0_dram", (B, L, D), F32, kind="ExternalOutput").ap())
    perceiver_layer(nc, *args)
    r = _run(nc, [arrays], core_ids=[0])
    return r.results[0]["out_0_dram"]
```

```python
from contextlib import ExitStack

import concourse.bass as bass
from concourse import mybir

F32 = mybir.dt.float32
F32R = mybir.dt.float32r
I32 = mybir.dt.int32
U32 = mybir.dt.uint32
ALU = mybir.AluOpType
ACT = mybir.ActivationFunctionType
AX = mybir.AxisListType

B, L, D = 128, 32, 128
S = 257
H, DK = 16, 8
NE, F = 8, 256
EPS_LN, EPS_EXPERT = 1e-5, 1e-6
SCALE = float(DK) ** -0.5

P = 128
NQ, HQ = 4, 4
TB = 8
HB = TB // 2
T = B // TB
KT = 2
STEPS = 2 * TB
HSTEPS = STEPS // 2
DECAY = -0.25
MASKED = -1.0e30


def perceiver_layer(nc, x, ctx, fmask, Wq, bq, Wk, bk, Wv, bv, Wo, bo, gate_w, w1, b1, w2, b2, ln_g, ln_b, out):
    with ExitStack() as es:
        def sb(name, shape, dt=F32):
            return es.enter_context(nc.sbuf_tensor(name, shape, dt))

        def sem(name):
            return es.enter_context(nc.semaphore(name))

        ident = sb("ident", [P, P])
        head_of = sb("head_of", [P, H])
        own_of = sb("own_of", [P, 2, HQ])
        hh_of = sb("hh_of", [P, HQ])
        hh_scaled = sb("hh_scaled", [P, HQ, L])
        mask_T = sb("mask_T", [P, 2, KT, HQ * L])
        mask_last = sb("mask_last", [HB * NQ, HQ * L])
        last_sel = sb("last_sel", [HB * NQ, HB, D])
        X = sb("X", [P, T, 2 * D])

        setup_in = sem("setup_in")
        xperm_in = sem("xperm_in")
        pool_set = sem("pool_set")
        dve_set = sem("dve_set")
        pe_set = sem("pe_set")
        w2_in, pool_set2, pe_set2, act_set2, dve_set2 = (sem(n) for n in ("w2_in", "pool_set2", "pe_set2", "act_set2", "dve_set2"))
        w3_in, b1_in, pool_set3, pe_set3, dve_set3 = (sem(n) for n in ("w3_in", "b1_in", "pool_set3", "pe_set3", "dve_set3"))

        W = {n: sb(f"W{n}", [P, D]) for n in "qkvo"}
        brow = sb("brow", [3, D])
        bo_row = sb("bo_row", [1, D])
        ones_row = sb("ones_row", [1, P])
        bcol = sb("bcol", [P, 3])
        out_bias = sb("out_bias", [P, D])
        lag_i = sb("lag_i", [L, L], I32)
        lag = sb("lag", [L, L])
        lag_ln = sb("lag_ln", [L, L])
        lag_p = sb("lag_p", [L, L])
        turn_l = sb("turn_l", [L, HQ, L])
        hh_wide = sb("hh_wide", [P, HQ, TB])
        decay = sb("decay", [P, HB * NQ, L])
        neg_half2 = sb("neg_half2", [P, 2])
        Kbd = sb("Kbd2", [P, TB, NQ, L])
        Vbd = sb("Vbd2", [P, TB, D])

        FH = F // P
        G = sb("G3", [P, NE])
        W1 = sb("W13", [P, NE, F])
        W2 = sb("W23", [P, NE, FH, D])
        b1_rows = sb("b1_rows", [NE * FH, P])
        b1c = sb("b1c", [P, NE * FH])
        b2r = sb("b2r", [P, NE, D])
        gr = sb("gr", [P, NE, D])
        b_rows = sb("b_rows", [NE, D])
        iota_i = sb("iota_i", [P, NE], I32)
        iota_f = sb("iota_f", [P, NE])
        neg_half3 = sb("neg_half3", [P, 8])

        with ExitStack() as s1:
            def sb1(name, shape, dt=F32):
                return s1.enter_context(nc.sbuf_tensor(name, shape, dt))

            def ps1(name, shape):
                return s1.enter_context(nc.psum_tensor(name, shape, F32))

            def sem1(name):
                return s1.enter_context(nc.semaphore(name))

            V = sb1("V", [P, TB, KT, D])
            last_rep = sb1("last_rep", [HB * NQ, 2, D])
            V_split = sb1("V_split", [P, 4, KT, H, 2, DK], F32R)
            last_split = sb1("last_split", [HB * NQ, 2, H, 2, DK], F32R)
            last_bd = sb1("last_bd", [HB * NQ, 2, HB, D])
            xh = sb1("xh", [P, 2, D])
            xn = sb1("xn", [P, H, 2, DK])
            xstat = sb1("xstat", [P, 6])
            xmv = sb1("xmv", [P, 2])
            xrs = sb1("xrs", [P, 1])
            xvar = sb1("xvar", [P, 1])
            neg_half = sb1("neg_half", [P, 1])
            ones = sb1("ones", [P, KT * D])
            QX = 2 * 2 * HB
            Qt = sb1("Qt", [P, L, QX], F32R)
            Qbd = sb1("Qbd", [P, 2, 2, HQ * L, QX], F32R)
            Kt = sb1("Kt", [P, 4, 2, S + 1], F32R)
            K_last = sb1("K_last", [P, 2, 2, HB], F32R)
            neg_max = sb1("neg_max", [P, 2, 2])
            E = sb1("E", [P, 2, HB * NQ, S])
            den = sb1("den", [P, 2, HB * NQ])
            rden = sb1("rden", [P, HB * NQ])
            Et = sb1("Et", [P, 4, 2, KT, HQ * L])
            last_Et = sb1("last_Et", [HB * NQ, HQ * L])
            O_c = sb1("O_c", [P, HB, HQ * L])
            O_n = sb1("O_n", [P, DK, TB * NQ])
            O_t = sb1("O_t", [P, DK, L])

            SC = [ps1(f"SC{i}", [P, 2, 512]) for i in range(2)]
            ETP = [ps1(f"ETP{i}", [P, 512]) for i in range(2)]
            AV = ps1("AV", [P, HB, HQ * L])
            MISC = ps1("MISC", [P, 512])
            QT_LAST = MISC[:, 2 * P:2 * P + 2 * HB * NQ]
            LAST = SC[1][0:HB * NQ, 1, 384:512]

            ctx_in = [sem1(f"ctx_in{k}") for k in range(TB // 2)]
            last_in = [sem1(f"last_in{h}") for h in range(2)]
            x_in = [sem1(f"x_in{h}") for h in range(2)]
            xstat_sb, xmean_sb, xvar_sb, xrs_sb, xn_sb = (sem1(n) for n in ("xstat_sb", "xmean_sb", "xvar_sb", "xrs_sb", "xn_sb"))
            consts, q_zero = sem1("consts"), sem1("q_zero")
            vs_sb, last_sb = sem1("vs_sb"), sem1("last_sb")
            kt_ps, kt_sb, kl_sb = sem1("kt_ps"), sem1("kt_sb"), sem1("kl_sb")
            qt_ps, q_hi, q_lo = sem1("qt_ps"), sem1("q_hi"), sem1("q_lo")
            q_in = [sem1(f"q_in{h}") for h in range(2)]
            sc_ps, max_sb, exp_sb = sem1("sc_ps"), sem1("max_sb"), sem1("exp_sb")
            et_ps, et_sb = sem1("et_ps"), sem1("et_sb")
            lastt_ps, lastt_sb, last_bd_set = sem1("lastt_ps"), sem1("lastt_sb"), sem1("last_bd_set")
            av_ps, av_full = sem1("av_ps"), sem1("av_full")
            rden_set = sem1("rden_set")
            o_c, o_ps, o_n, o_t, x1 = (sem1(n) for n in ("o_c", "o_ps", "o_n", "o_t", "x1"))
            Q_DMAS = 16 * 2 * HQ

            def load_ctx(sp, t, k):
                sp.dma_start(V[:, 2 * k:2 * k + 2, :, :].rearrange("p b k c -> p b (k c)"),
                             ctx[bass.ds(TB * t + 2 * k, 2), 0:KT * P, :].rearrange("b (p k) c -> p b (k c)", p=P)
                             ).then_inc(ctx_in[k], 16)

            def load_last(sp, t, h):
                b0 = TB * t + HB * h
                for j in range(HB):
                    sp.dma_start(last_rep[NQ * j:NQ * j + NQ, h, :],
                                 ctx[bass.ds(b0 + j, 1), S - 1, :].to_broadcast([NQ, D])).then_inc(last_in[h], 16)

            def load_x(sp, t, h):
                sp.dma_start(xh[:, h, :], x[bass.ds(TB * t + HB * h, HB), :, :].rearrange("b l c -> (b l) c")).then_inc(x_in[h], 16)

            fm = sb1("fm", [L, S])
            MISC2, MISC3 = ETP

            def run_tiles(steps, eng):
                steps(0, True, False)
                with eng.Fori(1, T - 1) as t:
                    steps(t, False, False)
                steps(T - 1, False, True)

            block = s1.enter_context(nc.Block())

            @block.sync
            def _(sp):
                def place_queries(t, h):
                    sp.wait_ge(q_lo, 2 * t + h + 1)
                    if isinstance(t, int) and t == 0:
                        sp.wait_ge(q_zero, 2)
                    for u in range(2):
                        for q in range(HQ):
                            r = slice(64 * u + 16 * q, 64 * u + 16 * q + 16)
                            sp.dma_start(Qbd[r, h, u, L * q:L * q + L, :].bitcast(F32), Qt[r, :, :].bitcast(F32)).then_inc(q_in[h], 16)

                def load_residual(q):
                    for b in range(TB):
                        sp.dma_start(X[32 * q + NQ * b:32 * q + NQ * b + NQ, :, :],
                                     x.rearrange("(t b) (g q e) c -> q b g t (e c)", t=T, g=NQ, q=HQ)[q, b]).then_inc(xperm_in, 16)

                def steps(t, fresh):
                    sp.wait_ge(xn_sb, 2 * t + 1)
                    sp.nop(nofuse=True)
                    load_x(sp, t + 1, 0)
                    place_queries(t, 1)
                    if not fresh:
                        sp.wait_ge(av_ps, TB * t)
                        sp.nop(nofuse=True)
                        load_ctx(sp, t, 3)
                    sp.wait_ge(last_bd_set, 2 * t + 1)
                    sp.nop(nofuse=True)
                    load_last(sp, t + 1, 0)
                    if fresh:
                        for q in range(HQ // 2):
                            load_residual(q)
                    sp.wait_ge(av_ps, TB * t + 2)
                    sp.nop(nofuse=True)
                    load_ctx(sp, t + 1, 0)
                    sp.wait_ge(xn_sb, 2 * t + 2)
                    sp.nop(nofuse=True)
                    load_x(sp, t + 1, 1)
                    place_queries(t + 1, 0)
                    sp.wait_ge(av_ps, TB * t + 4)
                    sp.nop(nofuse=True)
                    load_ctx(sp, t + 1, 1)
                    sp.wait_ge(last_bd_set, 2 * t + 2)
                    sp.nop(nofuse=True)
                    load_last(sp, t + 1, 1)
                    if fresh:
                        for q in range(HQ // 2, HQ):
                            load_residual(q)
                    sp.wait_ge(av_ps, TB * t + 6)
                    sp.nop(nofuse=True)
                    load_ctx(sp, t + 1, 2)

                sp.dma_start(fm[:, :], fmask).then_inc(setup_in, 16)
                load_x(sp, 0, 0)
                load_last(sp, 0, 0)
                load_ctx(sp, 0, 0)
                for n, src in zip("qkvo", (Wq, Wk, Wv, Wo)):
                    sp.dma_start(W[n][:, :], src).then_inc(w2_in, 16)
                for i, src in enumerate((bq, bk, bv)):
                    sp.dma_start(brow[i:i + 1, :], src.unsqueeze(0)).then_inc(w2_in, 16)
                sp.dma_start(bo_row[:, :], bo.unsqueeze(0)).then_inc(w2_in, 16)
                sp.dma_start(b1_rows[:, :], b1.rearrange("e (a f) -> (e a) f", a=FH)).then_inc(b1_in, 16)
                load_x(sp, 0, 1)
                load_ctx(sp, 0, 1)
                load_last(sp, 0, 1)
                load_ctx(sp, 0, 2)
                load_ctx(sp, 0, 3)
                place_queries(0, 0)
                steps(0, True)
                with sp.Fori(1, T - 1) as t:
                    steps(t, False)
                place_queries(T - 1, 1)
                sp.wait_ge(av_ps, TB * (T - 1))
                load_ctx(sp, T - 1, 3)
                sp.dma_start(W1[:, :, :], w1.rearrange("e c f -> c e f")).then_inc(w3_in, 16)
                sp.dma_start(G[:, :], gate_w).then_inc(w3_in, 16)
                for a in range(FH):
                    sp.dma_start(W2[:, :, a, :], w2[:, a * P:(a + 1) * P, :].rearrange("e f d -> f e d")).then_inc(w3_in, 16)
                sp.dma_start(b2r[:, :, :].rearrange("p e d -> p (e d)"),
                             b2.rearrange("e d -> (e d)").unsqueeze(0).to_broadcast([P, NE * D])).then_inc(w3_in, 16)
                sp.dma_start(gr[:, :, :].rearrange("p e d -> p (e d)"),
                             ln_g.rearrange("e d -> (e d)").unsqueeze(0).to_broadcast([P, NE * D])).then_inc(w3_in, 16)
                sp.dma_start(b_rows[:, :], ln_b).then_inc(w3_in, 16)

            @block.gpsimd
            def _(pool):
                pool.memset(ident[:, :], 0.0).then_inc(pool_set, 1)
                pool.memset(head_of[:, :], 1.0).then_inc(pool_set, 1)
                pool.memset(last_sel[:, :, :], 0.0).then_inc(pool_set, 1)
                pool.wait_ge(pool_set, 3)
                pool.affine_select(out=ident[:, :], in_=ident[:, :], compare_op=ALU.not_equal, fill=1.0, base=0,
                                   pattern=[[-1, P]], channel_multiplier=1).then_inc(pool_set, 1)
                pool.affine_select(out=head_of[:, :], in_=head_of[:, :], compare_op=ALU.is_ge, fill=0.0, base=0,
                                   pattern=[[-DK, H]], channel_multiplier=1).then_inc(pool_set, 1)
                pool.wait_ge(pool_set, 5)
                pool.affine_select(out=head_of[:, :], in_=head_of[:, :], compare_op=ALU.is_ge, fill=0.0, base=DK - 1,
                                   pattern=[[DK, H]], channel_multiplier=-1).then_inc(pool_set, 1)
                pool.affine_select(out=last_sel[:, :, :].rearrange("p j (g c) -> p j g c", g=NQ),
                                   in_=last_sel[:, :, :].rearrange("p j (g c) -> p j g c", g=NQ),
                                   compare_op=ALU.not_equal, fill=1.0, base=0,
                                   pattern=[[-NQ, HB], [-1, NQ], [0, D // NQ]], channel_multiplier=1).then_inc(pool_set, 1)
                pool.iota(lag_i[:, :], pattern=[[-1, L]], base=0, channel_multiplier=1).then_inc(pool_set2, 1)
                pool.memset(neg_half2[:, :], -0.5).then_inc(pool_set2, 1)
                pool.memset(ones_row[:, :], 1.0).then_inc(pool_set2, 1)
                pool.iota(iota_i[:, :], pattern=[[1, NE]], base=0, channel_multiplier=0).then_inc(pool_set3, 1)
                pool.memset(neg_half3[:, :], -0.5).then_inc(pool_set3, 1)
                pool.memset(neg_half[:, :], -0.5).then_inc(consts, 1)
                pool.memset(ones[:, :], 1.0).then_inc(consts, 1)
                pool.wait_ge(consts, 2)
                pool.wait_ge(pool_set, 7)

                def split(t, j, first=False):
                    b = TB * t + j
                    pool.wait_ge(ctx_in[j // 2], 16 * (t + 1))
                    if not first:
                        pool.wait_ge(kt_ps, b - 3)
                    r = j % 4
                    v = V[:, j, :, :].rearrange("p k (g c) -> p k g c", g=H)
                    pool.tensor_tensor(V_split[:, r, :, :, 0, :], v, ones[:, :].rearrange("p (k g c) -> p k g c", k=KT, g=H),
                                       ALU.mult).then_inc(vs_sb, 1)
                    pool.wait_ge(vs_sb, 2 * b + 1)
                    pool.tensor_tensor(V_split[:, r, :, :, 1, :], v, V_split[:, r, :, :, 0, :], ALU.subtract).then_inc(vs_sb, 1)

                def split_last(t, h):
                    m = 2 * t + h
                    pool.wait_ge(last_in[h], 16 * HB * (t + 1))
                    if not (isinstance(t, int) and t == 0):
                        pool.wait_ge(qt_ps, m - 1)
                    v = last_rep[:, h, :].rearrange("p (g c) -> p g c", g=H)
                    pool.tensor_tensor(last_split[:, h, :, 0, :], v, ones[0:HB * NQ, 0:D].rearrange("p (g c) -> p g c", g=H),
                                       ALU.mult).then_inc(last_sb, 1)
                    pool.wait_ge(last_sb, 2 * m + 1)
                    pool.tensor_tensor(last_split[:, h, :, 1, :], v, last_split[:, h, :, 0, :], ALU.subtract).then_inc(last_sb, 1)

                def power(t, h):
                    pool.wait_ge(xvar_sb, 2 * t + h + 1)
                    pool.tensor_tensor(xrs[:, :], xvar[:, :], neg_half[:, :], ALU.pow).then_inc(xrs_sb, 1)

                def place_last(t, h):
                    m = 2 * t + h
                    pool.wait_ge(last_in[h], 16 * HB * (t + 1))
                    if not (isinstance(t, int) and t == 0):
                        pool.wait_ge(av_full, m - 1)
                    pool.tensor_tensor(last_bd[:, h, :, :], last_rep[:, h, :].unsqueeze(1).to_broadcast([HB * NQ, HB, D]),
                                       last_sel[:, :, :], ALU.mult).then_inc(last_bd_set, 1)

                def add_tile(t):
                    pool.wait_ge(o_t, t + 1)
                    pool.wait_ge(xperm_in, 16 * HQ * TB)
                    xt = X[:, t, :] if isinstance(t, int) else X[:, bass.ds(t, 1), :].rearrange("p a c -> p (a c)")
                    pool.tensor_tensor(xt.rearrange("p (l d) -> p l d", d=DK), O_t[:, :, :].rearrange("p d l -> p l d"),
                                       xt.rearrange("p (l d) -> p l d", d=DK), ALU.add).then_inc(x1, 1)

                def steps(t, fresh, final):
                    for h in range(2):
                        t1, h1 = (t, 1) if h == 0 else (t + 1, 0)
                        place_last(t, h)
                        if not (final and h == 1):
                            split(t1, HB * h1)
                            split(t1, HB * h1 + 1)
                        if not final:
                            power(t + 1, h)
                            if not fresh:
                                split_last(t + 1, h)
                        if not (final and h == 1):
                            split(t1, HB * h1 + 2)
                            split(t1, HB * h1 + 3)
                        if fresh:
                            split_last(t + 1, h)
                        if h == 0 and not fresh:
                            add_tile(t - 1)

                power(0, 0)
                split_last(0, 0)
                split(0, 0, first=True)
                pool.memset(Qbd[:, 1, :, :, :].bitcast(F32), 0.0).then_inc(q_zero, 1)
                split(0, 1, first=True)
                power(0, 1)
                split_last(0, 1)
                pool.wait_ge(act_set2, 2)
                pool.affine_select(out=lag_ln[:, :], in_=lag_ln[:, :], compare_op=ALU.is_ge, fill=MASKED, base=0,
                                   pattern=[[-1, L]], channel_multiplier=1).then_inc(pool_set2, 1)
                pool.memset(Kbd[:, :, :, :], 0.0).then_inc(pool_set2, 1)
                pool.memset(Vbd[:, :, :], 0.0).then_inc(pool_set2, 1)
                split(0, 2, first=True)
                split(0, 3, first=True)
                run_tiles(steps, pool)
                add_tile(T - 1)

            @block.tensor
            def _(pe):
                def turn_keys(t, j, first=False):
                    b, m = TB * t + j, 2 * t + j // HB
                    pe.wait_ge(vs_sb, 2 * b + 2)
                    if first:
                        pe.wait_ge(q_lo, 1)
                        pe.wait_ge(q_hi, 1)
                    else:
                        pe.wait_ge(kt_sb, b)
                    if j % HB == 0 and not first and not (isinstance(t, int) and t == 0):
                        pe.wait_ge(o_n, m - 1)
                    if j % HB == 2 and not (isinstance(t, int) and t == T - 1 and j == TB - 2):
                        pe.wait_ge(q_hi, m + 2)
                        pe.wait_ge(q_lo, m + 2)
                    for p in range(2):
                        for k in range(KT):
                            c = (KT * p + k) * P
                            i = pe.transpose(MISC[:, c:c + P],
                                             V_split[:, j % 4, k, 8 * p:8 * p + 8, :, :].rearrange("p g x c -> p (g x c)").bitcast(F32),
                                             ident[:, :])
                    i.then_inc(kt_ps, 1)

                def turn_queries(t, h, first=False):
                    m = 2 * t + h
                    pe.wait_ge(xn_sb, m + 1)
                    pe.wait_ge(last_sb, 2 * m + 2)
                    if not first:
                        pe.wait_ge(kt_sb, HB * m - 2)
                    for p in range(2):
                        pe.transpose(MISC[:, p * P:(p + 1) * P], xn[:, 8 * p:8 * p + 8, :, :].rearrange("p g x c -> p (g x c)"),
                                     ident[:, :])
                        n = HB * NQ
                        i = pe.transpose(QT_LAST[:, p * n:(p + 1) * n],
                                         last_split[:, h, 8 * p:8 * p + 8, :, :].rearrange("p g x c -> p (g x c)").bitcast(F32),
                                         ident[0:n, 0:n])
                    i.then_inc(qt_ps, 1)

                def turn_last(t, h):
                    pe.transpose(LAST, E[:, h, :, S - 1], ident[:, :]).then_inc(lastt_ps, 1)

                def scores(t, s, first=False):
                    j, n = s // 2, STEPS * t + s
                    if s % 2 == 0:
                        pe.wait_ge(kt_sb, TB * t + j + 1)
                        pe.wait_ge(kl_sb, TB * t + j + 1)
                    if s % HSTEPS == 0:
                        pe.wait_ge(q_in[s // HSTEPS], Q_DMAS * (t + 1))
                    if not first:
                        pe.wait_ge(exp_sb, n - 1)
                    if not (isinstance(t, int) and t == 0 and s < HSTEPS):
                        m = 2 * t + s // HSTEPS
                        if s % HSTEPS == 1:
                            turn_last(*((t, 0) if s > HSTEPS else (t - 1, 1)))
                        if s % HSTEPS == 3:
                            pe.wait_ge(lastt_sb, m)
                    for u in range(2):
                        for x in range(2):
                            i = pe.matmul(SC[s % 2][:, u, 0:S + 1], Qbd[:, j // HB, u, :, (2 * x + s % 2) * HB + j % HB],
                                          Kt[:, j % 4, s % 2, :], start=(x == 0), stop=(x == 1))
                    i.then_inc(sc_ps, 1)

                def turn_probs(t, s, first=False):
                    n = STEPS * t + s
                    h, u0 = s // HSTEPS, 2 * (s % HSTEPS)
                    pe.wait_ge(exp_sb, n + 1)
                    if not first:
                        pe.wait_ge(et_sb, n - 1)
                    for u in range(2):
                        for k in range(KT):
                            c = (2 * u + k) * P
                            i = pe.transpose(ETP[s % 2][:, c:c + P], E[:, h, u0 + u, k * P:(k + 1) * P], ident[:, :])
                    i.then_inc(et_ps, 1)

                def weigh_values(t, j, first=False):
                    h = j // HB
                    pe.wait_ge(et_sb, STEPS * t + 2 * j + 2)
                    if j % HB == 0 and not first:
                        pe.wait_ge(o_c, 2 * t + h)
                    for k in range(KT):
                        for g in range(NQ):
                            i = pe.matmul(AV[32 * g:32 * g + 32, j % HB, :], V[:, j, k, 32 * g:32 * g + 32],
                                          Et[:, 2 * (j % 2) + g // 2, g % 2, k, :],
                                          start=(j % HB == 0 and k == 0), stop=False, skip_group_check=True)
                    i.then_inc(av_ps, 1)

                def weigh_last(t, h):
                    m = 2 * t + h
                    pe.wait_ge(lastt_sb, m + 1)
                    pe.wait_ge(last_bd_set, m + 1)
                    for j in range(HB):
                        i = pe.matmul(AV[:, j, :], last_bd[:, h, j, :], last_Et[:, :], start=False, stop=(j == HB - 1),
                                      skip_group_check=True)
                    i.then_inc(av_full, 1)

                def turn_out(t, h, final=False):
                    m = 2 * t + h
                    pe.wait_ge(o_c, m + 1)
                    if not final:
                        pe.wait_ge(kt_sb, HB * m + HB + 4)
                    for j in range(HB):
                        i = pe.transpose(MISC[:, P * j:P * j + P], O_c[:, j, :], ident[:, :])
                    i.then_inc(o_ps, 1)

                def back(t, s, lag):
                    return (t, s - lag) if s >= lag else (t - 1, s + STEPS - lag)

                def lagging(t, s):
                    fresh = isinstance(t, int) and t == 0
                    if not (fresh and s < 2):
                        tt, ss = back(t, s, 2)
                        turn_probs(tt, ss, first=fresh and s < 4)
                    if s % 2 == 1 and not (fresh and s < 5):
                        tt, ss = back(t, s, 5)
                        weigh_values(tt, ss // 2, first=fresh and s == 5)
                    if not (fresh and s < HSTEPS):
                        tt, ss = back(t, s, HSTEPS)
                        if s % HSTEPS == 3:
                            weigh_last(tt, ss // HSTEPS)
                        if s % HSTEPS == 5:
                            turn_out(tt, ss // HSTEPS)

                def steps(t, fresh, final):
                    for s in range(STEPS):
                        scores(t, s, first=fresh and s < 2)
                        if s % HSTEPS in (0, 3, 7):
                            if s // 2 + 1 < TB:
                                turn_keys(t, s // 2 + 1)
                            elif not final:
                                turn_keys(t + 1, 0)
                        if s == 1:
                            turn_queries(t, 1)
                        if s == 9 and not final:
                            turn_queries(t + 1, 0)
                        lagging(t, s)
                        if s % HSTEPS == 4:
                            if s // 2 + 1 < TB:
                                turn_keys(t, s // 2 + 1)
                            elif not final:
                                turn_keys(t + 1, 0)

                pe.wait_ge(setup_in, 16)
                pe.wait_ge(pool_set, 7)
                for k in range(KT):
                    pe.transpose(MISC[:, k * L:(k + 1) * L], fm[:, k:KT * P:KT], ident[0:L, 0:L])
                pe.matmul(MISC[0:HB * NQ, 64:64 + L], fm[:, S - 1:S].to_broadcast([L, HB * NQ]),
                          ident[0:L, 0:L], start=True, stop=True).then_inc(pe_set, 1)
                pe.wait_ge(dve_set, 8)
                turn_queries(0, 0, first=True)
                turn_keys(0, 0, first=True)
                pe.wait_ge(dve_set2, 8)
                pe.wait_ge(w2_in, 16 * 8)
                pe.matmul(MISC2[:, 0:L], turn_l[:, :, :].rearrange("p q l -> p (q l)"), lag_p[:, :], start=True, stop=True)
                pe.transpose(MISC2[:, 64:67], brow[:, :], ident[0:3, 0:3]).then_inc(pe_set2, 1)
                pe.wait_ge(dve_set2, 10)
                pe.matmul(MISC2[:, 128:128 + D], bcol[:, 2:3].to_broadcast([P, P]), W["o"][:, :], start=True, stop=False)
                pe.matmul(MISC2[:, 128:128 + D], ones_row[:, :], bo_row[:, :], start=False, stop=True).then_inc(pe_set2, 1)
                pe.wait_ge(b1_in, 16)
                pe.transpose(MISC3[:, 0:NE * FH], b1_rows[:, :], ident[0:NE * FH, 0:NE * FH]).then_inc(pe_set3, 1)
                run_tiles(steps, pe)
                turn_probs(T - 1, STEPS - 2)
                turn_probs(T - 1, STEPS - 1)
                turn_last(T - 1, 1)
                weigh_values(T - 1, TB - 2)
                weigh_values(T - 1, TB - 1)
                weigh_last(T - 1, 1)
                turn_out(T - 1, 1, final=True)

            @block.scalar
            def _(act):
                def keep_keys(t, j, first=False):
                    b = TB * t + j
                    act.wait_ge(kt_ps, b + 1)
                    if not first:
                        act.wait_ge(sc_ps, 2 * (b - 3))
                    act.activation(Kt[:, j % 4, :, 0:KT * P], MISC[:, :].rearrange("p (a s) -> p a s", a=2), ACT.Copy).then_inc(kt_sb, 1)

                def keep_queries(t, h, first=False):
                    m = 2 * t + h
                    act.wait_ge(qt_ps, m + 1)
                    if not first:
                        act.wait_ge(q_in[1 - h], Q_DMAS * (t + h))
                    act.activation(Qt[:, :, 0:QX // 2].rearrange("p l (a j) -> p a j l", a=2),
                                   MISC[:, 0:2 * P].rearrange("p (a j l) -> p a j l", a=2, j=HB), ACT.Copy,
                                   scale=SCALE).then_inc(q_hi, 1)

                def exponentials(t, s, first=False):
                    n = STEPS * t + s
                    h, u0 = s // HSTEPS, 2 * (s % HSTEPS)
                    act.wait_ge(max_sb, n + 1)
                    if s % HSTEPS == 0 and not first:
                        act.wait_ge(lastt_ps, 2 * t + h - 1)
                        act.wait_ge(rden_set, 2 * t + h - 1)
                    for u in range(2):
                        i = act.activation(E[:, h, u0 + u, :], SC[s % 2][:, u, 0:S], ACT.Exp,
                                           bias=neg_max[:, s % 2, u:u + 1], accum_out=den[:, h, u0 + u:u0 + u + 1])
                    i.then_inc(exp_sb, 1)

                def keep_sums(t, h):
                    act.wait_ge(av_full, 2 * t + h + 1)
                    act.activation(O_c[:, :, :], AV[:, :, :], ACT.Copy).then_inc(o_c, 1)

                def steps(t, fresh, final):
                    for s in range(STEPS):
                        if s % HSTEPS in (0, 3, 4, 7):
                            if s // 2 + 1 < TB:
                                keep_keys(t, s // 2 + 1, first=fresh and s < 6)
                            elif not final:
                                keep_keys(t + 1, 0)
                        if s % HSTEPS == 1 and not (final and s >= HSTEPS):
                            keep_queries(t if s < HSTEPS else t + 1, 1 if s < HSTEPS else 0)
                        exponentials(t, s, first=fresh)
                        if s % HSTEPS == 3 and not (fresh and s < HSTEPS):
                            keep_sums(t if s >= HSTEPS else t - 1, 0 if s >= HSTEPS else 1)

                keep_queries(0, 0, first=True)
                keep_keys(0, 0, first=True)
                act.wait_ge(dve_set2, 2)
                act.activation(lag_ln[:, :], lag[:, :], ACT.Ln).then_inc(act_set2, 1)
                act.wait_ge(act_set2, 1)
                act.activation(lag_ln[:, :], lag_ln[:, :], ACT.Copy, scale=DECAY).then_inc(act_set2, 1)
                run_tiles(steps, act)
                keep_sums(T - 1, 1)

            @block.vector
            def _(dve):
                def norm_stats(t, h):
                    dve.wait_ge(x_in[h], 16 * (t + 1))
                    dve.bn_stats(xstat[:, :], xh[:, h, :]).then_inc(xstat_sb, 1)

                def norm_mean(t, h):
                    m = 2 * t + h
                    dve.wait_ge(xstat_sb, m + 1)
                    dve.nop(nofuse=True)
                    dve.bn_aggr(xmv[:, :], xstat[:, :]).then_inc(xmean_sb, 1)

                def norm_var(t, h, first=False):
                    m = 2 * t + h
                    dve.wait_ge(xmean_sb, m + 1)
                    if not first:
                        dve.wait_ge(xrs_sb, m)
                    dve.tensor_scalar(xvar[:, :], xmv[:, 1:2], EPS_LN, None, ALU.add).then_inc(xvar_sb, 1)

                def normalise(t, h, first=False):
                    m = 2 * t + h
                    dve.wait_ge(xrs_sb, m + 1)
                    if not first:
                        dve.wait_ge(qt_ps, m)
                    dve.tensor_scalar(xn[:, :, :, :], xh[:, h, :].rearrange("p (g c) -> p g c", g=H).unsqueeze(2).to_broadcast([P, H, 2, DK]),
                                      xmv[:, 0:1], xrs[:, 0:1], ALU.subtract, ALU.mult).then_inc(xn_sb, 1)

                def keep_queries(t, h):
                    m = 2 * t + h
                    dve.wait_ge(q_hi, m + 1)
                    dve.scalar_tensor_tensor(Qt[:, :, QX // 2:QX].rearrange("p l (a j) -> p a j l", a=2),
                                             MISC[:, 0:2 * P].rearrange("p (a j l) -> p a j l", a=2, j=HB), SCALE,
                                             Qt[:, :, 0:QX // 2].rearrange("p l (a j) -> p a j l", a=2), ALU.mult, ALU.subtract)
                    dve.tensor_copy(K_last[:, h, :, :], QT_LAST.rearrange("p (a j g) -> p a j g", a=2, g=NQ)[:, :, :, 0]).then_inc(q_lo, 1)

                def place_last(t, j, first=False):
                    b = TB * t + j
                    dve.wait_ge(q_lo, 2 * t + j // HB + 1)
                    if not first:
                        dve.wait_ge(sc_ps, 2 * (b - 3))
                    dve.tensor_copy(Kt[:, j % 4, :, S - 1:S], K_last[:, j // HB, :, j % HB:j % HB + 1]).then_inc(kl_sb, 1)

                def maxima(t, s, first=False):
                    n = STEPS * t + s
                    dve.wait_ge(sc_ps, n + 1)
                    if not first:
                        dve.wait_ge(exp_sb, n - 1)
                    dve.tensor_reduce(neg_max[:, s % 2, :], SC[s % 2][:, :, 0:S], AX.X, ALU.max, negate=True).then_inc(max_sb, 1)

                def keep_probs(t, s, first=False):
                    n = STEPS * t + s
                    dve.wait_ge(et_ps, n + 1)
                    if not first:
                        dve.wait_ge(av_ps, (STEPS // 2) * t + s // 2 - 1)
                    dve.tensor_tensor(Et[:, s % 4, :, :, :].rearrange("p u k c -> p (u k c)"), ETP[s % 2][:, :],
                                      mask_T[:, :, :, :].rearrange("p u k c -> p (u k c)"), ALU.mult).then_inc(et_sb, 1)

                def keep_last(t, h, final=False):
                    m = 2 * t + h
                    if not final:
                        dve.wait_ge(sc_ps, HSTEPS * (m + 1) + 2)
                    dve.wait_ge(lastt_ps, m + 1)
                    if not (isinstance(t, int) and t == 0 and h == 0):
                        dve.wait_ge(av_full, m)
                    dve.tensor_tensor(last_Et[:, :], LAST, mask_last[:, :], ALU.mult).then_inc(lastt_sb, 1)

                def invert(t, h):
                    m = 2 * t + h
                    dve.reciprocal(rden[:, :], den[:, h, :]).then_inc(rden_set, 1)

                def own_outputs(t, h):
                    m = 2 * t + h
                    dve.wait_ge(o_ps, m + 1)
                    dve.wait_ge(rden_set, m + 1)
                    if not (isinstance(t, int) and t == 0):
                        if h == 0:
                            dve.wait_ge(o_t, t)
                    for q in range(HQ):
                        r = slice(32 * q, 32 * q + 32)
                        i = dve.tensor_tensor(
                            O_n[r, :, HB * NQ * h:HB * NQ * (h + 1)].rearrange("p d u -> p u d"),
                            MISC[r, :].rearrange("p (u c) -> p u c", c=D // NQ)[:, :, DK * q:DK * q + DK],
                            rden[r, :].unsqueeze(2).to_broadcast([32, HB * NQ, DK]), ALU.mult)
                    i.then_inc(o_n, 1)

                def turn_tile(t):
                    dve.wait_ge(o_n, 2 * t + 2)
                    if not (isinstance(t, int) and t == 0):
                        dve.wait_ge(x1, t)
                    dve.transpose(O_t[:, :, :].rearrange("p d l -> p (d l)"), O_n[:, :, :].rearrange("p d u -> p (d u)")).then_inc(o_t, 1)

                def back(t, s, lag):
                    return (t, s - lag) if s >= lag else (t - 1, s + STEPS - lag)

                def steps(t, fresh, final):
                    for s in range(STEPS):
                        q = (t, 1) if s < HSTEPS else (t + 1, 0)
                        more = not (final and s >= HSTEPS)
                        if not final and s % HSTEPS == 4:
                            norm_stats(t + 1, s // HSTEPS)
                        if s % HSTEPS == 1 and not (fresh and s < HSTEPS):
                            keep_last(*((t, 0) if s > HSTEPS else (t - 1, 1)))
                        maxima(t, s, first=fresh and s < 2)
                        if more and s % HSTEPS == 1:
                            keep_queries(*q)
                        if s % 2 == 0:
                            if s < STEPS - 2:
                                place_last(t, s // 2 + 1, first=fresh and s < 6)
                            elif not final:
                                place_last(t + 1, 0)
                        if not final and s % HSTEPS == 4:
                            norm_mean(t + 1, s // HSTEPS)
                        if not (fresh and s < 2):
                            tt, ss = back(t, s, 2)
                            keep_probs(tt, ss, first=fresh and s < 6)
                        if not final and s % HSTEPS == 4:
                            norm_var(t + 1, s // HSTEPS)
                        if not (fresh and s < HSTEPS):
                            tt, ss = back(t, s, HSTEPS)
                            hh = ss // HSTEPS
                            if s % HSTEPS == 3:
                                invert(tt, hh)
                            if s % HSTEPS == 5:
                                own_outputs(tt, hh)
                            if s == 6:
                                turn_tile(tt)
                        if not final and s % HSTEPS == 7:
                            normalise(t + 1, s // HSTEPS)

                dve.memset(Qbd[:, 0, 0, :, :].bitcast(F32), 0.0)
                dve.memset(Kt[:, :, :, S:S + 1].bitcast(F32), 0.0)
                dve.wait_ge(pool_set, 7)
                dve.tensor_reduce(own_of[:, :, :], head_of[:, :].rearrange("p (a u q) -> p u q a", u=2, q=HQ), AX.X,
                                  ALU.add).then_inc(dve_set, 1)
                dve.wait_ge(dve_set, 1)
                dve.tensor_tensor(hh_of[:, :], own_of[:, 0, :], own_of[:, 1, :], ALU.add).then_inc(dve_set, 1)
                dve.wait_ge(dve_set, 2)
                dve.tensor_scalar(hh_scaled[:, :, :], hh_of[:, :].unsqueeze(2).to_broadcast([P, HQ, L]), SCALE, None,
                                  ALU.mult).then_inc(dve_set, 1)
                norm_stats(0, 0)
                norm_mean(0, 0)
                norm_var(0, 0, first=True)
                dve.wait_ge(pe_set, 1)
                for u in range(2):
                    for k in range(KT):
                        dve.tensor_copy(mask_T[:, u, k, :].rearrange("p (q l) -> p q l", q=HQ),
                                        MISC[:, k * L:(k + 1) * L].unsqueeze(1).to_broadcast([P, HQ, L])).then_inc(dve_set, 1)
                dve.tensor_copy(mask_last[:, :].rearrange("p (q l) -> p q l", q=HQ),
                                MISC[0:HB * NQ, 64:64 + L].unsqueeze(1).to_broadcast([HB * NQ, HQ, L])).then_inc(dve_set, 1)
                normalise(0, 0, first=True)
                dve.memset(Qbd[:, 0, 1, :, :].bitcast(F32), 0.0).then_inc(q_zero, 1)
                keep_queries(0, 0)
                place_last(0, 0, first=True)
                norm_stats(0, 1)
                norm_mean(0, 1)
                norm_var(0, 1)
                normalise(0, 1)
                dve.wait_ge(pool_set2, 1)
                dve.tensor_copy(lag[:, :], lag_i[:, :]).then_inc(dve_set2, 1)
                dve.wait_ge(dve_set2, 1)
                dve.tensor_scalar(lag[:, :], lag[:, :], 1.0, None, ALU.max).then_inc(dve_set2, 1)
                for q in range(HQ):
                    dve.tensor_copy(turn_l[:, q, :].rearrange("p (e r g) -> p e r g", e=2, r=HQ),
                                    ident[0:L, 0:L].rearrange("p (g r e) -> p e r g", r=HQ, e=2)).then_inc(dve_set2, 1)
                dve.tensor_copy(hh_wide[:, :, :], hh_of[:, :].unsqueeze(2).to_broadcast([P, HQ, TB])).then_inc(dve_set2, 1)
                dve.wait_ge(pool_set2, 4)
                dve.tensor_copy(lag_p[:, :].rearrange("p (e r g) -> p e r g", e=2, r=HQ),
                                lag_ln[:, :].rearrange("p (g r e) -> p e r g", r=HQ, e=2)).then_inc(dve_set2, 1)
                dve.wait_ge(pe_set2, 1)
                dve.tensor_copy(decay[:, :, :], MISC2[:, 0:L].unsqueeze(1).to_broadcast([P, HB * NQ, L])).then_inc(dve_set2, 1)
                dve.tensor_copy(bcol[:, :], MISC2[:, 64:67]).then_inc(dve_set2, 1)
                dve.wait_ge(pe_set2, 2)
                dve.tensor_copy(out_bias[:, :], MISC2[:, 128:128 + D]).then_inc(dve_set2, 1)
                dve.wait_ge(pool_set3, 2)
                dve.tensor_copy(iota_f[:, :], iota_i[:, :]).then_inc(dve_set3, 1)
                dve.wait_ge(pe_set3, 1)
                dve.tensor_copy(b1c[:, :], MISC3[:, 0:NE * FH]).then_inc(dve_set3, 1)
                dve.wait_ge(dve_set, 8)
                run_tiles(steps, dve)
                for s in range(2):
                    keep_probs(T - 1, STEPS - 2 + s)
                keep_last(T - 1, 1, final=True)
                invert(T - 1, 1)
                own_outputs(T - 1, 1)
                turn_tile(T - 1)

        attend(nc, X, ident, hh_scaled, (W, hh_wide, decay, out_bias, bcol, neg_half2, Kbd, Vbd))
        mix_experts(nc, X, ident, (G, W1, W2, b1c, b2r, gr, b_rows, iota_f, neg_half3, w3_in), out)


def attend(nc, X, ident, hh_scaled, consts):
    with ExitStack() as s2:
        def sb(name, shape, dt=F32):
            return s2.enter_context(nc.sbuf_tensor(name, shape, dt))

        def ps(name, shape):
            return s2.enter_context(nc.psum_tensor(name, shape, F32))

        def sem(name):
            return s2.enter_context(nc.semaphore(name))

        W, hh_wide, decay, out_bias, bcol, neg_half, Kbd, Vbd = consts
        stat = sb("stat2", [P, 2, 6])
        mv = sb("mv2", [P, 2, 2])
        var = sb("var2", [P, 2])
        rs = sb("rs2", [P, 2])
        xn = sb("xn2", [P, 2, D])
        xT = sb("xT2", [P, TB, L])
        xT4 = sb("xT4", [P, TB, NQ, L])
        Qt = sb("Qt2", [P, TB, L])
        Qbd = sb("Qbd2", [P, TB, HQ, L])
        E = sb("E2", [P, 2, HB * NQ, L])
        mx = sb("mx2", [P, 2, HB * NQ])
        sm = sb("sm2", [P, 2, HB * NQ])
        En = sb("En2", [P, 2, HB * NQ, L])
        Et = sb("Et2", [P, 2, HB, HQ * L])
        Oc = sb("Oc2", [P, HQ * TB, TB, NQ])
        Xb = sb("Xb2", [P, 2 * D])

        PA = ps("PA", [P, 512])
        PV = [ps(f"PV{h}", [P, HB, D]) for h in range(2)]
        PS = [ps(f"PS{h}", [P, 512]) for h in range(2)]
        PE_ = [ps(f"PE{h}", [P, HB, HQ * L]) for h in range(2)]
        PY = ps("PY", [P, 2 * D])

        n_stat, n_mv, n_var, n_rs, n_xn = sem("n_stat"), sem("n_mv"), sem("n_var"), sem("n_rs"), sem("n_xn")
        xt_ps, xt_sb, xt4_sb = sem("xt_ps"), sem("xt_sb"), sem("xt4_sb")
        qk_ps, qt_sb, q_bd, k_bd = sem("qk_ps"), sem("qt_sb2"), sem("q_bd2"), sem("k_bd")
        v_ps, v_bd = [sem(f"v_ps{h}") for h in range(2)], [sem(f"v_bd{h}") for h in range(2)]
        s_ps, s_sb, m_sb, d_sb = sem("s_ps"), sem("s_sb"), sem("m_sb"), sem("d_sb")
        e_sb, sum_sb, inv_sb, en_sb = sem("e_sb"), sem("sum_sb"), sem("inv_sb"), sem("en_sb")
        et_ps, et_sb = sem("et_ps2"), sem("et_sb2")
        o_ps, o_sb = sem("o_ps2"), sem("o_sb2")
        y_ps, x2, xb = sem("y_ps"), sem("x2"), sem("xb")

        def tile_of(t):
            return X[:, t, :] if isinstance(t, int) else X[:, bass.ds(t, 1), :].rearrange("p a c -> p (a c)")

        def run(body, eng):
            body(0, 2, False)
            body(1, 2, True)
            with eng.Fori(2, T - 2) as t:
                body(t, 2, True)
            body(T - 2, 1, True)
            body(T - 1, 0, True)

        def later(t):
            return not (isinstance(t, int) and t == 0)

        with nc.Block() as block:
            @block.vector
            def _(dve):
                def norm_stats(t):
                    xt = tile_of(t)
                    for e in range(2):
                        i = dve.bn_stats(stat[:, e, :], xt[:, e * D:(e + 1) * D])
                    i.then_inc(n_stat, 1)

                def norm_mean(t):
                    dve.wait_ge(n_stat, t + 1)
                    dve.nop(nofuse=True)
                    for e in range(2):
                        i = dve.bn_aggr(mv[:, e, :], stat[:, e, :])
                    i.then_inc(n_mv, 1)

                def norm_var(t):
                    dve.wait_ge(n_mv, t + 1)
                    dve.tensor_scalar(var[:, :], mv[:, :, 1], EPS_LN, None, ALU.add).then_inc(n_var, 1)

                def norm(t):
                    dve.wait_ge(n_rs, t + 1)
                    if later(t):
                        dve.wait_ge(xt_ps, t)
                    xt = tile_of(t)
                    for e in range(2):
                        i = dve.tensor_scalar(xn[:, e, :], xt[:, e * D:(e + 1) * D], mv[:, e, 0:1], rs[:, e:e + 1],
                                              ALU.subtract, ALU.mult)
                    i.then_inc(n_xn, 1)

                def add_decay(t, h):
                    m = 2 * t + h
                    dve.wait_ge(s_ps, m + 1)
                    if later(t):
                        dve.wait_ge(en_sb, m - 1)
                    flat = E[:, h, :, :].rearrange("p u s -> p (u s)")
                    dve.tensor_tensor(flat, PS[h][:, :], decay[:, :, :].rearrange("p u s -> p (u s)"), ALU.add).then_inc(s_sb, 1)

                def maxima(t, h):
                    m = 2 * t + h
                    dve.wait_ge(s_sb, m + 1)
                    dve.tensor_reduce(mx[:, h, :], E[:, h, :, :], AX.X, ALU.max).then_inc(m_sb, 1)

                def less_maxima(t, h):
                    m = 2 * t + h
                    dve.wait_ge(m_sb, m + 1)
                    dve.tensor_tensor(E[:, h, :, :], E[:, h, :, :], mx[:, h, :].unsqueeze(2).to_broadcast([P, HB * NQ, L]),
                                      ALU.subtract).then_inc(d_sb, 1)

                def sums(t, h):
                    m = 2 * t + h
                    dve.wait_ge(e_sb, m + 1)
                    dve.tensor_reduce(sm[:, h, :], E[:, h, :, :], AX.X, ALU.add).then_inc(sum_sb, 1)

                def invert(t, h):
                    m = 2 * t + h
                    dve.wait_ge(sum_sb, m + 1)
                    dve.reciprocal(sm[:, h, :], sm[:, h, :]).then_inc(inv_sb, 1)

                def own(t, h):
                    m = 2 * t + h
                    dve.wait_ge(o_ps, m + 1)
                    if later(t):
                        dve.wait_ge(y_ps, t)
                    dve.tensor_tensor(Oc[:, :, HB * h:HB * h + HB, :].rearrange("p a b g -> p b a g"),
                                      PE_[h][:, :, :].rearrange("p j (a g) -> p j a g", g=NQ),
                                      hh_wide[:, :, :].rearrange("p q a -> p (q a)").unsqueeze(1).unsqueeze(3).to_broadcast(
                                          [P, HB, HQ * TB, NQ]), ALU.mult).then_inc(o_sb, 1)

                def add(t):
                    dve.wait_ge(y_ps, t + 1)
                    dve.wait_ge(xb, t + 1)
                    dve.tensor_tensor(tile_of(t), PY[:, :], Xb[:, :], ALU.add).then_inc(x2, 1)

                def body(t, after, before):
                    if after > 1:
                        norm_stats(t + 2)
                    add_decay(t, 0)
                    if after > 1:
                        norm_mean(t + 2)
                    maxima(t, 0)
                    if after > 1:
                        norm_var(t + 2)
                    add_decay(t, 1)
                    less_maxima(t, 0)
                    maxima(t, 1)
                    sums(t, 0)
                    less_maxima(t, 1)
                    invert(t, 0)
                    if before:
                        own(t - 1, 0)
                        own(t - 1, 1)
                    if after > 1:
                        norm(t + 2)
                    sums(t, 1)
                    invert(t, 1)
                    if before:
                        add(t - 1)

                for t in range(2):
                    norm_stats(t)
                    norm_mean(t)
                    norm_var(t)
                    norm(t)
                run(body, dve)
                own(T - 1, 0)
                own(T - 1, 1)
                add(T - 1)

            @block.gpsimd
            def _(pool):
                def front(t):
                    pool.wait_ge(qt_sb, t + 1)
                    if later(t):
                        pool.wait_ge(s_ps, 2 * t)
                    pool.tensor_tensor(Qbd[:, :, :, :], Qt[:, :, :].unsqueeze(2).to_broadcast([P, TB, HQ, L]),
                                       hh_scaled[:, :, :].unsqueeze(1).to_broadcast([P, TB, HQ, L]), ALU.mult).then_inc(q_bd, 1)

                def normalise(t, h):
                    m = 2 * t + h
                    pool.wait_ge(inv_sb, m + 1)
                    if later(t):
                        pool.wait_ge(et_ps, m - 1)
                    pool.tensor_tensor(En[:, h, :, :], E[:, h, :, :], sm[:, h, :].unsqueeze(2).to_broadcast([P, HB * NQ, L]),
                                       ALU.mult).then_inc(en_sb, 1)

                def power(t):
                    pool.wait_ge(n_var, t + 1)
                    if later(t):
                        pool.wait_ge(n_xn, t)
                    pool.tensor_tensor(rs[:, :], var[:, :], neg_half[:, :], ALU.pow).then_inc(n_rs, 1)

                def bias(t):
                    pool.wait_ge(n_xn, t + 1)
                    if later(t):
                        pool.wait_ge(x2, t)
                    xt = tile_of(t)
                    pool.tensor_tensor(Xb[:, :].rearrange("p (e c) -> p e c", e=2), xt.rearrange("p (e c) -> p e c", e=2),
                                       out_bias[:, :].unsqueeze(1).to_broadcast([P, 2, D]), ALU.add).then_inc(xb, 1)

                def body(t, after, before):
                    if before:
                        bias(t - 1)
                    if after > 1:
                        power(t + 2)
                    if after > 0:
                        front(t + 1)
                    normalise(t, 0)
                    normalise(t, 1)

                power(0)
                power(1)
                front(0)
                run(body, pool)
                bias(T - 1)

            @block.scalar
            def _(act):
                def turned(t):
                    act.wait_ge(xt_ps, t + 1)
                    if later(t):
                        act.wait_ge(qk_ps, t)
                        act.wait_ge(xt4_sb, t)
                    for e in range(2):
                        i = act.activation(xT[:, :, 16 * e:16 * e + 16].rearrange("p b (q g) -> p q b g", q=HQ),
                                           PA[:, e * P:(e + 1) * P].rearrange("p (q b g) -> p q b g", q=HQ, b=TB), ACT.Copy)
                    i.then_inc(xt_sb, 1)

                def repeated(t):
                    act.wait_ge(xt_sb, t + 1)
                    if later(t):
                        act.wait_ge(v_ps[0], t)
                        act.wait_ge(v_ps[1], t)
                    act.activation(xT4[:, :, :, :], xT[:, :, :].unsqueeze(2).to_broadcast([P, TB, NQ, L]), ACT.Copy).then_inc(xt4_sb, 1)

                def projected(t):
                    act.wait_ge(qk_ps, t + 1)
                    if later(t):
                        act.wait_ge(q_bd, t)
                    act.activation(Qt[:, :, :].rearrange("p b l -> p (b l)"), PA[:, 0:256], ACT.Identity,
                                   bias=bcol[:, 0:1]).then_inc(qt_sb, 1)
                    if later(t):
                        act.wait_ge(s_ps, 2 * t)
                    for g in range(NQ):
                        r = slice(32 * g, 32 * g + 32)
                        i = act.activation(Kbd[r, :, g, :], PA[r, 256:512].rearrange("p (b s) -> p b s", b=TB), ACT.Identity,
                                           bias=bcol[r, 1:2])
                    i.then_inc(k_bd, 1)

                def values(t, h):
                    act.wait_ge(v_ps[h], t + 1)
                    if later(t):
                        act.wait_ge(o_ps, 2 * t - 1 + h)
                    for g in range(NQ):
                        r = slice(32 * g, 32 * g + 32)
                        i = act.activation(Vbd[r, HB * h:HB * h + HB, 32 * g:32 * g + 32],
                                           PV[h][r, :, 32 * g:32 * g + 32], ACT.Copy)
                    i.then_inc(v_bd[h], 1)

                def exponentials(t, h):
                    act.wait_ge(d_sb, 2 * t + h + 1)
                    flat = E[:, h, :, :].rearrange("p u s -> p (u s)")
                    act.activation(flat, flat, ACT.Exp).then_inc(e_sb, 1)

                def probs(t, h):
                    m = 2 * t + h
                    act.wait_ge(et_ps, m + 1)
                    if later(t):
                        act.wait_ge(o_ps, m - 1)
                    act.activation(Et[:, h, :, :], PE_[h][:, :, :], ACT.Copy).then_inc(et_sb, 1)

                def body(t, after, before):
                    if after > 0:
                        turned(t + 1)
                    if before:
                        probs(t - 1, 0)
                        probs(t - 1, 1)
                    exponentials(t, 0)
                    if after > 0:
                        projected(t + 1)
                    exponentials(t, 1)
                    values(t, 0)
                    values(t, 1)
                    if after > 0:
                        repeated(t + 1)

                turned(0)
                projected(0)
                repeated(0)
                run(body, act)
                probs(T - 1, 0)
                probs(T - 1, 1)

            @block.tensor
            def _(pe):
                def turn(t):
                    pe.wait_ge(n_xn, t + 1)
                    if later(t):
                        pe.wait_ge(k_bd, t)
                    for e in range(2):
                        i = pe.transpose(PA[:, e * P:(e + 1) * P], xn[:, e, :], ident[:, :])
                    i.then_inc(xt_ps, 1)

                def project(t):
                    pe.wait_ge(xt_sb, t + 1)
                    rhs = xT[:, :, :].rearrange("p b l -> p (b l)")
                    pe.matmul(PA[:, 0:256], W["q"][:, :], rhs, start=True, stop=True)
                    pe.matmul(PA[:, 256:512], W["k"][:, :], rhs, start=True, stop=True).then_inc(qk_ps, 1)

                def values(t, h):
                    if later(t):
                        pe.wait_ge(v_bd[h], t)
                    pe.wait_ge(xt4_sb, t + 1)
                    for j in range(HB):
                        i = pe.matmul(PV[h][:, j, :], xT4[:, HB * h + j, :, :].rearrange("p g l -> p (g l)"), W["v"][:, :],
                                      start=True, stop=True)
                    i.then_inc(v_ps[h], 1)

                def scores(t, h):
                    m = 2 * t + h
                    if h == 0:
                        pe.wait_ge(q_bd, t + 1)
                        pe.wait_ge(k_bd, t + 1)
                    if later(t):
                        pe.wait_ge(s_sb, m - 1)
                    for j in range(HB):
                        b = HB * h + j
                        i = pe.matmul(PS[h][:, j * P:(j + 1) * P], Qbd[:, b, :, :].rearrange("p q l -> p (q l)"),
                                      Kbd[:, b, :, :].rearrange("p g s -> p (g s)"), start=True, stop=True)
                    i.then_inc(s_ps, 1)

                def turn_probs(t, h):
                    m = 2 * t + h
                    pe.wait_ge(en_sb, m + 1)
                    if later(t):
                        pe.wait_ge(o_sb, m - 1)
                    for j in range(HB):
                        i = pe.transpose(PE_[h][:, j, :], En[:, h, NQ * j:NQ * j + NQ, :].rearrange("p g s -> p (g s)"),
                                         ident[:, :])
                    i.then_inc(et_ps, 1)

                def weigh(t, h):
                    m = 2 * t + h
                    pe.wait_ge(et_sb, m + 1)
                    pe.wait_ge(v_bd[h], t + 1)
                    for j in range(HB):
                        i = pe.matmul(PE_[h][:, j, :], Vbd[:, HB * h + j, :], Et[:, h, j, :], start=True, stop=True)
                    i.then_inc(o_ps, 1)

                def project_out(t):
                    pe.wait_ge(o_sb, 2 * t + 2)
                    if later(t):
                        pe.wait_ge(x2, t)
                    for e in range(2):
                        for q in range(HQ):
                            a = TB * q + HQ * e
                            i = pe.matmul(PY[:, e * D:(e + 1) * D], Oc[:, a:a + HQ, :, :].rearrange("p a b g -> p (a b g)"),
                                          W["o"][:, :], start=(q == 0), stop=(q == HQ - 1))
                    i.then_inc(y_ps, 1)

                def body(t, after, before):
                    if after > 0:
                        turn(t + 1)
                    scores(t, 0)
                    if before:
                        turn_probs(t - 1, 0)
                    scores(t, 1)
                    if before:
                        turn_probs(t - 1, 1)
                    if after > 0:
                        project(t + 1)
                    values(t, 0)
                    if before:
                        weigh(t - 1, 0)
                        weigh(t - 1, 1)
                    values(t, 1)
                    if before:
                        project_out(t - 1)

                turn(0)
                project(0)
                run(body, pe)
                for h in range(2):
                    turn_probs(T - 1, h)
                for h in range(2):
                    weigh(T - 1, h)
                project_out(T - 1)


def mix_experts(nc, X, ident, consts, out):
    with ExitStack() as s3:
        def sb(name, shape, dt=F32):
            return s3.enter_context(nc.sbuf_tensor(name, shape, dt))

        def ps(name, shape):
            return s3.enter_context(nc.psum_tensor(name, shape, F32))

        def sem(name):
            return s3.enter_context(nc.semaphore(name))

        FH = F // P
        NP = NE // 2
        G, W1, W2, b1c, b2r, gr, b_rows, iota_f, neg_half, w_in = consts
        W_DMAS = 16 * 7
        stat = sb("stat3", [P, 2, 6])
        mv = sb("mv3", [P, 2, 2])
        var = sb("var3", [P, 2])
        rs = sb("rs3", [P, 2])
        xn = sb("xn3", [P, 2, D])
        xT = sb("xT3", [P, 2 * P])
        XB = sb("XB", [P, NE, 2, D])
        gs = sb("gs", [P, 2, NE])
        top = sb("top", [P, 2, 8])
        top_i = sb("top_i", [P, 2, 8], U32)
        top_f = sb("top_f", [P, 2, 2])
        gap = sb("gap", [P, 2])
        th = sb("th", [P, 2])
        pr = sb("pr", [P, 2, 2])
        hot = sb("hot", [P, 2, 2, NE])
        wt = sb("wt", [P, 2, NE])
        wT = sb("wT", [NE, 2 * P])
        hid = sb("hid", [P, 2, FH, 2 * P])
        Z = sb("Z", [P, NP, 4, D])
        zstat = sb("zstat", [P, NP, 4, 6])
        zm = sb("zm", [P, 2, 8])
        zd = sb("zd", [P, 2, 8])
        zv = sb("zv", [P, 2, 8])
        zr = sb("zr", [P, 2, 8])
        zs = sb("zs", [P, 2, 8])
        zb = sb("zb", [P, 2, 8])
        Y = sb("Y", [P, 2, 4, D])
        U = sb("U", [P, 2, 4, D])
        acc = sb("acc", [P, 4, D])
        res = sb("res", [P, 2, D])
        Xo = sb("Xo", [P, 2 * D])

        PH = [ps(f"PH{i}", [P, FH, 2 * P]) for i in range(2)]
        PO = [ps(f"PO{i}", [P, 4, D]) for i in range(2)]
        PA = ps("PA3", [P, 512])
        PW = ps("PW3", [P, 512])
        PB = ps("PB3", [P, 2 * D])

        n_stat, n_mv, n_var, n_rs, n_xn = sem("n_stat3"), sem("n_mv3"), sem("n_var3"), sem("n_rs3"), sem("n_xn3")
        xt_ps, xt_sb, xb_sb = sem("xt_ps3"), sem("xt_sb3"), sem("xb_sb3")
        g_ps, g_sb, t_max, t_idx, t_gap, t_th, t_pr, t_hot, w_sb = (sem(n) for n in (
            "g_ps", "g_sb", "t_max", "t_idx", "t_gap", "t_th", "t_pr", "t_hot", "w_sb"))
        wt_ps, wt_sb, b_ps = sem("wt_ps3"), sem("wt_sb3"), sem("b_ps3")
        h_ps, h_sb, o_ps = sem("h_ps3"), sem("h_sb3"), sem("o_ps3")
        z_sb, z_st, z_m, z_v, z_r, z_s, z_b, y_sb, u_sb, acc_sb = (sem(n) for n in (
            "z_sb", "z_st", "z_m", "z_v", "z_r", "z_s", "z_b", "y_sb3", "u_sb3", "acc_sb"))
        x_b, r1, x3 = sem("x_b"), sem("r1"), sem("x3")
        stored = sem("stored")

        def tile_of(t):
            return X[:, t, :] if isinstance(t, int) else X[:, bass.ds(t, 1), :].rearrange("p a c -> p (a c)")

        def later(t):
            return not (isinstance(t, int) and t == 0)

        def run(slots, eng):
            slots(0)
            slots(1)
            with eng.Fori(2, T - 1) as t:
                slots(t)
            slots(T - 1)

        block = s3.enter_context(nc.Block())

        @block.sync
        def _(sp):
            def keep(t):
                sp.wait_ge(x3, t + 1)
                for q in range(HQ):
                    sp.dma_start(out[bass.ds(TB * t, TB), :, :].rearrange("b (g q e) c -> q b g (e c)", g=NQ, q=HQ)[q],
                                 Xo[32 * q:32 * q + 32, :]).then_inc(stored, 16)

            keep(0)
            with sp.Fori(1, T) as t:
                keep(t)
            sp.wait_ge(stored, 16 * HQ * T)

        @block.gpsimd
        def _(pool):
            def power(t):
                pool.wait_ge(n_var, t + 1)
                if later(t):
                    pool.wait_ge(n_xn, t)
                pool.tensor_tensor(rs[:, :], var[:, :], neg_half[:, 0:2], ALU.pow).then_inc(n_rs, 1)

            def spread(t, p):
                pool.wait_ge(n_xn, t + 1)
                if later(t):
                    pool.wait_ge(z_sb, NP * (t - 1) + p + 1)
                pool.tensor_tensor(XB[:, 2 * p:2 * p + 2, :, :], xn[:, :, :].unsqueeze(1).to_broadcast([P, 2, 2, D]),
                                   b2r[:, 2 * p:2 * p + 2, :].unsqueeze(2).to_broadcast([P, 2, 2, D]), ALU.add).then_inc(xb_sb, 1)

            def inverse(t, q):
                pool.wait_ge(z_v, 2 * t + q + 1)
                pool.tensor_tensor(zr[:, q, :], zv[:, q, :], neg_half[:, :], ALU.pow).then_inc(z_r, 1)

            def gather(t, p):
                pool.wait_ge(u_sb, NP * t + p + 1)
                if p == 1:
                    pool.tensor_tensor(acc[:, :, :], U[:, 0, :, :], U[:, 1, :, :], ALU.add).then_inc(acc_sb, 1)
                else:
                    pool.wait_ge(acc_sb, (NP - 1) * t + p - 1)
                    pool.tensor_tensor(acc[:, :, :], acc[:, :, :], U[:, p % 2, :, :], ALU.add).then_inc(acc_sb, 1)

            def finish(t):
                pool.wait_ge(acc_sb, (NP - 1) * t + NP - 1)
                pool.tensor_tensor(res[:, :, :], acc[:, 0:2, :], acc[:, 2:4, :], ALU.add).then_inc(r1, 1)
                pool.wait_ge(x_b, t + 1)
                pool.wait_ge(r1, t + 1)
                if later(t):
                    pool.wait_ge(stored, 16 * HQ * t)
                pool.tensor_tensor(Xo[:, :], res[:, :, :].rearrange("p e d -> p (e d)"), tile_of(t), ALU.add).then_inc(x3, 1)

            def slots(t):
                last = isinstance(t, int) and t == T - 1
                if later(t):
                    inverse(t - 1, 1)
                    spread(t, 2)
                    if not (isinstance(t, int) and t == 1):
                        finish(t - 2)
                    spread(t, 3)
                    gather(t - 1, 1)
                if not last:
                    power(t + 1)
                inverse(t, 0)
                if later(t):
                    gather(t - 1, 2)
                if not last:
                    spread(t + 1, 0)
                if later(t):
                    gather(t - 1, 3)
                if not last:
                    spread(t + 1, 1)

            power(0)
            pool.wait_ge(w_in, W_DMAS)
            for p in range(NP):
                spread(0, p)
            run(slots, pool)
            inverse(T - 1, 1)
            finish(T - 2)
            for p in range(1, NP):
                gather(T - 1, p)
            finish(T - 1)

        @block.tensor
        def _(pe):
            def turn(t):
                pe.wait_ge(n_xn, t + 1)
                if later(t):
                    pe.wait_ge(g_sb, t)
                for e in range(2):
                    i = pe.transpose(PA[:, e * P:(e + 1) * P], xn[:, e, :], ident[:, :])
                i.then_inc(xt_ps, 1)

            def gates(t):
                for e in range(2):
                    i = pe.matmul(PA[:, 256 + NE * e:256 + NE * e + NE], xT[:, e * P:(e + 1) * P], G[:, :], start=True, stop=True)
                i.then_inc(g_ps, 1)

            def turn_weights(t):
                pe.wait_ge(w_sb, t + 1)
                if later(t):
                    pe.wait_ge(wt_sb, t)
                for e in range(2):
                    i = pe.transpose(PW[0:NE, e * P:(e + 1) * P], wt[:, e, :], ident[:, :])
                i.then_inc(wt_ps, 1)

            def mix_bias(t):
                pe.wait_ge(wt_sb, t + 1)
                if later(t):
                    pe.wait_ge(x_b, t)
                for e in range(2):
                    i = pe.matmul(PB[:, e * D:(e + 1) * D], wT[:, e * P:(e + 1) * P], b_rows[:, :], start=True, stop=True)
                i.then_inc(b_ps, 1)

            def first(t, x):
                n = NE * t + x
                if x == 0:
                    pe.wait_ge(xt_sb, t + 1)
                if not (isinstance(t, int) and t == 0 and x < 2):
                    pe.wait_ge(h_sb, n - 1)
                for a in range(FH):
                    i = pe.matmul(PH[x % 2][:, a, :], W1[:, x, a * P:(a + 1) * P], xT[:, :], start=True, stop=True)
                i.then_inc(h_ps, 1)

            def second(t, x):
                n = NE * t + x
                pe.wait_ge(h_sb, n + 1)
                p = x // 2
                if x % 2 == 0 and not (isinstance(t, int) and t == 0 and p < 2):
                    pe.wait_ge(z_sb, NP * t + p - 1)
                for e in range(2):
                    for a in range(FH):
                        i = pe.matmul(PO[p % 2][:, 2 * (x % 2) + e, :], hid[:, x % 2, a, e * P:(e + 1) * P], W2[:, x, a, :],
                                      start=(a == 0), stop=(a == FH - 1))
                i.then_inc(o_ps, 1)

            def slots(t):
                last = isinstance(t, int) and t == T - 1
                for x in range(NE):
                    first(t, x)
                    if x == 0:
                        gates(t)
                    if x == NE - 1 and not last:
                        turn(t + 1)
                    if x > 0:
                        second(t, x - 1)
                    elif later(t):
                        second(t - 1, NE - 1)
                    if x == 4:
                        turn_weights(t)
                    if x == 5:
                        mix_bias(t)

            pe.wait_ge(w_in, W_DMAS)
            turn(0)
            run(slots, pe)
            second(T - 1, NE - 1)

        @block.scalar
        def _(act):
            def turned(t):
                act.wait_ge(xt_ps, t + 1)
                if later(t):
                    act.wait_ge(h_ps, NE * t)
                    act.wait_ge(g_ps, t)
                act.activation(xT[:, :], PA[:, 0:256], ACT.Copy).then_inc(xt_sb, 1)

            def gelu(t, x):
                n = NE * t + x
                act.wait_ge(h_ps, n + 1)
                if not (isinstance(t, int) and t == 0 and x < 2):
                    act.wait_ge(o_ps, n - 1)
                for a in range(FH):
                    i = act.activation(hid[:, x % 2, a, :], PH[x % 2][:, a, :], ACT.Gelu, bias=b1c[:, FH * x + a:FH * x + a + 1])
                i.then_inc(h_sb, 1)

            def half_tangent(t):
                act.wait_ge(t_gap, t + 1)
                if later(t):
                    act.wait_ge(t_pr, t)
                act.activation(th[:, :], gap[:, :], ACT.Tanh, scale=0.5).then_inc(t_th, 1)

            def weights(t):
                act.wait_ge(wt_ps, t + 1)
                if later(t):
                    act.wait_ge(b_ps, t)
                act.activation(wT[:, :], PW[0:NE, 0:2 * P], ACT.Copy).then_inc(wt_sb, 1)

            def scaled(t, p, x):
                n = NP * t + p
                if x == 0:
                    act.wait_ge(z_b, 2 * t + p // 2 + 1)
                    if not (isinstance(t, int) and t == 0 and p < 2):
                        act.wait_ge(u_sb, n - 1)
                for k in range(2 * x, 2 * x + 2):
                    f = 4 * (p % 2) + k
                    i = act.activation(Y[:, p % 2, k, :], Z[:, p, k, :], ACT.Identity, scale=zs[:, p // 2, f:f + 1],
                                       bias=zb[:, p // 2, f:f + 1])
                if x == 1:
                    i.then_inc(y_sb, 1)

            def slots(t):
                last = isinstance(t, int) and t == T - 1
                for x in range(NE):
                    if x == NE - 1 and not last:
                        turned(t + 1)
                    gelu(t, x)
                    if x == 4:
                        weights(t)
                    if x == NE - 1:
                        scaled(t, 0, 0)
                    elif later(t):
                        scaled(t - 1, (x + 1) // 2, (x + 1) % 2)
                    if x == 1:
                        half_tangent(t)

            turned(0)
            run(slots, act)
            for x in range(NE - 1):
                scaled(T - 1, (x + 1) // 2, (x + 1) % 2)

        @block.vector
        def _(dve):
            def norm_stats(t):
                xt = tile_of(t)
                for e in range(2):
                    i = dve.bn_stats(stat[:, e, :], xt[:, e * D:(e + 1) * D])
                i.then_inc(n_stat, 1)

            def norm_mean(t):
                dve.wait_ge(n_stat, t + 1)
                dve.nop(nofuse=True)
                for e in range(2):
                    i = dve.bn_aggr(mv[:, e, :], stat[:, e, :])
                i.then_inc(n_mv, 1)

            def norm_var(t):
                dve.wait_ge(n_mv, t + 1)
                dve.tensor_scalar(var[:, :], mv[:, :, 1], EPS_LN, None, ALU.add).then_inc(n_var, 1)

            def norm(t):
                dve.wait_ge(n_rs, t + 1)
                if later(t):
                    dve.wait_ge(xt_ps, t)
                    dve.wait_ge(xb_sb, NP * t)
                xt = tile_of(t)
                for e in range(2):
                    i = dve.tensor_scalar(xn[:, e, :], xt[:, e * D:(e + 1) * D], mv[:, e, 0:1], rs[:, e:e + 1],
                                          ALU.subtract, ALU.mult)
                i.then_inc(n_xn, 1)

            def keep_gates(t):
                dve.wait_ge(g_ps, t + 1)
                dve.tensor_copy(gs[:, :, :], PA[:, 256:256 + 2 * NE].rearrange("p (e x) -> p e x", e=2)).then_inc(g_sb, 1)

            def choose(t):
                dve.wait_ge(g_sb, t + 1)
                dve.nop(nofuse=True)
                for e in range(2):
                    i = dve.max(top[:, e, :], gs[:, e, :])
                i.then_inc(t_max, 1)

            def places(t):
                dve.wait_ge(t_max, t + 1)
                dve.tensor_tensor(gap[:, :], top[:, :, 0], top[:, :, 1], ALU.subtract).then_inc(t_gap, 1)
                for e in range(2):
                    i = dve.max_index(top_i[:, e, :], top[:, e, :], gs[:, e, :])
                i.then_inc(t_idx, 1)

            def one_hot(t):
                dve.wait_ge(t_idx, 3 * t + 1)
                dve.tensor_copy(top_f[:, :, :], top_i[:, :, 0:2]).then_inc(t_idx, 1)

            def one_hot2(t):
                dve.wait_ge(t_idx, 3 * t + 2)
                dve.tensor_tensor(hot[:, :, :, :], iota_f[:, :].unsqueeze(1).unsqueeze(1).to_broadcast([P, 2, 2, NE]),
                                  top_f[:, :, :].unsqueeze(3).to_broadcast([P, 2, 2, NE]), ALU.is_equal).then_inc(t_idx, 1)

            def shares(t):
                dve.wait_ge(t_th, t + 1)
                dve.tensor_scalar(pr[:, :, 0], th[:, :], 0.5, 0.5, ALU.mult, ALU.add)
                dve.tensor_scalar(pr[:, :, 1], th[:, :], -0.5, 0.5, ALU.mult, ALU.add).then_inc(t_pr, 1)

            def weigh(t):
                if later(t):
                    dve.wait_ge(wt_ps, t)
                dve.wait_ge(t_pr, t + 1)
                dve.wait_ge(t_idx, 3 * t + 3)
                dve.tensor_tensor(hot[:, :, :, :], hot[:, :, :, :], pr[:, :, :].unsqueeze(3).to_broadcast([P, 2, 2, NE]),
                                  ALU.mult).then_inc(t_hot, 1)

            def weigh2(t):
                dve.wait_ge(t_hot, t + 1)
                dve.tensor_tensor(wt[:, :, :], hot[:, :, 0, :], hot[:, :, 1, :], ALU.add).then_inc(w_sb, 1)

            def collect(t, p):
                n = NP * t + p
                dve.wait_ge(o_ps, NE * t + 2 * p + 2)
                dve.wait_ge(xb_sb, n + 1)
                if later(t):
                    dve.wait_ge(y_sb, NP * (t - 1) + p + 1)
                dve.tensor_tensor(Z[:, p, :, :], PO[p % 2][:, :, :], XB[:, 2 * p:2 * p + 2, :, :].rearrange("p x e d -> p (x e) d"),
                                  ALU.add).then_inc(z_sb, 1)

            def stats(t, p):
                n = NP * t + p
                dve.wait_ge(z_sb, n + 1)
                for i4 in range(4):
                    i = dve.bn_stats(zstat[:, p, i4, :], Z[:, p, i4, :])
                i.then_inc(z_st, 1)

            def spans(q):
                return [zstat[:, 2 * q:2 * q + 2, :, j] for j in (1, 2, 4, 5)]

            def wide(a, q):
                return a[:, q, :].rearrange("p (a b) -> p a b", a=2)

            def variance(t, q):
                m = 2 * t + q
                me, ve, mo, vo = spans(q)
                dve.wait_ge(z_st, NP * t + 2 * q + 2)
                dve.tensor_tensor(wide(zd, q), me, mo, ALU.subtract)
                dve.tensor_tensor(wide(zv, q), ve, vo, ALU.add)
                dve.tensor_tensor(wide(zm, q), me, mo, ALU.add).then_inc(z_m, 1)
                dve.wait_ge(z_m, 2 * m + 1)
                dve.tensor_tensor(zd[:, q, :], zd[:, q, :], zd[:, q, :], ALU.mult)
                dve.tensor_scalar(zv[:, q, :], zv[:, q, :], 1.0 / D, EPS_EXPERT, ALU.mult, ALU.add).then_inc(z_m, 1)

            def variance2(t, q):
                m = 2 * t + q
                dve.wait_ge(z_m, 2 * m + 2)
                dve.scalar_tensor_tensor(zv[:, q, :], zd[:, q, :], 0.25, zv[:, q, :], ALU.mult, ALU.add).then_inc(z_v, 1)

            def factors(t, q):
                m = 2 * t + q
                dve.wait_ge(z_r, m + 1)
                dve.wait_ge(w_sb, t + 1)
                if later(t):
                    dve.wait_ge(y_sb, NP * (t - 1) + 2 * q + 2)
                dve.tensor_tensor(zs[:, q, :].rearrange("p (x e) -> p e x", x=4), zr[:, q, :].rearrange("p (x e) -> p e x", x=4),
                                  wt[:, :, 4 * q:4 * q + 4], ALU.mult).then_inc(z_s, 1)

            def factors2(t, q):
                m = 2 * t + q
                dve.wait_ge(z_s, m + 1)
                dve.scalar_tensor_tensor(zb[:, q, :], zm[:, q, :], -0.5, zs[:, q, :], ALU.mult, ALU.mult).then_inc(z_b, 1)

            def gained(t, p):
                n = NP * t + p
                k = p % 2
                dve.wait_ge(y_sb, n + 1)
                if p >= 2:
                    dve.wait_ge(acc_sb, (NP - 1) * t + p - 1)
                elif later(t):
                    dve.wait_ge(acc_sb, (NP - 1) * (t - 1) + 2 + p)
                dve.tensor_tensor(U[:, k, :, :].rearrange("p (x e) d -> p x e d", x=2),
                                  Y[:, k, :, :].rearrange("p (x e) d -> p x e d", x=2),
                                  gr[:, 2 * p:2 * p + 2, :].unsqueeze(2).to_broadcast([P, 2, 2, D]), ALU.mult).then_inc(u_sb, 1)

            def biased(t):
                dve.wait_ge(b_ps, t + 1)
                dve.tensor_tensor(tile_of(t), tile_of(t), PB[:, :], ALU.add).then_inc(x_b, 1)

            def slots(t):
                last = isinstance(t, int) and t == T - 1
                keep_gates(t)
                if later(t):
                    collect(t - 1, 3)
                choose(t)
                if later(t):
                    stats(t - 1, 3)
                places(t)
                if later(t):
                    variance(t - 1, 1)
                if later(t):
                    variance2(t - 1, 1)
                    gained(t - 1, 0)
                one_hot(t)
                collect(t, 0)
                one_hot2(t)
                stats(t, 0)
                if later(t):
                    factors(t - 1, 1)
                shares(t)
                if later(t):
                    factors2(t - 1, 1)
                weigh(t)
                if not last:
                    norm_stats(t + 1)
                weigh2(t)
                if not last:
                    norm_mean(t + 1)
                if later(t):
                    gained(t - 1, 1)
                if not last:
                    norm_var(t + 1)
                collect(t, 1)
                stats(t, 1)
                if later(t):
                    gained(t - 1, 2)
                variance(t, 0)
                variance2(t, 0)
                if not last:
                    norm(t + 1)
                collect(t, 2)
                biased(t)
                stats(t, 2)
                factors(t, 0)
                if later(t):
                    gained(t - 1, 3)
                factors2(t, 0)

            norm_stats(0)
            norm_mean(0)
            norm_var(0)
            norm(0)
            dve.wait_ge(w_in, W_DMAS)
            run(slots, dve)
            collect(T - 1, 3)
            stats(T - 1, 3)
            gained(T - 1, 0)
            variance(T - 1, 1)
            variance2(T - 1, 1)
            gained(T - 1, 1)
            factors(T - 1, 1)
            factors2(T - 1, 1)
            gained(T - 1, 2)
            gained(T - 1, 3)


_INS = ["x", "ctx_1024", "fside_SxS2_0"] + ["L0_attn_" + n for n in ("Wq", "bq", "Wk", "bk", "Wv", "bv", "Wo", "bo")] + [
    "L0_ffn_" + n for n in ("gate_w", "w1", "b1", "w2", "b2", "ln_g", "ln_b")]


def kernel(**inputs):
    import numpy as _np
    import concourse.bacc as _bacc
    from concourse import mybir as _mybir
    from concourse.bass_utils import run_bass_kernel_spmd as _run

    nc = _bacc.Bacc("TRN2", target_bir_lowering=False, num_devices=1)
    arrays, args = {}, []
    for name in _INS:
        a = _np.ascontiguousarray(inputs[name])
        arrays[f"in_{name}_dram"] = a
        args.append(nc.dram_tensor(f"in_{name}_dram", a.shape, _mybir.dt.from_np(a.dtype), kind="ExternalInput").ap())
    args.append(nc.dram_tensor("out_0_dram", (B, L, D), F32, kind="ExternalOutput").ap())
    perceiver_layer(nc, *args)
    r = _run(nc, [arrays], core_ids=[0])
    return r.results[0]["out_0_dram"]
```
